# Optimizing a Trainium2 kernel written in Bass

```python
import numpy as np
import jax
import jax.numpy as jnp

def _softmax(x, axis=-1):
    return jax.nn.softmax(x, axis=axis)

def _gelu(x):
    return jax.nn.gelu(x, approximate=True)

def _silu(x):
    return jax.nn.silu(x)

def _sigmoid(x):
    return jax.nn.sigmoid(x)

def _layernorm(x, axis=-1, eps=1e-05):
    m = jnp.mean(x, axis=axis, keepdims=True)
    v = jnp.var(x, axis=axis, keepdims=True)
    return (x - m) / jnp.sqrt(v + eps)

def _scatter_add(tgt, idx, src, axis=0):
    return tgt.at[idx].add(src)

def _segment_sum(src, seg, n):
    return jax.ops.segment_sum(src, seg, n)
kernel_name = 'mk_conv_seq_d4_conv_nchw512_r4_4348cc'

def setup_inputs(seed: int=0):
    np.random.seed(seed)
    _w = jnp.asarray

    def _rec_inputs():
        import jax
        import jax.numpy as jnp
        _gk = jax.random.key(seed)
        x = -0.0003929 + 0.9999 * jax.random.normal(jax.random.fold_in(_gk, 1), (32, 128, 32, 32), jnp.float32)
        return x
    x = _rec_inputs()

    def _L0_conv_setup():
        import jax, jax.numpy as jnp
        import numpy as np
        GROUPS = 8
        EPS = 1e-05

        def group_norm(x, gamma, beta):
            B, C, H, W = x.shape
            xg = x.reshape(B, GROUPS, C // GROUPS, H, W)
            mean = xg.mean(axis=(2, 3, 4), keepdims=True)
            var = xg.var(axis=(2, 3, 4), keepdims=True)
            xn = ((xg - mean) * jax.lax.rsqrt(var + EPS)).reshape(B, C, H, W)
            return xn * gamma[None, :, None, None] + beta[None, :, None, None]
        key = jax.random.key(seed)
        ks = jax.random.split(key, 12)
        B, C, H, W = (32, 128, 32, 32)
        s = 1.0 / np.sqrt(C)
        inp = {'x': jax.random.normal(ks[0], (B, C, H, W), dtype=jnp.float32), 'gamma': jnp.ones((C,), dtype=jnp.float32), 'beta': jnp.zeros((C,), dtype=jnp.float32), 'Wq': jax.random.uniform(ks[1], (C, C), jnp.float32, -s, s), 'bq': jax.random.uniform(ks[2], (C,), jnp.float32, -s, s), 'Wk': jax.random.uniform(ks[3], (C, C), jnp.float32, -s, s), 'bk': jax.random.uniform(ks[4], (C,), jnp.float32, -s, s), 'Wv': jax.random.uniform(ks[5], (C, C), jnp.float32, -s, s), 'bv': jax.random.uniform(ks[6], (C,), jnp.float32, -s, s), 'Wp': jax.random.uniform(ks[7], (C, C), jnp.float32, -s, s), 'bp': jax.random.uniform(ks[8], (C,), jnp.float32, -s, s)}
        return inp
    _L0_conv_all = _L0_conv_setup()
    _L0_conv_in = {k: v for k, v in _L0_conv_all.items() if k in ('gamma', 'beta', 'Wq', 'bq', 'Wk', 'bk', 'Wv', 'bv', 'Wp', 'bp')}
    del _L0_conv_all

    def _L1_conv_setup():
        import jax, jax.numpy as jnp
        import numpy as np
        C = 128
        HEADS = 8
        DH = 16
        G = 32
        EPS = 1e-05
        SCALE = DH ** (-0.25)
        key = jax.random.key(seed)
        ks = jax.random.split(key, 10)
        B, H, W = (2, 16, 16)

        def w(k):
            return jax.random.normal(k, (C, C), jnp.float32) * 0.02

        def b(k):
            return jax.random.normal(k, (C,), jnp.float32) * 0.02
        return {'x': jax.random.normal(ks[0], (B, C, H, W), jnp.float32), 'gn_w': jnp.ones((C,), jnp.float32), 'gn_b': jnp.zeros((C,), jnp.float32), 'wq': w(ks[1]), 'bq': b(ks[2]), 'wk': w(ks[3]), 'bk': b(ks[4]), 'wv': w(ks[5]), 'bv': b(ks[6]), 'wp': w(ks[7]), 'bp': b(ks[8])}
    _L1_conv_all = _L1_conv_setup()
    _L1_conv_in = {k: v for k, v in _L1_conv_all.items() if k in ('gn_w', 'gn_b', 'wq', 'bq', 'wk', 'bk', 'wv', 'bv', 'wp', 'bp')}
    del _L1_conv_all

    def _L2_conv_setup():
        import jax, jax.numpy as jnp
        import numpy as np
        EPS = 1e-05

        def _conv1x1(h, w, b):
            return jnp.einsum('bchw,oc->bohw', h, w) + b[None, :, None, None]
        key = jax.random.key(seed)
        ks = jax.random.split(key, 7)
        B, C, H, W = (4, 128, 16, 16)
        s = 0.02
        return {'x': jax.random.normal(ks[0], (B, C, H, W), dtype=jnp.float32), 'wq': jax.random.normal(ks[1], (C, C), dtype=jnp.float32) * s, 'bq': jax.random.normal(ks[2], (C,), dtype=jnp.float32) * s, 'wk': jax.random.normal(ks[3], (C, C), dtype=jnp.float32) * s, 'bk': jax.random.normal(ks[4], (C,), dtype=jnp.float32) * s, 'wv': jax.random.normal(ks[5], (C, C), dtype=jnp.float32) * s, 'bv': jax.random.normal(ks[6], (C,), dtype=jnp.float32) * s}
    _L2_conv_all = _L2_conv_setup()
    _L2_conv_in = {k: v for k, v in _L2_conv_all.items() if k in ('wq', 'bq', 'wk', 'bk', 'wv', 'bv')}
    del _L2_conv_all

    def _L3_conv_setup():
        import jax, jax.numpy as jnp
        import numpy as np
        EPS = 1e-06

        def _conv1x1(x, W, b):
            return jnp.einsum('oc,bchw->bohw', W, x) + b[None, :, None, None]

        def _l2_norm(x):
            return x / jnp.linalg.norm(x, axis=-2, keepdims=True)
        key = jax.random.key(seed)
        ks = jax.random.split(key, 8)
        B, C, H, W = (8, 128, 16, 16)
        Cq = C // 8
        s = 0.02
        return {'x': jax.random.normal(ks[0], (B, C, H, W), jnp.float32), 'Wq': jax.random.normal(ks[1], (Cq, C), jnp.float32) * s, 'bq': jax.random.normal(ks[2], (Cq,), jnp.float32) * s, 'Wk': jax.random.normal(ks[3], (Cq, C), jnp.float32) * s, 'bk': jax.random.normal(ks[4], (Cq,), jnp.float32) * s, 'Wv': jax.random.normal(ks[5], (C, C), jnp.float32) * s, 'bv': jax.random.normal(ks[6], (C,), jnp.float32) * s, 'gamma': jax.random.normal(ks[7], (1,), jnp.float32)}
    _L3_conv_all = _L3_conv_setup()
    _L3_conv_in = {k: v for k, v in _L3_conv_all.items() if k in ('Wq', 'bq', 'Wk', 'bk', 'Wv', 'bv', 'gamma')}
    del _L3_conv_all
    return {'x': x, 'L0_conv_gamma': _L0_conv_in['gamma'], 'L0_conv_beta': _L0_conv_in['beta'], 'L0_conv_Wq': _L0_conv_in['Wq'], 'L0_conv_bq': _L0_conv_in['bq'], 'L0_conv_Wk': _L0_conv_in['Wk'], 'L0_conv_bk': _L0_conv_in['bk'], 'L0_conv_Wv': _L0_conv_in['Wv'], 'L0_conv_bv': _L0_conv_in['bv'], 'L0_conv_Wp': _L0_conv_in['Wp'], 'L0_conv_bp': _L0_conv_in['bp'], 'L1_conv_gn_w': _L1_conv_in['gn_w'], 'L1_conv_gn_b': _L1_conv_in['gn_b'], 'L1_conv_wq': _L1_conv_in['wq'], 'L1_conv_bq': _L1_conv_in['bq'], 'L1_conv_wk': _L1_conv_in['wk'], 'L1_conv_bk': _L1_conv_in['bk'], 'L1_conv_wv': _L1_conv_in['wv'], 'L1_conv_bv': _L1_conv_in['bv'], 'L1_conv_wp': _L1_conv_in['wp'], 'L1_conv_bp': _L1_conv_in['bp'], 'L2_conv_wq': _L2_conv_in['wq'], 'L2_conv_bq': _L2_conv_in['bq'], 'L2_conv_wk': _L2_conv_in['wk'], 'L2_conv_bk': _L2_conv_in['bk'], 'L2_conv_wv': _L2_conv_in['wv'], 'L2_conv_bv': _L2_conv_in['bv'], 'L3_conv_Wq': _L3_conv_in['Wq'], 'L3_conv_bq': _L3_conv_in['bq'], 'L3_conv_Wk': _L3_conv_in['Wk'], 'L3_conv_bk': _L3_conv_in['bk'], 'L3_conv_Wv': _L3_conv_in['Wv'], 'L3_conv_bv': _L3_conv_in['bv'], 'L3_conv_gamma': _L3_conv_in['gamma']}

def reference(x, L0_conv_gamma, L0_conv_beta, L0_conv_Wq, L0_conv_bq, L0_conv_Wk, L0_conv_bk, L0_conv_Wv, L0_conv_bv, L0_conv_Wp, L0_conv_bp, L1_conv_gn_w, L1_conv_gn_b, L1_conv_wq, L1_conv_bq, L1_conv_wk, L1_conv_bk, L1_conv_wv, L1_conv_bv, L1_conv_wp, L1_conv_bp, L2_conv_wq, L2_conv_bq, L2_conv_wk, L2_conv_bk, L2_conv_wv, L2_conv_bv, L3_conv_Wq, L3_conv_bq, L3_conv_Wk, L3_conv_bk, L3_conv_Wv, L3_conv_bv, L3_conv_gamma):
    import jax
    import jax.numpy as jnp

    def _L0_conv_ref(x, gamma, beta, Wq, bq, Wk, bk, Wv, bv, Wp, bp):
        import jax, jax.numpy as jnp
        import numpy as np
        GROUPS = 8
        EPS = 1e-05

        def group_norm(x, gamma, beta):
            B, C, H, W = x.shape
            xg = x.reshape(B, GROUPS, C // GROUPS, H, W)
            mean = xg.mean(axis=(2, 3, 4), keepdims=True)
            var = xg.var(axis=(2, 3, 4), keepdims=True)
            xn = ((xg - mean) * jax.lax.rsqrt(var + EPS)).reshape(B, C, H, W)
            return xn * gamma[None, :, None, None] + beta[None, :, None, None]
        B, C, H, W = x.shape
        scale = C ** (-0.5)
        xn = group_norm(x, gamma, beta)
        h = xn.reshape(B, C, H * W).transpose(0, 2, 1)
        q = jnp.einsum('bnc,dc->bnd', h, Wq) + bq
        k = jnp.einsum('bnc,dc->bnd', h, Wk) + bk
        v = jnp.einsum('bnc,dc->bnd', h, Wv) + bv
        attn = jax.nn.softmax(jnp.einsum('bnd,bmd->bnm', q, k) * scale, axis=-1)
        out = jnp.einsum('bnm,bmd->bnd', attn, v)
        out = jnp.einsum('bnd,ed->bne', out, Wp) + bp
        out = out.transpose(0, 2, 1).reshape(B, C, H, W)
        return out + xn

    def _L1_conv_ref(x, gn_w, gn_b, wq, bq, wk, bk, wv, bv, wp, bp):
        import jax, jax.numpy as jnp
        import numpy as np
        C = 128
        HEADS = 8
        DH = 16
        G = 32
        EPS = 1e-05
        SCALE = DH ** (-0.25)
        B, Cc, H, W = x.shape
        xr = x.reshape(B, G, Cc // G, H * W)
        mean = xr.mean(axis=(2, 3), keepdims=True)
        var = xr.var(axis=(2, 3), keepdims=True)
        h = ((xr - mean) * jax.lax.rsqrt(var + EPS)).reshape(B, Cc, H, W)
        h = h * gn_w[None, :, None, None] + gn_b[None, :, None, None]
        t = h.reshape(B, Cc, H * W).transpose(0, 2, 1)
        q = (t @ wq.T + bq) * SCALE
        k = (t @ wk.T + bk) * SCALE
        v = t @ wv.T + bv

        def split_heads(a):
            return a.reshape(B, H * W, HEADS, DH).transpose(0, 2, 1, 3)
        q, k, v = (split_heads(q), split_heads(k), split_heads(v))
        attn = jax.nn.softmax(jnp.einsum('bhqd,bhkd->bhqk', q, k), axis=-1)
        o = jnp.einsum('bhqk,bhkd->bhqd', attn, v)
        o = o.transpose(0, 2, 1, 3).reshape(B, H * W, Cc)
        o = o @ wp.T + bp
        return o.transpose(0, 2, 1).reshape(B, Cc, H, W) + x

    def _L2_conv_ref(x, wq, bq, wk, bk, wv, bv):
        import jax, jax.numpy as jnp
        import numpy as np
        EPS = 1e-05

        def _conv1x1(h, w, b):
            return jnp.einsum('bchw,oc->bohw', h, w) + b[None, :, None, None]
        B, C, H, W = x.shape
        mu = jnp.mean(x, axis=(2, 3), keepdims=True)
        var = jnp.var(x, axis=(2, 3), keepdims=True)
        h_ = (x - mu) * jax.lax.rsqrt(var + EPS)
        q = _conv1x1(h_, wq, bq).reshape(B, C, H * W)
        k = _conv1x1(h_, wk, bk).reshape(B, C, H * W)
        v = _conv1x1(h_, wv, bv).reshape(B, C, H * W)
        scale = float(int(C)) ** (-0.5)
        attn = jnp.einsum('bcq,bck->bqk', q, k) * scale
        attn = jax.nn.softmax(attn, axis=-1)
        A = jnp.einsum('bck,bqk->bcq', v, attn).reshape(B, C, H, W)
        return x + A

    def _L3_conv_ref(x, Wq, bq, Wk, bk, Wv, bv, gamma):
        import jax, jax.numpy as jnp
        import numpy as np
        EPS = 1e-06

        def _conv1x1(x, W, b):
            return jnp.einsum('oc,bchw->bohw', W, x) + b[None, :, None, None]

        def _l2_norm(x):
            return x / jnp.linalg.norm(x, axis=-2, keepdims=True)
        B, C, H, W = x.shape
        N = H * W
        Q = _conv1x1(x, Wq, bq).reshape(B, -1, N)
        K = _conv1x1(x, Wk, bk).reshape(B, -1, N)
        V = _conv1x1(x, Wv, bv).reshape(B, C, N)
        Qn = _l2_norm(Q).transpose(0, 2, 1)
        Kn = _l2_norm(K)
        tailor_sum = 1.0 / (N + jnp.einsum('bnc,bc->bn', Qn, Kn.sum(-1) + EPS))
        value_sum = V.sum(-1)
        matrix = jnp.einsum('bmn,bcn->bmc', Kn, V)
        matrix_sum = value_sum[:, :, None] + jnp.einsum('bnm,bmc->bcn', Qn, matrix)
        weight_value = (matrix_sum * tailor_sum[:, None, :]).reshape(B, C, H, W)
        return gamma * weight_value

    def _gn(v, G=32, eps=1e-05):
        B_, C_, H_, W_ = v.shape
        g = v.reshape(B_, G, C_ // G, H_, W_)
        m = jnp.mean(g, axis=(2, 3, 4), keepdims=True)
        s = jnp.var(g, axis=(2, 3, 4), keepdims=True)
        return ((g - m) / jnp.sqrt(s + eps)).reshape(v.shape)

    def _ln_c(v, eps=1e-06):
        m = jnp.mean(v, axis=1, keepdims=True)
        s = jnp.var(v, axis=1, keepdims=True)
        return (v - m) / jnp.sqrt(s + eps)

    def _ln_t(v, eps=1e-05):
        m = jnp.mean(v, axis=-1, keepdims=True)
        s = jnp.var(v, axis=-1, keepdims=True)
        return (v - m) / jnp.sqrt(s + eps)

    def _to_tokens(v):
        B_, C_, H_, W_ = v.shape
        return v.reshape(B_, C_, H_ * W_).transpose(0, 2, 1)

    def _from_tokens(t, like):
        B_, C_, H_, W_ = like.shape
        return t.transpose(0, 2, 1).reshape(B_, C_, H_, W_)
    x = _L0_conv_ref(x, L0_conv_gamma, L0_conv_beta, L0_conv_Wq, L0_conv_bq, L0_conv_Wk, L0_conv_bk, L0_conv_Wv, L0_conv_bv, L0_conv_Wp, L0_conv_bp)
    x = _L1_conv_ref(x, L1_conv_gn_w, L1_conv_gn_b, L1_conv_wq, L1_conv_bq, L1_conv_wk, L1_conv_bk, L1_conv_wv, L1_conv_bv, L1_conv_wp, L1_conv_bp)
    x = _L2_conv_ref(x, L2_conv_wq, L2_conv_bq, L2_conv_wk, L2_conv_bk, L2_conv_wv, L2_conv_bv)
    x = _L3_conv_ref(x, L3_conv_Wq, L3_conv_bq, L3_conv_Wk, L3_conv_bk, L3_conv_Wv, L3_conv_bv, L3_conv_gamma)
    return x

_drawn_inputs = setup_inputs


def setup_inputs(seed=0):
    import zlib

    import numpy as np

    out = dict(_drawn_inputs(seed))
    spreads = {'L0_conv_gamma': (1.0, 0.2),
     'L0_conv_beta': (0.0, 0.1),
     'L1_conv_gn_w': (1.0, 0.6),
     'L1_conv_gn_b': (0.0, 0.336)}
    factors = {'L0_conv_Wq': 7.673,
     'L0_conv_bq': 8.0,
     'L0_conv_Wk': 5.836,
     'L0_conv_bk': 64.0,
     'L1_conv_wq': 8.0,
     'L1_conv_bq': 27.907,
     'L1_conv_wk': 8.0,
     'L1_conv_bk': 64.0,
     'L2_conv_wq': 8.0,
     'L2_conv_bq': 8.0,
     'L2_conv_wk': 8.0,
     'L2_conv_bk': 64.0,
     'L2_conv_wv': 8.0,
     'L3_conv_bq': 4.76,
     'L3_conv_bk': 8.0}
    for name, (base, spread) in spreads.items():
        noise = np.random.default_rng([zlib.crc32(name.encode()), seed]).standard_normal(out[name].shape)
        drawn = base * np.exp(spread * noise) if base else spread * noise
        out[name] = jnp.asarray(drawn.astype(out[name].dtype))
    for name, factor in factors.items():
        out[name] = (out[name] * factor).astype(out[name].dtype)
    return out
```

```python
import concourse.bass as bass
from concourse import mybir
from contextlib import ExitStack

F32 = mybir.dt.float32
F32R = mybir.dt.float32r
ALU = mybir.AluOpType
ACT = mybir.ActivationFunctionType
AX = mybir.AxisListType

C = 128
N = 1024
HALF = N // 2
T = N // C
HEADS, DH = 8, 16
A_END, B_END, C_PAUSE, C_END = 0.95, 1.0, 8, 0.95
G1 = 4
EPS = 1e-5
EPS3 = 1e-6
PAIR = 2 * DH
SHIFT_ROW = 3 * PAIR
D3 = 16
W3 = 2 * D3 + C

MATRICES = ["wq0", "wk0", "wv0", "wp0", "wq1", "wk1", "wv1", "wp1", "wp1a", "wp1b",
            "wq2", "wk2", "wv2", "ident", "neg_ident", "group0", "group1"]
VECTORS = ["bq0", "bk0", "bv0", "bp0", "gamma0", "beta0", "bq1", "bk1", "bv1", "bp1",
           "gamma1", "beta1", "bq2", "bk2", "bv2", "gamma3", "one", "zero"]
COL = {name: C * i for i, name in enumerate(MATRICES)}
COL["w3"] = C * len(MATRICES)
COL["zsel"] = COL["w3"] + W3
COL.update({name: COL["zsel"] + G1 + i for i, name in enumerate(VECTORS)})
PACKED = COL["zsel"] + G1 + len(VECTORS)


class Batch:

    def __init__(self, index, plus=0, times=1):
        self.index, self.plus, self.times = index, plus, times

    @property
    def has_prev(self):
        return not isinstance(self.index, int) or self.times * self.index + self.plus > 0

    def at(self, per_batch, count):
        return self.index * (self.times * per_batch) + (self.plus * per_batch + count)

    def previous(self):
        return Batch(self.index, self.plus - 1, self.times)

    def next(self):
        return Batch(self.index, self.plus + 1, self.times)


class PER:
    x_loaded = 16
    f_stat = 1
    f_gstat = 1
    f_veps = 1
    f_rstd = 1
    f_xn = 1
    f_qk = 4
    f_hi = 4
    f_lo = 4
    f_v = 2
    f_vout = 2
    f_max_s = 16
    f_max = 16
    f_shift = 1
    f_sc = 16
    f_p = 16
    f_pv = 16
    f_sum = 14
    f_t = 2
    f_z = 1
    f_r = 1
    f_rb = 1
    f_out = 1
    f_dve = 8
    p_stat = 1
    p_gstat = 1
    p_veps = 1
    p_rstd = 1
    p_h = 1
    p_qk = 4
    p_hi = 4
    p_lo = 4
    p_v = 2
    p_vout = 2
    p_res = 1
    p_dve = 6
    stacked_first = 9 * 16
    stacked_rest = 27 * 16
    m_s = 96
    m_max = 96
    m_both = 1
    m_t = 2
    m_neg = 2
    m_row = 2 * 4 * 16
    s_sc = 64
    s_p = 64
    s_pv = 16
    o_ev = 2
    o_z = 2
    o_r = 2
    o_rb = 2
    o_n = 2
    o_pj = 1
    o_x2 = 1
    o_dve = 2
    t_q = 3
    t_tm = 3
    t_ns = 1
    t_rn = 1
    t_k = 1
    t_m = 1
    t_ma = 1
    t_qs = 1
    t_tr = 1
    t_qt = 1
    t_o = 2
    t_ev = 2
    t_dve = 7
    stored = 16


class Semaphores:
    def __init__(self, new):
        self.x_loaded = new("x_loaded")
        self.f_stat = new("f_stat")
        self.f_gstat = new("f_gstat")
        self.f_veps = new("f_veps")
        self.f_rstd = new("f_rstd")
        self.f_xn = new("f_xn")
        self.f_qk = new("f_qk")
        self.f_hi = new("f_hi")
        self.f_lo = new("f_lo")
        self.f_v = new("f_v")
        self.f_vout = new("f_vout")
        self.f_max_s = new("f_max_s")
        self.f_max = new("f_max")
        self.f_shift = new("f_shift")
        self.f_sc = new("f_sc")
        self.f_p = new("f_p")
        self.f_pv = new("f_pv")
        self.f_sum = new("f_sum")
        self.f_t = new("f_t")
        self.f_z = new("f_z")
        self.f_r = new("f_r")
        self.f_rb = new("f_rb")
        self.f_out = new("f_out")
        self.f_dve = new("f_dve")
        self.p_stat = new("p_stat")
        self.p_gstat = new("p_gstat")
        self.p_veps = new("p_veps")
        self.p_rstd = new("p_rstd")
        self.p_h = new("p_h")
        self.p_qk = new("p_qk")
        self.p_hi = new("p_hi")
        self.p_lo = new("p_lo")
        self.p_v = new("p_v")
        self.p_vout = new("p_vout")
        self.p_res = new("p_res")
        self.p_dve = new("p_dve")
        self.stacked_first = new("stacked_first")
        self.stacked_rest = new("stacked_rest")
        self.m_s = new("m_s")
        self.m_max = new("m_max")
        self.m_both = new("m_both")
        self.m_t = new("m_t")
        self.m_neg = new("m_neg")
        self.m_row = new("m_row")
        self.s_sc = new("s_sc")
        self.s_p = new("s_p")
        self.s_pv = new("s_pv")
        self.o_ev = new("o_ev")
        self.o_z = new("o_z")
        self.o_r = new("o_r")
        self.o_rb = new("o_rb")
        self.o_n = new("o_n")
        self.o_pj = new("o_pj")
        self.o_x2 = new("o_x2")
        self.o_dve = new("o_dve")
        self.t_q = new("t_q")
        self.t_tm = new("t_tm")
        self.t_ns = new("t_ns")
        self.t_rn = new("t_rn")
        self.t_k = new("t_k")
        self.t_m = new("t_m")
        self.t_ma = new("t_ma")
        self.t_qs = new("t_qs")
        self.t_tr = new("t_tr")
        self.t_qt = new("t_qt")
        self.t_o = new("t_o")
        self.t_ev = new("t_ev")
        self.t_dve = new("t_dve")
        self.stored = new("stored")


def heads_kernel(nc, images, x, packed, bias3, out):
    ctx = ExitStack()
    with ctx:
        def sb(name, shape, dtype=F32):
            return ctx.enter_context(nc.sbuf_tensor(name, shape, dtype))

        cw = sb("cw", [C, PACKED])
        b3row = sb("b3row", [1, W3])
        ones = sb("ones", [C, C])
        ones_r = sb("ones_r", [C, C], F32R)
        minus_half = sb("minus_half", [C, 16])
        wvp0 = sb("wvp0", [C, C])
        const_bias = sb("const_bias", [C, 2])

        x_in = sb("x_in", [C, N])
        f_bn = sb("f_bn", [C, 2, 6])
        f_mv = sb("f_mv", [C, 2])
        f_gs = sb("f_gs", [C, 2])
        f_ve = sb("f_ve", [C, 2])
        f_rs = sb("f_rs", [C, 1])
        f_ac = sb("f_ac", [C, 2])
        xn = sb("xn", [C, N])
        fq = [sb("fq_hi", [C, N], F32R), sb("fq_lo", [C, N], F32R)]
        fk = [sb("fk_hi", [C, N], F32R), sb("fk_lo", [C, N], F32R)]
        fv = sb("fv", [C, T, C])
        f_mx2 = sb("f_mx2", [C, T, 2])
        f_mx = sb("f_mx", [C, T])
        f_diag = sb("f_diag", [C, T, C], F32R)
        fp = [sb(f"fp{i}", [C, HALF]) for i in range(3)]
        fsum = sb("fsum", [C, N])
        f_recip = sb("f_recip", [C, T])
        f_num = sb("f_num", [C, N])
        x1 = sb("x1", [C, N])
        x2 = sb("x2", [C, N])
        x3 = sb("x3", [C, N])

        x1_res = sb("x1_res", [C, N])
        p_bn = sb("p_bn", [C, 2, 6])
        p_mv = sb("p_mv", [C, 2])
        p_gs = sb("p_gs", [C, 2])
        p_ve = sb("p_ve", [C, 2])
        p_rs = sb("p_rs", [C, 1])
        p_ac = sb("p_ac", [C, 2])
        h1 = sb("h1", [C, N])
        cq = [sb("cq_hi", [C, N], F32R), sb("cq_lo", [C, N], F32R)]
        ck = [sb("ck_hi", [C, N], F32R), sb("ck_lo", [C, N], F32R)]
        qs = sb("qs", [C, HEADS, N], F32R)
        ks = sb("ks", [C, HEADS // 2, N], F32R)
        v1 = sb("v1", [C, T, HEADS, 32])
        mx_half = sb("mx_half", [C, G1 * T, 2])
        mx1 = sb("mx1", [C, 2, G1 * T])
        neg = sb("neg", [G1 * T, 2, C], F32R)
        p1 = [sb(f"p1_{i}", [C, G1, N]) for i in range(2)]
        o1 = [sb(f"o1_{g}", [C, N]) for g in range(2)]
        rz = [sb(f"rz{g}", [C, T, G1]) for g in range(2)]
        rx = [p1[0][:, g, :].rearrange("p (t j r) -> p t j r", t=T, j=G1) for g in range(2)]

        tm = sb("tm", [C, T, W3 + 1])
        t_sq = sb("t_sq", [C, T, 2, D3])
        t_ns = sb("t_ns", [C, T * 2])
        t_rn = sb("t_rn", [C, T * 2])
        qa = sb("qa", [C, T, D3 + 1])
        ka = sb("ka", [C, T, D3 + 1])
        ma = sb("ma", [D3 + 1, C])
        wb = sb("wb", [C, D3 + 1])
        t_dn = sb("t_dn", [C, T, D3 + 1])
        t_ds = sb("t_ds", [C, 3, T])
        qt3 = sb("qt3", [D3 + 1, N])

        pairs = [ctx.enter_context(nc.psum_tensor(f"pair{i}", [C, N], F32)) for i in range(4)]
        P_EVEN, P_ODD, P_ACC, P_F = pairs

        def t_bank(k):
            return P_F[:, half(k % 2)]

        sem = Semaphores(lambda name: ctx.enter_context(nc.semaphore(name)))
        s_const = ctx.enter_context(nc.semaphore("s_const"))
        s_ones = ctx.enter_context(nc.semaphore("s_ones"))
        s_fill = ctx.enter_context(nc.semaphore("s_fill"))
        s_fold = ctx.enter_context(nc.semaphore("s_fold"))
        s_folded = ctx.enter_context(nc.semaphore("s_folded"))

        def col(name, width=1):
            return cw[:, COL[name]:COL[name] + width]

        def mat(name):
            return col(name, C)

        def f32(ap):
            return ap.bitcast(F32)

        def tile(t):
            return slice(t * C, (t + 1) * C)

        def half(h):
            return slice(h * HALF, (h + 1) * HALF)

        def sums_through(u):
            return (T - 1) * (u // T) + max(u % T, 1)


        def full_attention(n, b, layer):
            yield ("f_stat", 4, n, b, layer)
            yield ("f_var", 4, n)
            yield ("f_apply", 4, n, layer)
            for u in range(4):
                yield ("f_qk", 4, n, u, layer)
            for h in range(2):
                yield ("f_value", 4, n, h, layer)
            for u in range(2 * T):
                yield ("f_max", 2, n, u)
            yield ("f_shift", 6, n)
            for u in range(2 * T):
                yield ("f_scores", 4, n, u)
                if u:
                    yield ("f_pv", 4, n, u - 1)
            yield ("f_pv", 4, n, 2 * T - 1)
            yield ("f_sums", 8, n)
            yield ("f_spread", 10, n)
            yield ("f_out", 6, n, b, layer)

        def heads(b, g):
            for u in range(G1 * T):
                kt, j = u // G1, u % G1
                yield ("s_scores", 2, b, g, u)
                if kt and j % 2:
                    yield ("s_pv", 4, b, g, kt - 1, j // 2)
            yield ("s_pv", 4, b, g, T - 1, 0)
            yield ("s_pv", 4, b, g, T - 1, 1)
            yield ("s_out", 0, b, g)

        def maxima_0(b):
            for u in range(G1 * T):
                yield ("m_max_0", 2, b, u)
            yield ("m_rows", 1, b, 0, P_EVEN)

        def maxima_1(b):
            for u in range(2 * G1 * T):
                yield ("m_max_1", 1, b, u)
            yield ("m_rows", 1, b, 1, P_F)

        def prepare(b, n):
            yield ("p_stat", 2, b, n)
            yield ("p_var", 2, b)
            yield ("p_apply", 2, b)
            for u in range(4):
                yield ("p_qk", 4, b, u)
            yield ("p_stack", 0, b)
            for h in range(2):
                yield ("p_value", 4, b, h)

        def finish_heads(b, last):
            yield ("o_sums", 6, b, last)
            yield ("o_spread", 10, b, last)
            yield ("o_divide", 6, b)
            yield ("o_project", 8, b)
            yield ("o_residual", 4, b)

        def linear_attention(b, n, beside):
            for k in range(3):
                yield ("t_project", 6, b, n, k, beside)
            yield ("t_norms", 4, b)
            yield ("t_keys", 4, b)
            yield ("t_matrix", 8, b)
            yield ("t_scale", 6, b)
            yield ("t_turn", 4, b)
            yield ("t_out", 8, b)

        def pause(cost):
            yield ("pause", cost)

        def merged(main, side, end=1.0):
            main, side = list(main), list(side)
            pace = (sum(s[1] for s in side) or 1) / (end * sum(s[1] for s in main) or 1)
            done = at = spent = 0
            for step in main:
                while at < len(side) and spent < done * pace:
                    yield side[at]
                    spent += side[at][1]
                    at += 1
                yield step
                done += step[1]
            yield from side[at:]

        def run0(b):
            return Batch(0) if isinstance(b.index, int) and b.index + b.plus == 0 else \
                Batch(b.index, 2 * b.plus - 1, 2)

        def run2(b, last):
            return Batch(b.index, 2 * b.plus + (1 if last else 2), 2)

        def first():
            b = Batch(0)
            yield ("load", 0, b, run0(b))
            yield from full_attention(run0(b), b, 0)
            yield from prepare(b, run0(b))
            yield ("p_residual", 0, b, run0(b))
            yield from maxima_0(b)

        def image(b, last):
            nxt, n2 = b.next(), run2(b, last)
            if not last:
                yield ("load", 0, nxt, run0(nxt))
            yield from merged(heads(b, 0), maxima_1(b), A_END)
            before = [*linear_attention(b.previous(), run2(b.previous(), False), b)] if b.has_prev else []
            if last:
                yield from merged(heads(b, 1), before)
                yield from finish_heads(b, last)
                yield from full_attention(n2, b, 2)
                yield from linear_attention(b, n2, None)
            else:
                yield from merged([*heads(b, 1), *finish_heads(b, last)],
                                  [*before, *full_attention(run0(nxt), nxt, 0),
                                   *prepare(nxt, run0(nxt))], B_END)
                yield ("p_residual", 0, nxt, run0(nxt))
                yield from merged(full_attention(n2, b, 2), [*pause(C_PAUSE), *maxima_0(nxt)], C_END)

        def play(eng, steps):
            def do(order):
                for name, _, *args in order:
                    if name in steps:
                        steps[name](*args)
            do(first())
            do(image(Batch(0), images == 1))
            if images > 2:
                with eng.Fori(1, images - 1) as i:
                    do(image(Batch(i), False))
            if images > 1:
                do(image(Batch(images - 1), True))

        block = ctx.enter_context(nc.Block())

        @block.sync
        def _(sp):
            sp.dma_start(cw[:, :], packed).then_inc(s_const, 16)
            sp.dma_start(b3row[:, :], bias3).then_inc(s_const, 16)

            def one(images_ap, b):
                i = b.at(1, 0)
                if isinstance(i, int):
                    return images_ap[i, :, :]
                return images_ap[bass.ds(i, 1), :, :].rearrange("a c n -> (a c) n")

            def load(b, n):
                if n.has_prev:
                    sp.wait_ge(sem.f_xn, n.at(PER.f_xn, 0))
                sp.dma_start(x_in[:, :], one(x, b)).then_inc(sem.x_loaded, 16)

            def p_stack(b):
                def stack_keys(part, t, row, done):
                    sp.dma_start(f32(ks[row:row + PAIR, t, :]),
                                 f32(ck[part][t * PAIR:(t + 1) * PAIR, :])).then_inc(done, 16)

                def stack_queries(part, t, row, done):
                    for e in range(2):
                        h = 2 * t + e
                        sp.dma_start(f32(qs[row + e * DH:row + (e + 1) * DH, h, :]),
                                     f32(cq[part][h * DH:(h + 1) * DH, :])).then_inc(done, 16)

                for t in range(HEADS // 2):
                    done = sem.stacked_rest if t else sem.stacked_first
                    if t == 0:
                        sp.wait_ge(sem.p_hi, b.at(PER.p_hi, 4))
                    stack_queries(0, t, 0, done)
                    stack_keys(0, t, 0, done)
                    stack_queries(0, t, 2 * PAIR, done)
                    stack_keys(0, t, PAIR, done)
                    if t == 0:
                        sp.wait_ge(sem.p_lo, b.at(PER.p_lo, 4))
                    stack_queries(1, t, PAIR, done)
                    stack_keys(1, t, 2 * PAIR, done)

            def m_rows(b, g, pair):
                sp.wait_ge(sem.m_neg, b.at(PER.m_neg, g + 1))
                for j in range(G1):
                    sp.dma_start(f32(qs[SHIFT_ROW:SHIFT_ROW + 1, G1 * g + j, :]),
                                 f32(neg[j * T:(j + 1) * T, g, :])).then_inc(sem.m_row, 16)

            def t_out(b):
                sp.wait_ge(sem.t_ev, b.at(PER.t_ev, 2))
                sp.dma_start(one(out, b), x3[:, :]).then_inc(sem.stored, 16)

            sp.wait_ge(s_fill, 2)
            play(sp, dict(load=load, p_stack=p_stack, m_rows=m_rows, t_out=t_out))
            sp.wait_ge(sem.stored, 16 * images)

        @block.gpsimd
        def _(pool):
            pool.memset(f32(qs[:, :, :]), 0.0).then_inc(s_fill, 1)
            pool.memset(f32(ks[:, :, :]), 1.0).then_inc(s_fill, 1)
            pool.memset(ones[:, :], 1.0).then_inc(s_ones, 1)
            pool.memset(f32(ones_r[:, :]), 1.0).then_inc(s_ones, 1)
            pool.memset(minus_half[:, :], -0.5).then_inc(s_ones, 1)
            pool.memset(v1[:, :, :, :], 0.0).then_inc(s_ones, 1)
            pool.memset(tm[:, :, W3:W3 + 1], 1.0).then_inc(s_ones, 1)
            pool.memset(qa[:, :, D3:D3 + 1], 1.0).then_inc(s_ones, 1)
            pool.memset(ka[:, :, D3:D3 + 1], 1.0).then_inc(s_ones, 1)
            pool.wait_ge(s_ones, 7)
            pool.memset(v1[:, :, :, DH:DH + 1], 1.0).then_inc(s_ones, 1)

            def f_var(n):
                pool.wait_ge(sem.f_veps, n.at(PER.f_veps, 1))
                pool.tensor_tensor(f_rs[:, :], f_ve[:, 1:2], minus_half[:, 0:1], ALU.pow)\
                    .then_inc(sem.f_rstd, 1)

            def f_pv(n, u):
                h, kt = u // T, u % T
                dst = fsum[:, half(h)]
                pool.wait_ge(sem.f_p, n.at(PER.f_p, u + 1))
                if kt == 1:
                    if u == 1:
                        if n.has_prev:
                            pool.wait_ge(sem.f_z, n.at(PER.f_z, 0))
                    pool.tensor_tensor(dst, fp[(u - 1) % 3][:, :], fp[u % 3][:, :], ALU.add)\
                        .then_inc(sem.f_sum, 1)
                elif kt > 1:
                    pool.wait_ge(sem.f_sum, n.at(PER.f_sum, sums_through(u) - 1))
                    pool.tensor_tensor(dst, dst, fp[u % 3][:, :], ALU.add).then_inc(sem.f_sum, 1)

            def p_var(b):
                pool.wait_ge(sem.p_veps, b.at(PER.p_veps, 1))
                pool.tensor_tensor(p_rs[:, :], p_ve[:, 1:2], minus_half[:, 0:1], ALU.pow)\
                    .then_inc(sem.p_rstd, 1)

            def p_residual(b, n):
                if b.has_prev:
                    pool.wait_ge(sem.o_x2, b.at(PER.o_x2, 0))
                pool.wait_ge(sem.f_out, n.at(PER.f_out, 1))
                pool.tensor_tensor(x1_res[:, :], x1[:, :], const_bias[:, 1:2].broadcast_to([C, N]),
                                   ALU.add).then_inc(sem.p_res, 1)

            def t_norms(b):
                pool.wait_ge(sem.t_ns, b.at(PER.t_ns, 1))
                pool.tensor_tensor(t_rn[:, :], t_ns[:, :], minus_half[:, :], ALU.pow)\
                    .then_inc(sem.t_rn, 1)

            pool.wait_ge(s_folded, 3)
            play(pool, dict(f_var=f_var, f_pv=f_pv, p_var=p_var, p_residual=p_residual,
                            t_norms=t_norms))

        @block.scalar
        def _(act):
            def f_qk(n, u, layer):
                dst, bias = (fq, f"bq{layer}") if u < 2 else (fk, f"bk{layer}")
                act.wait_ge(sem.f_qk, n.at(PER.f_qk, u + 1))
                act.activation(dst[0][:, half(u % 2)], P_F[:, half(u % 2)], ACT.Identity,
                               bias=col(bias)).then_inc(sem.f_hi, 1)

            def f_value(n, h, layer):
                act.wait_ge(sem.f_v, n.at(PER.f_v, h + 1))
                act.activation(fv[:, 4 * h:4 * h + 4, :].rearrange("p t c -> p (t c)"), P_F[:, half(h)],
                               ACT.Copy).then_inc(sem.f_vout, 1)

            def f_scores(n, u):
                act.wait_ge(sem.f_sc, n.at(PER.f_sc, u + 1))
                if u >= 3:
                    act.wait_ge(sem.f_pv, n.at(PER.f_pv, u - 2))
                    act.wait_ge(sem.f_sum, n.at(PER.f_sum, sums_through(u - 3)))
                else:
                    if n.has_prev:
                        act.wait_ge(sem.f_pv, n.at(PER.f_pv, 0))
                    if n.has_prev:
                        act.wait_ge(sem.f_sum, n.at(PER.f_sum, 0))
                act.activation(fp[u % 3][:, :], P_F[:, half(0)], ACT.Exp, scale=float(C) ** -0.5)\
                    .then_inc(sem.f_p, 1)

            def f_pv(n, u):
                if u % T == T - 1:
                    h = u // T
                    act.wait_ge(sem.f_pv, n.at(PER.f_pv, u + 1))
                    if h == 0:
                        if n.has_prev:
                            act.wait_ge(sem.f_out, n.at(PER.f_out, 0))
                    act.activation(f_num[:, half(h)], P_F[:, half(1)], ACT.Copy).then_inc(sem.f_t, 1)

            def p_qk(b, u):
                if u == 0:
                    if b.has_prev:
                        act.wait_ge(sem.stacked_first, b.at(PER.stacked_first, 0))
                        act.wait_ge(sem.stacked_rest, b.at(PER.stacked_rest, 0))
                dst, bias = (cq, "bq1") if u < 2 else (ck, "bk1")
                act.wait_ge(sem.p_qk, b.at(PER.p_qk, u + 1))
                act.activation(dst[0][:, half(u % 2)], P_ODD[:, half(u % 2)], ACT.Identity,
                               bias=col(bias)).then_inc(sem.p_hi, 1)

            def p_value(b, h):
                act.wait_ge(sem.p_v, b.at(PER.p_v, h + 1))
                act.activation(v1[:, 4 * h:4 * h + 4, :, 0:DH],
                               P_ODD[:, half(h)].rearrange("p (t h d) -> p t h d", t=4, h=HEADS),
                               ACT.Copy).then_inc(sem.p_vout, 1)

            def s_scores(b, g, u):
                kt, j = u // G1, u % G1
                act.wait_ge(sem.s_sc, b.at(PER.s_sc, 32 * g + u + 1))
                if 8 * g + kt >= 2:
                    if j == 0:
                        act.wait_ge(sem.s_pv, b.at(PER.s_pv, 8 * g + kt - 1))
                elif j == 0:
                    if b.has_prev:
                        act.wait_ge(sem.s_pv, b.at(PER.s_pv, 0))
                        act.wait_ge(sem.o_rb, b.at(PER.o_rb, 0))
                act.activation(p1[kt % 2][:, j, :], (P_EVEN, P_ODD)[u % 2][:, :], ACT.Exp,
                               scale=float(DH) ** -0.5).then_inc(sem.s_p, 1)

            def s_out(b, g):
                act.wait_ge(sem.s_pv, b.at(PER.s_pv, 8 * (g + 1)))
                if b.has_prev:
                    act.wait_ge(sem.o_pj, b.at(PER.o_pj, 0))
                act.activation(o1[g][:, :], P_ACC[:, :], ACT.Copy).then_inc(sem.o_ev, 1)

            def t_project(b, n, k, beside):
                t0, t1 = 3 * k, min(3 * k + 3, T)
                act.wait_ge(sem.t_q, b.at(PER.t_q, k + 1))
                act.activation(tm[:, t0:t1, 0:W3],
                               t_bank(k)[:, 0:(t1 - t0) * W3].rearrange("p (t w) -> p t w", w=W3),
                               ACT.Copy).then_inc(sem.t_tm, 1)

            def t_matrix(b):
                act.wait_ge(sem.t_m, b.at(PER.t_m, 1))
                act.activation(ma[:, :], P_F[0:D3 + 1, 0:C], ACT.Copy).then_inc(sem.t_ma, 1)

            def t_turn(b):
                act.wait_ge(sem.t_tr, b.at(PER.t_tr, 1))
                act.activation(qt3[:, :], P_F[0:D3 + 1, :], ACT.Copy).then_inc(sem.t_qt, 1)

            def t_out(b):
                for h in range(2):
                    act.wait_ge(sem.t_o, b.at(PER.t_o, h + 1))
                    act.activation(x3[:, half(h)], P_F[:, half(h)], ACT.Copy).then_inc(sem.t_ev, 1)

            act.wait_ge(s_const, 32)
            act.wait_ge(s_ones, 8)
            act.wait_ge(s_fold, 3)
            act.activation(wvp0[:, :], P_EVEN[:, 0:C], ACT.Copy).then_inc(s_folded, 1)
            act.activation(const_bias[:, 0:1], P_EVEN[:, C:C + 1], ACT.Identity, bias=col("bp0"))\
               .then_inc(s_folded, 1)
            act.activation(const_bias[:, 1:2], P_EVEN[:, C + 1:C + 2], ACT.Identity, bias=col("bp1"))\
               .then_inc(s_folded, 1)
            play(act, dict(f_qk=f_qk, f_value=f_value, f_scores=f_scores, f_pv=f_pv, p_qk=p_qk,
                           p_value=p_value, s_scores=s_scores, s_out=s_out, t_project=t_project,
                           t_matrix=t_matrix, t_turn=t_turn, t_out=t_out))

        @block.vector
        def _(dve):
            def f_stat(n, b, layer):
                if layer == 0:
                    dve.wait_ge(sem.x_loaded, b.at(PER.x_loaded, 16))
                else:
                    dve.wait_ge(sem.o_x2, b.at(PER.o_x2, 1))
                src = x_in if layer == 0 else x2
                dve.bn_stats(f_bn[:, 0, :], src[:, half(0)])
                dve.bn_stats(f_bn[:, 1, :], src[:, half(1)]).then_inc(sem.f_dve, 1)
                dve.wait_ge(sem.f_dve, n.at(PER.f_dve, 1))
                dve.memset(f_ve[:, :], 0.0)
                dve.bn_aggr(f_mv[:, :], f_bn[:, :, :].rearrange("p a s -> p (a s)"))\
                   .then_inc(sem.f_dve, 1)
                dve.wait_ge(sem.f_dve, n.at(PER.f_dve, 2))
                dve.scalar_tensor_tensor(out=f_mv[:, 1:2], in0=f_mv[:, 0:1],
                                         scalar=f_mv[:, 0:1], in1=f_mv[:, 1:2],
                                         op0=ALU.mult, op1=ALU.add).then_inc(sem.f_stat, 1)

            def f_var(n):
                dve.wait_ge(sem.f_gstat, n.at(PER.f_gstat, 1))
                dve.tensor_copy(f_gs[:, :], P_F[:, 0:2]).then_inc(sem.f_dve, 1)
                dve.wait_ge(sem.f_dve, n.at(PER.f_dve, 3))
                dve.scalar_tensor_tensor(out=f_ve[:, 0:1], in0=f_gs[:, 0:1],
                                         scalar=f_gs[:, 0:1], in1=f_gs[:, 1:2],
                                         op0=ALU.mult, op1=ALU.subtract).then_inc(sem.f_dve, 1)
                dve.wait_ge(sem.f_dve, n.at(PER.f_dve, 4))
                dve.tensor_scalar(f_ve[:, 1:2], f_ve[:, 0:1], -1.0, EPS, ALU.mult, ALU.add)\
                   .then_inc(sem.f_veps, 1)

            def f_apply(n, layer):
                src, gamma, beta = (x_in, "gamma0", "beta0") if layer == 0 else (x2, "one", "zero")
                dve.wait_ge(sem.f_rstd, n.at(PER.f_rstd, 1))
                dve.tensor_scalar(f_ac[:, 0:1], f_rs[:, :], col(gamma), None, ALU.mult)\
                   .then_inc(sem.f_dve, 1)
                dve.wait_ge(sem.f_dve, n.at(PER.f_dve, 5))
                dve.scalar_tensor_tensor(out=f_ac[:, 1:2], in0=f_gs[:, 0:1],
                                         scalar=f_ac[:, 0:1], in1=col(beta),
                                         op0=ALU.mult, op1=ALU.subtract).then_inc(sem.f_dve, 1)
                dve.wait_ge(sem.f_dve, n.at(PER.f_dve, 6))
                dve.tensor_scalar(xn[:, :], src[:, :], f_ac[:, 0:1], f_ac[:, 1:2], ALU.mult,
                                  ALU.subtract).then_inc(sem.f_xn, 1)

            def f_qk(n, u, layer):
                dst, bias = (fq, f"bq{layer}") if u < 2 else (fk, f"bk{layer}")
                dve.wait_ge(sem.f_hi, n.at(PER.f_hi, u + 1))
                h = half(u % 2)
                dve.scalar_tensor_tensor(out=dst[1][:, h], in0=P_F[:, h], scalar=col(bias),
                                         in1=f32(dst[0][:, h]), op0=ALU.add, op1=ALU.subtract)\
                   .then_inc(sem.f_lo, 1)

            def f_max(n, u):
                dve.wait_ge(sem.f_max_s, n.at(PER.f_max_s, u + 1))
                dve.reduce_max(f_mx2[:, u // 2, u % 2:u % 2 + 1], P_F[:, half(u % 2)], AX.X)\
                   .then_inc(sem.f_max, 1)

            def f_shift(n):
                dve.wait_ge(sem.f_max, n.at(PER.f_max, 2 * T))
                dve.tensor_tensor(f_mx[:, :], f_mx2[:, :, 0], f_mx2[:, :, 1], ALU.max)\
                   .then_inc(sem.f_dve, 1)
                dve.wait_ge(sem.f_dve, n.at(PER.f_dve, 7))
                dve.tensor_tensor(f_diag[:, :, :],
                                  mat("neg_ident").rearrange("p (a c) -> p a c", a=1).broadcast_to([C, T, C]),
                                  f_mx[:, :].rearrange("p (t a) -> p t a", a=1).broadcast_to([C, T, C]),
                                  ALU.mult).then_inc(sem.f_shift, 1)

            def f_sums(n):
                dve.wait_ge(sem.f_z, n.at(PER.f_z, 1))
                dve.reciprocal(f_recip[:, :], P_F[:, 0:T]).then_inc(sem.f_r, 1)

            def f_out(n, b, layer):
                dve.wait_ge(sem.f_rb, n.at(PER.f_rb, 1))
                dve.tensor_tensor(f_num[:, :], f_num[:, :], P_F[:, :], ALU.mult)\
                   .then_inc(sem.f_dve, 1)
                dve.wait_ge(sem.f_dve, n.at(PER.f_dve, 8))
                if layer == 0:
                    dst, bias, residual = x1, const_bias[:, 0:1], xn
                    if b.has_prev:
                        dve.wait_ge(sem.p_h, b.at(PER.p_h, 0))
                    if b.has_prev:
                        dve.wait_ge(sem.p_res, b.at(PER.p_res, 0))
                else:
                    dst, bias, residual = x3, col("bv2"), x2
                    if b.has_prev:
                        dve.wait_ge(sem.stored, b.at(PER.stored, 0))
                dve.scalar_tensor_tensor(out=dst[:, :], in0=f_num[:, :], scalar=bias,
                                         in1=residual[:, :], op0=ALU.add, op1=ALU.add)\
                   .then_inc(sem.f_out, 1)

            def p_stat(b, n):
                dve.wait_ge(sem.f_out, n.at(PER.f_out, 1))
                dve.bn_stats(p_bn[:, 0, :], x1[:, half(0)])
                dve.bn_stats(p_bn[:, 1, :], x1[:, half(1)]).then_inc(sem.p_dve, 1)
                dve.wait_ge(sem.p_dve, b.at(PER.p_dve, 1))
                dve.memset(p_ve[:, :], 0.0)
                dve.bn_aggr(p_mv[:, :], p_bn[:, :, :].rearrange("p a s -> p (a s)"))\
                   .then_inc(sem.p_dve, 1)
                dve.wait_ge(sem.p_dve, b.at(PER.p_dve, 2))
                dve.scalar_tensor_tensor(out=p_mv[:, 1:2], in0=p_mv[:, 0:1],
                                         scalar=p_mv[:, 0:1], in1=p_mv[:, 1:2],
                                         op0=ALU.mult, op1=ALU.add).then_inc(sem.p_stat, 1)

            def p_var(b):
                dve.wait_ge(sem.p_gstat, b.at(PER.p_gstat, 1))
                dve.tensor_copy(p_gs[:, :], P_ODD[:, 0:2]).then_inc(sem.p_dve, 1)
                dve.wait_ge(sem.p_dve, b.at(PER.p_dve, 3))
                dve.scalar_tensor_tensor(out=p_ve[:, 0:1], in0=p_gs[:, 0:1],
                                         scalar=p_gs[:, 0:1], in1=p_gs[:, 1:2],
                                         op0=ALU.mult, op1=ALU.subtract).then_inc(sem.p_dve, 1)
                dve.wait_ge(sem.p_dve, b.at(PER.p_dve, 4))
                dve.tensor_scalar(p_ve[:, 1:2], p_ve[:, 0:1], -1.0, EPS, ALU.mult, ALU.add)\
                   .then_inc(sem.p_veps, 1)

            def p_apply(b):
                dve.wait_ge(sem.p_rstd, b.at(PER.p_rstd, 1))
                dve.tensor_scalar(p_ac[:, 0:1], p_rs[:, :], col("gamma1"), None, ALU.mult)\
                   .then_inc(sem.p_dve, 1)
                dve.wait_ge(sem.p_dve, b.at(PER.p_dve, 5))
                dve.scalar_tensor_tensor(out=p_ac[:, 1:2], in0=p_gs[:, 0:1],
                                         scalar=p_ac[:, 0:1], in1=col("beta1"),
                                         op0=ALU.mult, op1=ALU.subtract).then_inc(sem.p_dve, 1)
                dve.wait_ge(sem.p_dve, b.at(PER.p_dve, 6))
                dve.tensor_scalar(h1[:, :], x1[:, :], p_ac[:, 0:1], p_ac[:, 1:2], ALU.mult,
                                  ALU.subtract).then_inc(sem.p_h, 1)

            def p_qk(b, u):
                if u == 0:
                    if b.has_prev:
                        dve.wait_ge(sem.stacked_first, b.at(PER.stacked_first, 0))
                        dve.wait_ge(sem.stacked_rest, b.at(PER.stacked_rest, 0))
                dst, bias = (cq, "bq1") if u < 2 else (ck, "bk1")
                dve.wait_ge(sem.p_hi, b.at(PER.p_hi, u + 1))
                h = half(u % 2)
                dve.scalar_tensor_tensor(out=dst[1][:, h], in0=P_ODD[:, h], scalar=col(bias),
                                         in1=f32(dst[0][:, h]), op0=ALU.add, op1=ALU.subtract)\
                   .then_inc(sem.p_lo, 1)

            def m_max_0(b, u):
                dve.wait_ge(sem.m_s, b.at(PER.m_s, u + 1))
                dve.reduce_max(mx1[:, 0, u:u + 1], (P_EVEN, P_ODD)[u % 2][:, :], AX.X)\
                   .then_inc(sem.m_max, 1)

            def m_max_1(b, u):
                dve.wait_ge(sem.m_s, b.at(PER.m_s, 32 + u + 1))
                dve.reduce_max(mx_half[:, u // 2, u % 2:u % 2 + 1], P_F[:, half(u % 2)], AX.X)\
                   .then_inc(sem.m_max, 1)
                if u == 2 * G1 * T - 1:
                    dve.wait_ge(sem.m_max, b.at(PER.m_max, 96))
                    dve.tensor_tensor(mx1[:, 1, :], mx_half[:, :, 0], mx_half[:, :, 1], ALU.max)\
                       .then_inc(sem.m_both, 1)

            def m_rows(b, g, pair):
                dve.wait_ge(sem.m_t, b.at(PER.m_t, g + 1))
                if b.has_prev:
                    dve.wait_ge(sem.m_row, b.at(PER.m_row, 0))
                dve.tensor_copy(neg[:, g, :], pair[0:G1 * T, 0:C]).then_inc(sem.m_neg, 1)

            def o_sums(b, last):
                for g in range(2):
                    dve.wait_ge(sem.o_z, b.at(PER.o_z, g + 1))
                    dve.reciprocal(rz[g][:, :, :].rearrange("p t j -> p (t j)"),
                                   P_ACC[:, g * HALF:g * HALF + T * G1])\
                       .then_inc(sem.o_dve, 1)
                    dve.wait_ge(sem.o_dve, b.at(PER.o_dve, g + 1))
                    dve.tensor_copy(rx[g], rz[g][:, :, :].rearrange(
                        "p t (j a) -> p t j a", a=1).broadcast_to([C, T, G1, 32])).then_inc(sem.o_r, 1)

            def o_divide(b):
                for g in range(2):
                    dve.wait_ge(sem.o_rb, b.at(PER.o_rb, g + 1))
                    dve.tensor_tensor(o1[g][:, :], o1[g][:, :], (P_ACC, P_EVEN)[g][:, :], ALU.mult)\
                       .then_inc(sem.o_n, 1)

            def o_residual(b):
                dve.wait_ge(sem.o_pj, b.at(PER.o_pj, 1))
                dve.wait_ge(sem.p_res, b.at(PER.p_res, 1))
                dve.tensor_tensor(x2[:, :], P_ACC[:, :], x1_res[:, :], ALU.add)\
                   .then_inc(sem.o_x2, 1)

            def t_norms(b):
                dve.wait_ge(sem.t_tm, b.at(PER.t_tm, 3))
                qk = tm[:, :, 0:2 * D3].rearrange("p t (a d) -> p t a d", a=2)
                dve.tensor_tensor(t_sq[:, :, :, :], qk, qk, ALU.mult)\
                   .then_inc(sem.t_dve, 1)
                dve.wait_ge(sem.t_dve, b.at(PER.t_dve, 1))
                dve.reduce_sum(t_ns[:, :], t_sq[:, :, :, :].rearrange("p t a d -> p (t a) d"), AX.X)\
                   .then_inc(sem.t_ns, 1)

            def t_keys(b):
                dve.wait_ge(sem.t_rn, b.at(PER.t_rn, 1))
                rn = t_rn[:, :].rearrange("p (t a) -> p t a", a=2)
                dve.tensor_tensor(ka[:, :, 0:D3], tm[:, :, D3:2 * D3],
                                  rn[:, :, 1:2].broadcast_to([C, T, D3]), ALU.mult)\
                   .then_inc(sem.t_k, 1)
                dve.tensor_tensor(qa[:, :, 0:D3], tm[:, :, 0:D3],
                                  rn[:, :, 0:1].broadcast_to([C, T, D3]), ALU.mult)\
                   .then_inc(sem.t_dve, 1)
                dve.wait_ge(sem.t_dve, b.at(PER.t_dve, 2))

            def t_scale(b):
                dve.wait_ge(sem.t_m, b.at(PER.t_m, 1))
                dve.tensor_scalar(wb[:, 0:D3], P_F[:, HALF:HALF + D3], EPS3, None, ALU.add)
                dve.tensor_copy(wb[:, D3:D3 + 1], P_F[:, HALF + D3:HALF + D3 + 1])\
                   .then_inc(sem.t_dve, 1)
                dve.wait_ge(sem.t_dve, b.at(PER.t_dve, 3))
                dve.tensor_tensor(t_dn[:, :, :], qa[:, :, :],
                                  wb[:, :].rearrange("p (a d) -> p a d", a=1).broadcast_to([C, T, D3 + 1]),
                                  ALU.mult)\
                   .then_inc(sem.t_dve, 1)
                dve.wait_ge(sem.t_dve, b.at(PER.t_dve, 4))
                dve.reduce_sum(t_ds[:, 0, :], t_dn[:, :, :], AX.X)\
                   .then_inc(sem.t_dve, 1)
                dve.wait_ge(sem.t_dve, b.at(PER.t_dve, 5))
                dve.reciprocal(t_ds[:, 1, :], t_ds[:, 0, :])\
                   .then_inc(sem.t_dve, 1)
                dve.wait_ge(sem.t_dve, b.at(PER.t_dve, 6))
                dve.tensor_scalar(t_ds[:, 2, :], t_ds[:, 1, :], col("gamma3"), None, ALU.mult)\
                   .then_inc(sem.t_dve, 1)
                dve.wait_ge(sem.t_dve, b.at(PER.t_dve, 7))
                dve.tensor_tensor(t_dn[:, :, :], qa[:, :, :],
                                  t_ds[:, 2, :].rearrange("p (t a) -> p t a", a=1).broadcast_to([C, T, D3 + 1]),
                                  ALU.mult).then_inc(sem.t_qs, 1)

            dve.wait_ge(s_const, 32)
            dve.wait_ge(s_ones, 8)
            dve.wait_ge(s_folded, 3)
            play(dve, dict(f_stat=f_stat, f_var=f_var, f_apply=f_apply, f_qk=f_qk, f_max=f_max,
                           f_shift=f_shift, f_sums=f_sums, f_out=f_out, p_stat=p_stat, p_var=p_var,
                           p_apply=p_apply, p_qk=p_qk, m_max_0=m_max_0, m_max_1=m_max_1, m_rows=m_rows, o_sums=o_sums,
                           o_divide=o_divide, o_residual=o_residual, t_norms=t_norms,
                           t_keys=t_keys, t_scale=t_scale))

        @block.tensor
        def _(pe):
            def mm(dst, lhsT, rhs, start=True, stop=True):
                return pe.matmul(dst, lhsT, rhs, start=start, stop=stop)

            def f_stat(n, b, layer):
                pe.wait_ge(sem.f_stat, n.at(PER.f_stat, 1))
                if layer == 0 and b.has_prev:
                    before = b.previous()
                    if before.has_prev:
                        pe.wait_ge(sem.t_ev, before.at(PER.t_ev, 0))
                    pe.wait_ge(sem.m_neg, before.at(PER.m_neg, 2))
                mm(P_F[:, 0:2], mat("group0" if layer == 0 else "ident"), f_mv[:, :])\
                    .then_inc(sem.f_gstat, 1)

            def f_qk(n, u, layer):
                if u == 0:
                    pe.wait_ge(sem.f_xn, n.at(PER.f_xn, 1))
                if u >= 2:
                    pe.wait_ge(sem.f_lo, n.at(PER.f_lo, u - 1))
                mm(P_F[:, half(u % 2)], mat(f"wq{layer}" if u < 2 else f"wk{layer}"),
                   xn[:, half(u % 2)]).then_inc(sem.f_qk, 1)

            def f_value(n, h, layer):
                pe.wait_ge(sem.f_lo, n.at(PER.f_lo, 3 + h))
                for t in range(4 * h, 4 * h + 4):
                    last = mm(P_F[:, tile(t)], xn[:, tile(t)], wvp0[:, :] if layer == 0 else mat("wv2"))
                last.then_inc(sem.f_v, 1)

            def f_max(n, u):
                if u < 2:
                    pe.wait_ge(sem.f_vout, n.at(PER.f_vout, u + 1))
                else:
                    pe.wait_ge(sem.f_max, n.at(PER.f_max, u - 1))
                mm(P_F[:, half(u % 2)], fq[0][:, tile(u // 2)], fk[0][:, half(u % 2)])\
                    .then_inc(sem.f_max_s, 1)

            def f_scores(n, u):
                h, kt = u // T, u % T
                if u == 0:
                    pe.wait_ge(sem.f_shift, n.at(PER.f_shift, 1))
                else:
                    pe.wait_ge(sem.f_p, n.at(PER.f_p, u))
                dst = P_F[:, half(0)]
                mm(dst, fk[0][:, tile(kt)], fq[0][:, half(h)], stop=False)
                mm(dst, fk[0][:, tile(kt)], fq[1][:, half(h)], start=False, stop=False)
                mm(dst, fk[1][:, tile(kt)], fq[0][:, half(h)], start=False, stop=False)
                mm(dst, ones_r[:, :], f_diag[:, 4 * h:4 * h + 4, :].rearrange("p t c -> p (t c)"),
                   start=False).then_inc(sem.f_sc, 1)

            def f_pv(n, u):
                h, kt = u // T, u % T
                pe.wait_ge(sem.f_p, n.at(PER.f_p, u + 1))
                if u == T:
                    pe.wait_ge(sem.f_t, n.at(PER.f_t, 1))
                mm(P_F[:, half(1)], fv[:, kt, :], fp[u % 3][:, :], start=kt == 0, stop=kt == T - 1)\
                    .then_inc(sem.f_pv, 1)

            def f_sums(n):
                pe.wait_ge(sem.f_sum, n.at(PER.f_sum, PER.f_sum))
                for t in range(T):
                    last = mm(P_F[:, t:t + 1], fsum[:, tile(t)], ones[:, 0:1])
                last.then_inc(sem.f_z, 1)

            def f_spread(n):
                pe.wait_ge(sem.f_r, n.at(PER.f_r, 1))
                pe.wait_ge(sem.f_t, n.at(PER.f_t, 2))
                for t in range(T):
                    last = mm(P_F[:, tile(t)], f_recip[:, t:t + 1].broadcast_to([C, C]), mat("ident"))
                last.then_inc(sem.f_rb, 1)

            def p_stat(b, n):
                pe.wait_ge(sem.p_stat, b.at(PER.p_stat, 1))
                mm(P_ODD[:, 0:2], mat("group1"), p_mv[:, :]).then_inc(sem.p_gstat, 1)

            def p_qk(b, u):
                if u == 0:
                    pe.wait_ge(sem.p_h, b.at(PER.p_h, 1))
                if u >= 2:
                    pe.wait_ge(sem.p_lo, b.at(PER.p_lo, u - 1))
                mm(P_ODD[:, half(u % 2)], mat("wq1" if u < 2 else "wk1"),
                   h1[:, half(u % 2)]).then_inc(sem.p_qk, 1)

            def p_value(b, h):
                pe.wait_ge(sem.p_lo, b.at(PER.p_lo, 3 + h))
                for t in range(4 * h, 4 * h + 4):
                    last = mm(P_ODD[:, tile(t)], h1[:, tile(t)], mat("wv1"))
                last.then_inc(sem.p_v, 1)

            def m_max_0(b, u):
                h, t = u // T, u % T
                if u == 0:
                    pe.wait_ge(sem.stacked_first, b.at(PER.stacked_first, PER.stacked_first))
                    if b.has_prev:
                        pe.wait_ge(sem.o_n, b.at(PER.o_n, 0))
                elif u == 1:
                    pe.wait_ge(sem.p_vout, b.at(PER.p_vout, 2))
                else:
                    pe.wait_ge(sem.m_max, b.at(PER.m_max, u - 1))
                if u == 2 * T:
                    pe.wait_ge(sem.stacked_rest, b.at(PER.stacked_rest, PER.stacked_rest))
                for k in range(2):
                    last = mm((P_EVEN, P_ODD)[u % 2][:, half(k)], qs[0:SHIFT_ROW, h, tile(t)],
                              ks[0:SHIFT_ROW, h // 2, half(k)])
                last.then_inc(sem.m_s, 1)

            def m_max_1(b, u):
                h, t, k = G1 + u // (2 * T), u // 2 % T, u % 2
                if u < 2:
                    n = run2(b.previous(), False) if b.has_prev else run0(b)
                    pe.wait_ge(sem.f_out, n.at(PER.f_out, 1))
                else:
                    pe.wait_ge(sem.m_max, b.at(PER.m_max, 32 + u - 1))
                mm(P_F[:, half(k)], qs[0:SHIFT_ROW, h, tile(t)], ks[0:SHIFT_ROW, h // 2, half(k)])\
                    .then_inc(sem.m_s, 1)

            def m_rows(b, g, pair):
                if g == 0:
                    pe.wait_ge(sem.m_max, b.at(PER.m_max, 32))
                else:
                    pe.wait_ge(sem.m_both, b.at(PER.m_both, 1))
                mm(pair[0:G1 * T, 0:C], mx1[:, g, :], mat("neg_ident")).then_inc(sem.m_t, 1)

            def s_scores(b, g, u):
                kt, h = u // G1, G1 * g + u % G1
                if u == 0:
                    pe.wait_ge(sem.m_row, b.at(PER.m_row, 64 * (g + 1)))
                    if g == 0:
                        pe.wait_ge(sem.p_vout, b.at(PER.p_vout, 2))
                if 32 * g + u >= 2:
                    pe.wait_ge(sem.s_p, b.at(PER.s_p, 32 * g + u - 1))
                for k in range(2):
                    last = mm((P_EVEN, P_ODD)[u % 2][:, half(k)], ks[:, h // 2, tile(kt)],
                              qs[:, h, half(k)])
                last.then_inc(sem.s_sc, 1)

            def s_pv(b, g, kt, k):
                pe.wait_ge(sem.s_p, b.at(PER.s_p, 32 * g + G1 * (kt + 1)))
                if kt == 0 and k == 0 and g == 0 and b.has_prev:
                    pe.wait_ge(sem.o_x2, b.at(PER.o_x2, 0))
                if kt == 0 and k == 0 and g == 1:
                    pe.wait_ge(sem.o_ev, b.at(PER.o_ev, 1))
                for j in range(G1):
                    last = mm(P_ACC[32 * j:32 * j + 32, half(k)], v1[:, kt, G1 * g + j, :],
                              p1[kt % 2][:, j, half(k)], start=kt == 0, stop=kt == T - 1)
                if k == 1:
                    last.then_inc(sem.s_pv, 1)

            def o_sums(b, last_image):
                pe.wait_ge(sem.o_ev, b.at(PER.o_ev, 2))
                for g in range(2):
                    for t in range(T):
                        last = mm(P_ACC[:, g * HALF + t * G1:g * HALF + (t + 1) * G1],
                                  o1[g][:, tile(t)], col("zsel", G1))
                    last.then_inc(sem.o_z, 1)

            def o_spread(b, last_image):
                pe.wait_ge(sem.o_r, b.at(PER.o_r, 2))
                for g in range(2):
                    for t in range(T):
                        last = mm((P_ACC, P_EVEN)[g][:, tile(t)],
                                  rx[g][:, t, :, :].rearrange("p j a -> p (j a)"), mat("ident"))
                    last.then_inc(sem.o_rb, 1)

            def o_project(b):
                pe.wait_ge(sem.o_n, b.at(PER.o_n, 2))
                for k in range(2):
                    for g in range(2):
                        last = mm(P_ACC[:, half(k)], mat(("wp1a", "wp1b")[g]), o1[g][:, half(k)],
                                  start=g == 0, stop=g == 1)
                last.then_inc(sem.o_pj, 1)

            def t_project(b, n, k, beside):
                if k == 0:
                    pe.wait_ge(sem.f_out, n.at(PER.f_out, 1))
                    if beside:
                        pe.wait_ge(sem.m_neg, beside.at(PER.m_neg, 2))
                if k == 2:
                    pe.wait_ge(sem.t_tm, b.at(PER.t_tm, 1))
                for t in range(3 * k, min(3 * k + 3, T)):
                    dst = t_bank(k)[:, (t - 3 * k) * W3:(t - 3 * k + 1) * W3]
                    mm(dst, x3[:, tile(t)], col("w3", W3), stop=False)
                    last = mm(dst, ones[0:1, :], b3row[:, :], start=False)
                last.then_inc(sem.t_q, 1)

            def t_matrix(b):
                pe.wait_ge(sem.t_k, b.at(PER.t_k, 1))
                pe.wait_ge(sem.t_tm, b.at(PER.t_tm, 3))
                for t in range(T):
                    mm(P_F[0:D3 + 1, 0:C + 1], ka[:, t, :], tm[:, t, 2 * D3:W3 + 1],
                       start=t == 0, stop=t == T - 1)
                for t in range(T):
                    last = mm(P_F[:, HALF:HALF + D3 + 1], ones[:, :], ka[:, t, :],
                              start=t == 0, stop=t == T - 1)
                last.then_inc(sem.t_m, 1)

            def t_turn(b):
                pe.wait_ge(sem.t_qs, b.at(PER.t_qs, 1))
                pe.wait_ge(sem.t_ma, b.at(PER.t_ma, 1))
                for t in range(T):
                    last = mm(P_F[0:D3 + 1, tile(t)], t_dn[:, t, :], mat("ident"))
                last.then_inc(sem.t_tr, 1)

            def t_out(b):
                pe.wait_ge(sem.t_qt, b.at(PER.t_qt, 1))
                for k in range(2):
                    mm(P_F[:, half(k)], ma[:, :], qt3[:, half(k)]).then_inc(sem.t_o, 1)

            pe.wait_ge(s_const, 32)
            pe.wait_ge(s_ones, 8)
            mm(P_EVEN[:, 0:C], mat("wv0"), mat("wp0")).then_inc(s_fold, 1)
            mm(P_EVEN[:, C:C + 1], mat("wp0"), col("bv0")).then_inc(s_fold, 1)
            mm(P_EVEN[:, C + 1:C + 2], mat("wp1"), col("bv1")).then_inc(s_fold, 1)
            pe.wait_ge(s_folded, 3)
            play(pe, dict(f_stat=f_stat, f_qk=f_qk, f_value=f_value, f_max=f_max, f_scores=f_scores,
                          f_pv=f_pv, f_sums=f_sums, f_spread=f_spread, p_stat=p_stat, p_qk=p_qk,
                          p_value=p_value, m_max_0=m_max_0, m_max_1=m_max_1, m_rows=m_rows, s_scores=s_scores, s_pv=s_pv,
                          o_sums=o_sums, o_spread=o_spread, o_project=o_project,
                          t_project=t_project, t_matrix=t_matrix, t_turn=t_turn, t_out=t_out))


def kernel(x, **w):
    import numpy as np
    import concourse.bacc as bacc
    from concourse.bass_utils import run_bass_kernel_spmd as run

    a = {k: np.asarray(v) for k, v in w.items()}
    images = x.shape[0]

    packed = np.zeros((C, PACKED), np.float32)

    def put(name, value):
        packed[:, COL[name]:COL[name] + value.shape[1]] = value

    put("wq0", a["L0_conv_Wq"].T)
    put("wk0", a["L0_conv_Wk"].T)
    put("wv0", a["L0_conv_Wv"])
    put("wp0", a["L0_conv_Wp"].T)
    put("wq1", a["L1_conv_wq"].T)
    put("wk1", a["L1_conv_wk"].T)
    put("wv1", a["L1_conv_wv"].T)
    put("wp1", a["L1_conv_wp"].T)
    for g, name in enumerate(("wp1a", "wp1b")):
        for j in range(G1):
            h = G1 * g + j
            packed[32 * j:32 * j + DH, COL[name]:COL[name] + C] = a["L1_conv_wp"].T[h * DH:(h + 1) * DH]
    put("wq2", a["L2_conv_wq"].T)
    put("wk2", a["L2_conv_wk"].T)
    put("wv2", a["L2_conv_wv"].T)
    put("ident", np.eye(C, dtype=np.float32))
    put("neg_ident", -np.eye(C, dtype=np.float32))
    for name, group in (("group0", C // 8), ("group1", C // 32)):
        put(name, np.kron(np.eye(C // group), np.full((group, group), 1.0 / group)).astype(np.float32))
    put("w3", np.concatenate([a["L3_conv_Wq"].T, a["L3_conv_Wk"].T, a["L3_conv_Wv"].T], axis=1))
    for j in range(G1):
        packed[32 * j + DH, COL["zsel"] + j] = 1.0
    for name, key in dict(bq0="L0_conv_bq", bk0="L0_conv_bk", bv0="L0_conv_bv", bp0="L0_conv_bp",
                          gamma0="L0_conv_gamma", beta0="L0_conv_beta", bq1="L1_conv_bq",
                          bk1="L1_conv_bk", bv1="L1_conv_bv", bp1="L1_conv_bp",
                          gamma1="L1_conv_gn_w", beta1="L1_conv_gn_b", bq2="L2_conv_bq",
                          bk2="L2_conv_bk", bv2="L2_conv_bv").items():
        put(name, a[key].reshape(C, 1))
    put("gamma3", np.broadcast_to(a["L3_conv_gamma"].reshape(1, 1), (C, 1)))
    put("one", np.ones((C, 1), np.float32))
    bias3 = np.concatenate([a["L3_conv_bq"], a["L3_conv_bk"], a["L3_conv_bv"]]).reshape(1, W3)

    nc = bacc.Bacc("TRN2", target_bir_lowering=False, num_devices=1)
    arrays = {"x_dram": np.ascontiguousarray(x).reshape(images, C, N), "packed_dram": packed,
              "bias3_dram": np.ascontiguousarray(bias3)}
    args = [nc.dram_tensor(k, v.shape, F32, kind="ExternalInput").ap() for k, v in arrays.items()]
    args.append(nc.dram_tensor("out_dram", (images, C, N), F32, kind="ExternalOutput").ap())
    heads_kernel(nc, images, *args)
    r = run(nc, [arrays], core_ids=[0])
    return r.results[0]["out_dram"].reshape(x.shape)
```

```python
import concourse.bass as bass
from concourse import mybir
from contextlib import ExitStack

F32 = mybir.dt.float32
F32R = mybir.dt.float32r
ALU = mybir.AluOpType
ACT = mybir.ActivationFunctionType
AX = mybir.AxisListType

C = 128
N = 1024
HALF = N // 2
T = N // C
HEADS, DH = 8, 16
A_END, B_END, C_PAUSE, C_END, FM, PP, F_END, SPLIT, TN, TK, OS, OD, IS, GS, FS, FO, M0, MP, M_FULL, MH, FM0, R_END = 0.92, 1.0, 0, 0.9, 2, (6, 4), 0.9, 16, 8, 4, 6, 6, 6, 4, 8, 6, 2, 0, 34, 3, 3, 0.9
G1 = 4
EPS = 1e-5
EPS3 = 1e-6
PAIR = 2 * DH
SHIFT_ROW = 3 * PAIR
D3 = 16
W3 = 2 * D3 + C

MATRICES = ["wq0", "wk0", "wv0", "wp0", "wq1", "wk1", "wv1", "wp1", "wp1a", "wp1b",
            "wq2", "wk2", "wv2", "ident", "neg_ident", "group0", "group1"]
VECTORS = ["bq0", "bk0", "bv0", "bp0", "gamma0", "beta0", "bq1", "bk1", "bv1", "bp1",
           "gamma1", "beta1", "bq2", "bk2", "bv2", "gamma3", "one", "zero"]
COL = {name: C * i for i, name in enumerate(MATRICES)}
COL["w3"] = C * len(MATRICES)
COL["zsel"] = COL["w3"] + W3
COL.update({name: COL["zsel"] + G1 + i for i, name in enumerate(VECTORS)})
PACKED = COL["zsel"] + G1 + len(VECTORS)


class Batch:

    def __init__(self, index, plus=0, times=1):
        self.index, self.plus, self.times = index, plus, times

    @property
    def has_prev(self):
        return not isinstance(self.index, int) or self.times * self.index + self.plus > 0

    def at(self, per_batch, count):
        return self.index * (self.times * per_batch) + (self.plus * per_batch + count)

    def previous(self):
        return Batch(self.index, self.plus - 1, self.times)

    def next(self):
        return Batch(self.index, self.plus + 1, self.times)


class PER:
    x_loaded = 16
    g_stat = 1
    g_gstat = 1
    g_veps = 1
    g_rstd = 1
    g_xn = 1
    g_dve = 6
    i_veps = 1
    i_rstd = 1
    i_xn = 1
    i_dve = 3
    f_qk = 4
    f_hi = 4
    f_lo = 4
    f_v = 2
    f_vout = 2
    f_max_s = 16
    f_max = 16
    f_shift = 2
    f_sc = 16
    f_p = 16
    f_pv = 16
    f_sum = 14
    f_t = 2
    f_z = 1
    f_r = 1
    f_rb = 1
    f_out = 1
    f_div = 1
    f_dve = 2
    p_stat = 1
    p_gstat = 1
    p_veps = 1
    p_rstd = 1
    p_h = 1
    p_qk = 4
    p_hi = 4
    p_lo = 4
    p_v = 2
    p_vout = 2
    p_res = 1
    p_dve = 6
    stacked_first = 9 * 16
    stacked_rest = 27 * 16
    m_s = M_FULL + 2 * (HEADS * T - M_FULL)
    m_max = M_FULL + 2 * (HEADS * T - M_FULL)
    m_both = 1
    m_t = 2
    m_neg = 2
    m_row = 2 * 4 * 16
    s_sc = 64
    s_p = 64
    s_pv = 16
    o_ev = 2
    o_z = 2
    o_r = 2
    o_rb = 2
    o_n = 2
    o_pj = 1
    o_x2 = 1
    o_dve = 2
    t_q = 3
    t_tm = 3
    t_ns = 1
    t_rn = 1
    t_k = 1
    t_m = 1
    t_ma = 1
    t_qs = 1
    t_tr = 1
    t_qt = 1
    t_o = 2
    t_ev = 2
    t_dve = 7
    stored = 16


class Semaphores:
    def __init__(self, new):
        self.x_loaded = new("x_loaded")
        self.g_stat = new("g_stat")
        self.g_gstat = new("g_gstat")
        self.g_veps = new("g_veps")
        self.g_rstd = new("g_rstd")
        self.g_xn = new("g_xn")
        self.g_dve = new("g_dve")
        self.i_veps = new("i_veps")
        self.i_rstd = new("i_rstd")
        self.i_xn = new("i_xn")
        self.i_dve = new("i_dve")
        self.f_qk = new("f_qk")
        self.f_hi = new("f_hi")
        self.f_lo = new("f_lo")
        self.f_v = new("f_v")
        self.f_vout = new("f_vout")
        self.f_max_s = new("f_max_s")
        self.f_max = new("f_max")
        self.f_shift = new("f_shift")
        self.f_sc = new("f_sc")
        self.f_p = new("f_p")
        self.f_pv = new("f_pv")
        self.f_sum = new("f_sum")
        self.f_t = new("f_t")
        self.f_z = new("f_z")
        self.f_r = new("f_r")
        self.f_rb = new("f_rb")
        self.f_out = new("f_out")
        self.f_div = new("f_div")
        self.f_dve = new("f_dve")
        self.p_stat = new("p_stat")
        self.p_gstat = new("p_gstat")
        self.p_veps = new("p_veps")
        self.p_rstd = new("p_rstd")
        self.p_h = new("p_h")
        self.p_qk = new("p_qk")
        self.p_hi = new("p_hi")
        self.p_lo = new("p_lo")
        self.p_v = new("p_v")
        self.p_vout = new("p_vout")
        self.p_res = new("p_res")
        self.p_dve = new("p_dve")
        self.stacked_first = new("stacked_first")
        self.stacked_rest = new("stacked_rest")
        self.m_s = new("m_s")
        self.m_max = new("m_max")
        self.m_both = new("m_both")
        self.m_t = new("m_t")
        self.m_neg = new("m_neg")
        self.m_row = new("m_row")
        self.s_sc = new("s_sc")
        self.s_p = new("s_p")
        self.s_pv = new("s_pv")
        self.o_ev = new("o_ev")
        self.o_z = new("o_z")
        self.o_r = new("o_r")
        self.o_rb = new("o_rb")
        self.o_n = new("o_n")
        self.o_pj = new("o_pj")
        self.o_x2 = new("o_x2")
        self.o_dve = new("o_dve")
        self.t_q = new("t_q")
        self.t_tm = new("t_tm")
        self.t_ns = new("t_ns")
        self.t_rn = new("t_rn")
        self.t_k = new("t_k")
        self.t_m = new("t_m")
        self.t_ma = new("t_ma")
        self.t_qs = new("t_qs")
        self.t_tr = new("t_tr")
        self.t_qt = new("t_qt")
        self.t_o = new("t_o")
        self.t_ev = new("t_ev")
        self.t_dve = new("t_dve")
        self.stored = new("stored")


def heads_kernel(nc, images, x, packed, bias3, out):
    ctx = ExitStack()
    with ctx:
        def sb(name, shape, dtype=F32):
            return ctx.enter_context(nc.sbuf_tensor(name, shape, dtype))

        cw = sb("cw", [C, PACKED])
        b3row = sb("b3row", [1, W3])
        ones = sb("ones", [C, C])
        ones_r = sb("ones_r", [C, C], F32R)
        minus_half = sb("minus_half", [C, 16])
        wvp0 = sb("wvp0", [C, C])
        const_bias = sb("const_bias", [C, 2])

        x_in = sb("x_in", [C, N])
        g_bn = sb("g_bn", [C, 2, 6])
        g_mv = sb("g_mv", [C, 2])
        g_gs = sb("g_gs", [C, 2])
        g_ve = sb("g_ve", [C, 2])
        g_rs = sb("g_rs", [C, 1])
        g_ac = sb("g_ac", [C, 2])
        i_bn = sb("i_bn", [C, 2, 6])
        i_mv = sb("i_mv", [C, 2])
        i_ve = sb("i_ve", [C, 1])
        i_rs = sb("i_rs", [C, 1])
        i_ac = sb("i_ac", [C, 1])
        xn = sb("xn", [C, N])

        fq2 = [sb("fq2_hi", [C, N], F32R), sb("fq2_lo", [C, N], F32R)]
        fk2 = [sb("fk2_hi", [C, N], F32R), sb("fk2_lo", [C, N], F32R)]
        fv = sb("fv", [C, T, C])
        f_mx2 = sb("f_mx2", [C, T, 2])
        f_mx = sb("f_mx", [C, T])
        f_diag = sb("f_diag", [C, T, C], F32R)
        fp = [sb(f"fp{i}", [C, HALF]) for i in range(3)]
        fsum = sb("fsum", [C, N])
        f_recip = sb("f_recip", [C, T])
        f_num = sb("f_num", [C, N])
        x1 = sb("x1", [C, N])
        x2 = sb("x2", [C, N])
        x3 = sb("x3", [C, N])

        x1_res = sb("x1_res", [C, N])
        p_bn = sb("p_bn", [C, 2, 6])
        p_mv = sb("p_mv", [C, 2])
        p_gs = sb("p_gs", [C, 2])
        p_ve = sb("p_ve", [C, 2])
        p_rs = sb("p_rs", [C, 1])
        p_ac = sb("p_ac", [C, 2])
        h1 = sb("h1", [C, N])
        cq = fq0 = [sb("cq_hi", [C, N], F32R), sb("cq_lo", [C, N], F32R)]
        ck = fk0 = [sb("ck_hi", [C, N], F32R), sb("ck_lo", [C, N], F32R)]
        qs = sb("qs", [C, HEADS, N], F32R)
        ks = sb("ks", [C, HEADS // 2, N], F32R)
        v1 = sb("v1", [C, T, HEADS, 32])
        mx_half = sb("mx_half", [C, G1 * T, 2])
        mx1 = sb("mx1", [C, 2, G1 * T])
        neg = sb("neg", [G1 * T, 2, C], F32R)
        p1 = [sb(f"p1_{i}", [C, G1, N]) for i in range(2)]
        o1 = [sb(f"o1_{g}", [C, N]) for g in range(2)]
        rz = [sb(f"rz{g}", [C, T, G1]) for g in range(2)]
        xn2 = p1[0][:, 2, :]
        rx = [p1[0][:, g, :].rearrange("p (t j r) -> p t j r", t=T, j=G1) for g in range(2)]

        tm = sb("tm", [C, T, W3 + 1])
        t_sq = sb("t_sq", [C, T, 2, D3])
        t_ns = sb("t_ns", [C, T * 2])
        t_rn = sb("t_rn", [C, T * 2])
        qa = sb("qa", [C, T, D3 + 1])
        ka = sb("ka", [C, T, D3 + 1])
        ma = sb("ma", [D3 + 1, C])
        wb = sb("wb", [C, D3 + 1])
        t_dn = sb("t_dn", [C, T, D3 + 1])
        t_ds = sb("t_ds", [C, 3, T])
        qt3 = sb("qt3", [D3 + 1, N])

        pairs = [ctx.enter_context(nc.psum_tensor(f"pair{i}", [C, N], F32)) for i in range(4)]
        P_EVEN, P_ODD, P_ACC, P_F = pairs

        def full_pair(layer):
            return P_F if layer == 0 else P_ACC

        def queries(layer):
            return fq0 if layer == 0 else fq2

        def keys(layer):
            return fk0 if layer == 0 else fk2

        def t_bank(k):
            return P_F[:, half(k % 2)]

        sem = Semaphores(lambda name: ctx.enter_context(nc.semaphore(name)))
        s_const = ctx.enter_context(nc.semaphore("s_const"))
        s_ones = ctx.enter_context(nc.semaphore("s_ones"))
        s_fill = ctx.enter_context(nc.semaphore("s_fill"))
        s_fold = ctx.enter_context(nc.semaphore("s_fold"))
        s_folded = ctx.enter_context(nc.semaphore("s_folded"))

        def col(name, width=1):
            return cw[:, COL[name]:COL[name] + width]

        def mat(name):
            return col(name, C)

        def f32(ap):
            return ap.bitcast(F32)

        def tile(t):
            return slice(t * C, (t + 1) * C)

        def half(h):
            return slice(h * HALF, (h + 1) * HALF)

        def sums_through(u):
            return (T - 1) * (u // T) + max(u % T, 1)


        def group_norm(b):
            yield ("g_stat", GS, b)
            yield ("g_var", GS, b)
            yield ("g_apply", GS, b)

        def full_project(n, b, layer):
            for u in range(4):
                yield ("f_qk", 4, n, b, u, layer)

        def full_maxima(n, layer):
            for u in range(2 * T):
                yield ("f_max", FM if layer else FM0, n, u, layer)

        def full_values(n, layer):
            for h in range(2):
                yield ("f_value", 4, n, h, layer)
                yield ("f_shift", 0, n, h)

        def full_products(n, layer):
            for u in range(2 * T):
                yield ("f_scores", 4, n, u, layer)
                if u:
                    yield ("f_pv", 4, n, u - 1, layer)
            yield ("f_pv", 4, n, 2 * T - 1, layer)

        def full_finish(n, b, layer):
            yield ("f_sums", FS, n, layer)
            yield ("f_spread", 10, n, layer)
            yield ("f_out", FO, n, b, layer)

        def full_attention(n, b, layer):
            yield from full_project(n, b, layer)
            yield from full_maxima(n, layer)
            yield from full_values(n, layer)
            yield from full_products(n, layer)
            yield from full_finish(n, b, layer)

        def heads(b, g):
            for u in range(G1 * T):
                kt, j = u // G1, u % G1
                yield ("s_scores", 2, b, g, u)
                if kt and j % 2:
                    yield ("s_pv", 4, b, g, kt - 1, j // 2)
            if g == 1:
                yield ("o_sums", 4, b, 0)
            yield ("s_pv", 4, b, g, T - 1, 0)
            yield ("s_pv", 4, b, g, T - 1, 1)
            yield ("s_out", 0, b, g)

        def maxima(b):
            for u in range(M_FULL):
                yield ("m_max", M0, b, u)
                if u == G1 * T - 1:
                    yield ("m_rows", 1, b, 0)

        def rest_of_maxima(b):
            for v in range(2 * (HEADS * T - M_FULL)):
                yield ("m_half", MH, b, v)
            yield from pause(MP)
            yield ("m_rows", 1, b, 1)

        def prepare(b, n):
            yield ("p_stat", 0, b, n)
            yield from pause(PP[0])
            yield ("p_average", 0, b)
            yield ("p_var", 2, b)
            yield ("p_apply", 2, b)
            yield from pause(PP[1])
            for u in range(4):
                yield ("p_qk", 4, b, u)
            yield ("p_stack", 0, b)
            for h in range(2):
                yield ("p_value", 4, b, h)

        def finish_heads(b):
            yield ("o_spread", 5, b, 0)
            yield ("o_sums", OS, b, 1)
            yield ("o_divide", OD // 2, b, 0)
            yield ("o_spread", 5, b, 1)
            yield ("o_divide", OD // 2, b, 1)
            yield ("o_project", 8, b)
            yield ("o_residual", 4, b)
            yield ("i_stat", IS, b)
            yield ("i_apply", IS, b)

        def linear_attention(b, n, beside):
            for k in range(3):
                yield ("t_project", 6, b, n, k, beside)
            yield ("t_norms", TN, b)
            yield ("t_keys", TK, b)
            yield ("t_matrix", 8, b)
            yield ("t_scale", 6, b)
            yield ("t_turn", 4, b)
            yield ("t_out", 8, b)

        def pause(cost):
            yield ("pause", cost)

        def after(name):
            yield ("after", 0, name)

        def merged(main, side, end=1.0):
            main, side = list(main), list(side)
            pace = (sum(s[1] for s in side) or 1) / (end * sum(s[1] for s in main) or 1)
            done = at = spent = 0
            for step in main:
                if step[0] == "after":
                    needed = max(i + 1 for i, s in enumerate(side) if s[0] == step[2])
                else:
                    needed = 0
                while at < len(side) and (spent < done * pace or at < needed):
                    yield side[at]
                    spent += side[at][1]
                    at += 1
                yield step
                done += step[1]
            yield from side[at:]

        def run0(b):
            return Batch(0) if isinstance(b.index, int) and b.index + b.plus == 0 else \
                Batch(b.index, 2 * b.plus - 1, 2)

        def run2(b, last):
            return Batch(b.index, 2 * b.plus + (1 if last else 2), 2)

        def first():
            b = Batch(0)
            yield ("load", 0, b)
            yield from group_norm(b)
            yield from full_attention(run0(b), b, 0)
            yield from prepare(b, run0(b))
            yield ("p_residual", 0, b, run0(b))
            yield from maxima(b)

        def image(b, last):
            nxt, n2 = b.next(), run2(b, last)
            if not last:
                yield ("load", 0, nxt)
            before = [*linear_attention(b.previous(), run2(b.previous(), False), b)] if b.has_prev else []
            if last:
                yield from merged([*heads(b, 0), *after("m_rows"), *heads(b, 1)], [*rest_of_maxima(b), *before], B_END)
                yield from finish_heads(b)
                yield from full_attention(n2, b, 2)
                yield from linear_attention(b, n2, b)
            else:
                n0 = run0(nxt)
                products = [*full_products(n0, 0)]
                first_products, rest_products = products[:SPLIT], products[SPLIT:]
                yield from merged([*heads(b, 0), *after("m_rows"), *heads(b, 1)],
                                  [*rest_of_maxima(b), *before, *group_norm(nxt),
                                   *full_project(n0, nxt, 0), *full_maxima(n0, 0),
                                   *full_values(n0, 0), *first_products], B_END)
                yield from merged(rest_products, finish_heads(b), R_END)
                yield from merged([*full_project(n2, b, 2), *full_maxima(n2, 2)],
                                  [*full_finish(n0, nxt, 0), *prepare(nxt, n0),
                                   ("p_residual", 0, nxt, n0)], F_END)
                yield from merged([*full_values(n2, 2), *full_products(n2, 2),
                                   *full_finish(n2, b, 2)],
                                  [*pause(C_PAUSE), *maxima(nxt)], C_END)

        def play(eng, steps):
            def do(order):
                for name, _, *args in order:
                    if name in steps:
                        steps[name](*args)
            do(first())
            do(image(Batch(0), images == 1))
            if images > 2:
                with eng.Fori(1, images - 1) as i:
                    do(image(Batch(i), False))
            if images > 1:
                do(image(Batch(images - 1), True))

        block = ctx.enter_context(nc.Block())

        @block.sync
        def _(sp):
            sp.dma_start(cw[:, :], packed).then_inc(s_const, 16)
            sp.dma_start(b3row[:, :], bias3).then_inc(s_const, 16)

            def one(images_ap, b):
                i = b.at(1, 0)
                if isinstance(i, int):
                    return images_ap[i, :, :]
                return images_ap[bass.ds(i, 1), :, :].rearrange("a c n -> (a c) n")

            def load(b):
                if b.has_prev:
                    sp.wait_ge(sem.g_xn, b.at(PER.g_xn, 0))
                sp.dma_start(x_in[:, :], one(x, b)).then_inc(sem.x_loaded, 16)

            def p_stack(b):
                def stack_keys(part, t, row, done):
                    sp.dma_start(f32(ks[row:row + PAIR, t, :]),
                                 f32(ck[part][t * PAIR:(t + 1) * PAIR, :])).then_inc(done, 16)

                def stack_queries(part, t, row, done):
                    for e in range(2):
                        h = 2 * t + e
                        sp.dma_start(f32(qs[row + e * DH:row + (e + 1) * DH, h, :]),
                                     f32(cq[part][h * DH:(h + 1) * DH, :])).then_inc(done, 16)

                sp.wait_ge(sem.p_hi, b.at(PER.p_hi, 2))
                stack_queries(0, 0, 0, sem.stacked_first)
                stack_queries(0, 0, 2 * PAIR, sem.stacked_first)
                sp.wait_ge(sem.p_lo, b.at(PER.p_lo, 2))
                stack_queries(1, 0, PAIR, sem.stacked_first)
                sp.wait_ge(sem.p_hi, b.at(PER.p_hi, 4))
                stack_keys(0, 0, 0, sem.stacked_first)
                stack_keys(0, 0, PAIR, sem.stacked_first)
                sp.wait_ge(sem.p_lo, b.at(PER.p_lo, 4))
                stack_keys(1, 0, 2 * PAIR, sem.stacked_first)
                for t in range(1, HEADS // 2):
                    stack_queries(0, t, 0, sem.stacked_rest)
                    stack_queries(0, t, 2 * PAIR, sem.stacked_rest)
                    stack_queries(1, t, PAIR, sem.stacked_rest)
                    stack_keys(0, t, 0, sem.stacked_rest)
                    stack_keys(0, t, PAIR, sem.stacked_rest)
                    stack_keys(1, t, 2 * PAIR, sem.stacked_rest)

            def m_rows(b, g):
                sp.wait_ge(sem.m_neg, b.at(PER.m_neg, g + 1))
                for j in range(G1):
                    sp.dma_start(f32(qs[SHIFT_ROW:SHIFT_ROW + 1, G1 * g + j, :]),
                                 f32(neg[j * T:(j + 1) * T, g, :])).then_inc(sem.m_row, 16)

            def t_out(b):
                sp.wait_ge(sem.t_ev, b.at(PER.t_ev, 2))
                sp.dma_start(one(out, b), x3[:, :]).then_inc(sem.stored, 16)

            sp.wait_ge(s_fill, 2)
            play(sp, dict(load=load, p_stack=p_stack, m_rows=m_rows, t_out=t_out))
            sp.wait_ge(sem.stored, 16 * images)

        @block.gpsimd
        def _(pool):
            pool.memset(f32(qs[:, :, :]), 0.0).then_inc(s_fill, 1)
            pool.memset(f32(ks[:, :, :]), 1.0).then_inc(s_fill, 1)
            pool.memset(ones[:, :], 1.0).then_inc(s_ones, 1)
            pool.memset(f32(ones_r[:, :]), 1.0).then_inc(s_ones, 1)
            pool.memset(minus_half[:, :], -0.5).then_inc(s_ones, 1)
            pool.memset(v1[:, :, :, :], 0.0).then_inc(s_ones, 1)
            pool.memset(tm[:, :, W3:W3 + 1], 1.0).then_inc(s_ones, 1)
            pool.memset(qa[:, :, D3:D3 + 1], 1.0).then_inc(s_ones, 1)
            pool.memset(ka[:, :, D3:D3 + 1], 1.0).then_inc(s_ones, 1)
            pool.wait_ge(s_ones, 7)
            pool.memset(v1[:, :, :, DH:DH + 1], 1.0).then_inc(s_ones, 1)

            def g_var(b):
                pool.wait_ge(sem.g_veps, b.at(PER.g_veps, 1))
                pool.tensor_tensor(g_rs[:, :], g_ve[:, 1:2], minus_half[:, 0:1], ALU.pow)\
                    .then_inc(sem.g_rstd, 1)

            def i_stat(b):
                pool.wait_ge(sem.i_veps, b.at(PER.i_veps, 1))
                pool.tensor_tensor(i_rs[:, :], i_ve[:, :], minus_half[:, 0:1], ALU.pow)\
                    .then_inc(sem.i_rstd, 1)

            def f_pv(n, u, layer):
                h, kt = u // T, u % T
                dst = fsum[:, half(h)]
                pool.wait_ge(sem.f_p, n.at(PER.f_p, u + 1))
                if kt == 1:
                    if u == 1:
                        if n.has_prev:
                            pool.wait_ge(sem.f_z, n.at(PER.f_z, 0))
                    pool.tensor_tensor(dst, fp[(u - 1) % 3][:, :], fp[u % 3][:, :], ALU.add)\
                        .then_inc(sem.f_sum, 1)
                elif kt > 1:
                    pool.wait_ge(sem.f_sum, n.at(PER.f_sum, sums_through(u) - 1))
                    pool.tensor_tensor(dst, dst, fp[u % 3][:, :], ALU.add).then_inc(sem.f_sum, 1)

            def p_var(b):
                pool.wait_ge(sem.p_veps, b.at(PER.p_veps, 1))
                pool.tensor_tensor(p_rs[:, :], p_ve[:, 1:2], minus_half[:, 0:1], ALU.pow)\
                    .then_inc(sem.p_rstd, 1)

            def p_residual(b, n):
                if b.has_prev:
                    pool.wait_ge(sem.o_x2, b.at(PER.o_x2, 0))
                pool.wait_ge(sem.f_out, n.at(PER.f_out, 1))
                pool.tensor_tensor(x1_res[:, :], x1[:, :], const_bias[:, 1:2].broadcast_to([C, N]),
                                   ALU.add).then_inc(sem.p_res, 1)

            def t_norms(b):
                pool.wait_ge(sem.t_ns, b.at(PER.t_ns, 1))
                pool.tensor_tensor(t_rn[:, :], t_ns[:, :], minus_half[:, :], ALU.pow)\
                    .then_inc(sem.t_rn, 1)

            pool.wait_ge(s_folded, 3)
            play(pool, dict(g_var=g_var, i_stat=i_stat, f_pv=f_pv, p_var=p_var, p_residual=p_residual,
                            t_norms=t_norms))

        @block.scalar
        def _(act):
            def f_qk(n, b, u, layer):
                if layer == 0 and u == 0 and b.has_prev:
                    act.wait_ge(sem.stacked_first, b.at(PER.stacked_first, 0))
                    act.wait_ge(sem.stacked_rest, b.at(PER.stacked_rest, 0))
                dst, bias = (queries(layer), f"bq{layer}") if u < 2 else (keys(layer), f"bk{layer}")
                act.wait_ge(sem.f_qk, n.at(PER.f_qk, u + 1))
                act.activation(dst[0][:, half(u % 2)], full_pair(layer)[:, half(u % 2)], ACT.Identity,
                               bias=col(bias)).then_inc(sem.f_hi, 1)

            def f_value(n, h, layer):
                act.wait_ge(sem.f_v, n.at(PER.f_v, h + 1))
                act.activation(fv[:, 4 * h:4 * h + 4, :].rearrange("p t c -> p (t c)"), full_pair(layer)[:, half(h)],
                               ACT.Copy).then_inc(sem.f_vout, 1)

            def f_scores(n, u, layer):
                act.wait_ge(sem.f_sc, n.at(PER.f_sc, u + 1))
                if u >= 3:
                    act.wait_ge(sem.f_pv, n.at(PER.f_pv, u - 2))
                    act.wait_ge(sem.f_sum, n.at(PER.f_sum, sums_through(u - 3)))
                else:
                    if n.has_prev:
                        act.wait_ge(sem.f_pv, n.at(PER.f_pv, 0))
                    if n.has_prev:
                        act.wait_ge(sem.f_sum, n.at(PER.f_sum, 0))
                act.activation(fp[u % 3][:, :], full_pair(layer)[:, half(0)], ACT.Exp, scale=float(C) ** -0.5)\
                    .then_inc(sem.f_p, 1)

            def f_pv(n, u, layer):
                if u % T == T - 1:
                    h = u // T
                    act.wait_ge(sem.f_pv, n.at(PER.f_pv, u + 1))
                    if h == 0:
                        if n.has_prev:
                            act.wait_ge(sem.f_out, n.at(PER.f_out, 0))
                    act.activation(f_num[:, half(h)], full_pair(layer)[:, half(1)], ACT.Copy).then_inc(sem.f_t, 1)

            def p_qk(b, u):
                dst, bias = (cq, "bq1") if u < 2 else (ck, "bk1")
                act.wait_ge(sem.p_qk, b.at(PER.p_qk, u + 1))
                act.activation(dst[0][:, half(u % 2)], P_ODD[:, half(u % 2)], ACT.Identity,
                               bias=col(bias)).then_inc(sem.p_hi, 1)

            def p_value(b, h):
                act.wait_ge(sem.p_v, b.at(PER.p_v, h + 1))
                act.activation(v1[:, 4 * h:4 * h + 4, :, 0:DH],
                               P_ODD[:, half(h)].rearrange("p (t h d) -> p t h d", t=4, h=HEADS),
                               ACT.Copy).then_inc(sem.p_vout, 1)

            def s_scores(b, g, u):
                kt, j = u // G1, u % G1
                act.wait_ge(sem.s_sc, b.at(PER.s_sc, 32 * g + u + 1))
                if 8 * g + kt >= 2:
                    if j == 0:
                        act.wait_ge(sem.s_pv, b.at(PER.s_pv, 8 * g + kt - 1))
                elif j == 0:
                    if b.has_prev:
                        act.wait_ge(sem.s_pv, b.at(PER.s_pv, 0))
                        act.wait_ge(sem.o_rb, b.at(PER.o_rb, 0))
                act.activation(p1[kt % 2][:, j, :], (P_EVEN, P_ODD)[u % 2][:, :], ACT.Exp,
                               scale=float(DH) ** -0.5).then_inc(sem.s_p, 1)

            def s_out(b, g):
                act.wait_ge(sem.s_pv, b.at(PER.s_pv, 8 * (g + 1)))
                if b.has_prev:
                    act.wait_ge(sem.o_pj, b.at(PER.o_pj, 0))
                act.activation(o1[g][:, :], P_ACC[:, :], ACT.Copy).then_inc(sem.o_ev, 1)

            def t_project(b, n, k, beside):
                t0, t1 = 3 * k, min(3 * k + 3, T)
                act.wait_ge(sem.t_q, b.at(PER.t_q, k + 1))
                act.activation(tm[:, t0:t1, 0:W3],
                               t_bank(k)[:, 0:(t1 - t0) * W3].rearrange("p (t w) -> p t w", w=W3),
                               ACT.Copy).then_inc(sem.t_tm, 1)

            def t_matrix(b):
                act.wait_ge(sem.t_m, b.at(PER.t_m, 1))
                act.activation(ma[:, :], P_F[0:D3 + 1, 0:C], ACT.Copy).then_inc(sem.t_ma, 1)

            def t_turn(b):
                act.wait_ge(sem.t_tr, b.at(PER.t_tr, 1))
                act.activation(qt3[:, :], P_F[0:D3 + 1, :], ACT.Copy).then_inc(sem.t_qt, 1)

            def t_out(b):
                for h in range(2):
                    act.wait_ge(sem.t_o, b.at(PER.t_o, h + 1))
                    act.activation(x3[:, half(h)], P_F[:, half(h)], ACT.Copy).then_inc(sem.t_ev, 1)

            act.wait_ge(s_const, 32)
            act.wait_ge(s_ones, 8)
            act.wait_ge(s_fold, 3)
            act.activation(wvp0[:, :], P_EVEN[:, 0:C], ACT.Copy).then_inc(s_folded, 1)
            act.activation(const_bias[:, 0:1], P_EVEN[:, C:C + 1], ACT.Identity, bias=col("bp0"))\
               .then_inc(s_folded, 1)
            act.activation(const_bias[:, 1:2], P_EVEN[:, C + 1:C + 2], ACT.Identity, bias=col("bp1"))\
               .then_inc(s_folded, 1)
            play(act, dict(f_qk=f_qk, f_value=f_value, f_scores=f_scores, f_pv=f_pv, p_qk=p_qk,
                           p_value=p_value, s_scores=s_scores, s_out=s_out, t_project=t_project,
                           t_matrix=t_matrix, t_turn=t_turn, t_out=t_out))

        @block.vector
        def _(dve):
            def g_stat(b):
                dve.wait_ge(sem.x_loaded, b.at(PER.x_loaded, 16))
                dve.bn_stats(g_bn[:, 0, :], x_in[:, half(0)])
                dve.bn_stats(g_bn[:, 1, :], x_in[:, half(1)]).then_inc(sem.g_dve, 1)
                dve.wait_ge(sem.g_dve, b.at(PER.g_dve, 1))
                dve.memset(g_ve[:, :], 0.0)
                dve.bn_aggr(g_mv[:, :], g_bn[:, :, :].rearrange("p a s -> p (a s)"))\
                   .then_inc(sem.g_dve, 1)
                dve.wait_ge(sem.g_dve, b.at(PER.g_dve, 2))
                dve.scalar_tensor_tensor(out=g_mv[:, 1:2], in0=g_mv[:, 0:1],
                                         scalar=g_mv[:, 0:1], in1=g_mv[:, 1:2],
                                         op0=ALU.mult, op1=ALU.add).then_inc(sem.g_stat, 1)

            def g_var(b):
                dve.wait_ge(sem.g_gstat, b.at(PER.g_gstat, 1))
                dve.tensor_copy(g_gs[:, :], P_F[:, 0:2]).then_inc(sem.g_dve, 1)
                dve.wait_ge(sem.g_dve, b.at(PER.g_dve, 3))
                dve.scalar_tensor_tensor(out=g_ve[:, 0:1], in0=g_gs[:, 0:1],
                                         scalar=g_gs[:, 0:1], in1=g_gs[:, 1:2],
                                         op0=ALU.mult, op1=ALU.subtract).then_inc(sem.g_dve, 1)
                dve.wait_ge(sem.g_dve, b.at(PER.g_dve, 4))
                dve.tensor_scalar(g_ve[:, 1:2], g_ve[:, 0:1], -1.0, EPS, ALU.mult, ALU.add)\
                   .then_inc(sem.g_veps, 1)

            def g_apply(b):
                dve.wait_ge(sem.g_rstd, b.at(PER.g_rstd, 1))
                dve.tensor_scalar(g_ac[:, 0:1], g_rs[:, :], col("gamma0"), None, ALU.mult)\
                   .then_inc(sem.g_dve, 1)
                dve.wait_ge(sem.g_dve, b.at(PER.g_dve, 5))
                dve.scalar_tensor_tensor(out=g_ac[:, 1:2], in0=g_gs[:, 0:1],
                                         scalar=g_ac[:, 0:1], in1=col("beta0"),
                                         op0=ALU.mult, op1=ALU.subtract).then_inc(sem.g_dve, 1)
                dve.wait_ge(sem.g_dve, b.at(PER.g_dve, 6))
                dve.tensor_scalar(xn[:, :], x_in[:, :], g_ac[:, 0:1], g_ac[:, 1:2], ALU.mult,
                                  ALU.subtract).then_inc(sem.g_xn, 1)

            def i_stat(b):
                dve.wait_ge(sem.o_x2, b.at(PER.o_x2, 1))
                dve.bn_stats(i_bn[:, 0, :], x2[:, half(0)])
                dve.bn_stats(i_bn[:, 1, :], x2[:, half(1)]).then_inc(sem.i_dve, 1)
                dve.wait_ge(sem.i_dve, b.at(PER.i_dve, 1))
                dve.memset(i_ve[:, :], 0.0)
                dve.bn_aggr(i_mv[:, :], i_bn[:, :, :].rearrange("p a s -> p (a s)"))\
                   .then_inc(sem.i_dve, 1)
                dve.wait_ge(sem.i_dve, b.at(PER.i_dve, 2))
                dve.tensor_scalar(i_ve[:, :], i_mv[:, 1:2], EPS, None, ALU.add).then_inc(sem.i_veps, 1)

            def i_apply(b):
                dve.wait_ge(sem.i_rstd, b.at(PER.i_rstd, 1))
                dve.tensor_scalar(i_ac[:, :], i_mv[:, 0:1], i_rs[:, :], None, ALU.mult)\
                   .then_inc(sem.i_dve, 1)
                dve.wait_ge(sem.i_dve, b.at(PER.i_dve, 3))
                dve.tensor_scalar(xn2, x2[:, :], i_rs[:, :], i_ac[:, :], ALU.mult, ALU.subtract)\
                   .then_inc(sem.i_xn, 1)

            def f_qk(n, b, u, layer):
                if layer == 0 and u == 0 and b.has_prev:
                    dve.wait_ge(sem.stacked_first, b.at(PER.stacked_first, 0))
                    dve.wait_ge(sem.stacked_rest, b.at(PER.stacked_rest, 0))
                dst, bias = (queries(layer), f"bq{layer}") if u < 2 else (keys(layer), f"bk{layer}")
                dve.wait_ge(sem.f_hi, n.at(PER.f_hi, u + 1))
                h = half(u % 2)
                dve.scalar_tensor_tensor(out=dst[1][:, h], in0=full_pair(layer)[:, h], scalar=col(bias),
                                         in1=f32(dst[0][:, h]), op0=ALU.add, op1=ALU.subtract)\
                   .then_inc(sem.f_lo, 1)

            def f_max(n, u, layer):
                dve.wait_ge(sem.f_max_s, n.at(PER.f_max_s, u + 1))
                dve.reduce_max(f_mx2[:, u // 2, u % 2:u % 2 + 1], full_pair(layer)[:, half(u % 2)], AX.X)\
                   .then_inc(sem.f_max, 1)

            def f_shift(n, h):
                q = slice(h * T // 2, (h + 1) * T // 2)
                dve.wait_ge(sem.f_max, n.at(PER.f_max, T * (h + 1)))
                dve.tensor_tensor(f_mx[:, q], f_mx2[:, q, 0], f_mx2[:, q, 1], ALU.max)\
                   .then_inc(sem.f_dve, 1)
                dve.wait_ge(sem.f_dve, n.at(PER.f_dve, h + 1))
                if h == 0 and n.has_prev:
                    dve.wait_ge(sem.f_sc, n.at(PER.f_sc, 0))
                shape = [C, T // 2, C]
                dve.tensor_tensor(f_diag[:, q, :],
                                  mat("neg_ident").rearrange("p (a c) -> p a c", a=1).broadcast_to(shape),
                                  f_mx[:, q].rearrange("p (t a) -> p t a", a=1).broadcast_to(shape),
                                  ALU.mult).then_inc(sem.f_shift, 1)

            def f_sums(n, layer):
                dve.wait_ge(sem.f_z, n.at(PER.f_z, 1))
                dve.reciprocal(f_recip[:, :], full_pair(layer)[:, 0:T]).then_inc(sem.f_r, 1)

            def f_out(n, b, layer):
                dve.wait_ge(sem.f_rb, n.at(PER.f_rb, 1))
                dve.tensor_tensor(f_num[:, :], f_num[:, :], full_pair(layer)[:, :], ALU.mult)\
                   .then_inc(sem.f_div, 1)
                dve.wait_ge(sem.f_div, n.at(PER.f_div, 1))
                if layer == 0:
                    dst, bias, residual = x1, const_bias[:, 0:1], xn
                    if b.has_prev:
                        dve.wait_ge(sem.p_h, b.at(PER.p_h, 0))
                    if b.has_prev:
                        dve.wait_ge(sem.p_res, b.at(PER.p_res, 0))
                else:
                    dst, bias, residual = x3, col("bv2"), x2
                    if b.has_prev:
                        dve.wait_ge(sem.stored, b.at(PER.stored, 0))
                dve.scalar_tensor_tensor(out=dst[:, :], in0=f_num[:, :], scalar=bias,
                                         in1=residual[:, :], op0=ALU.add, op1=ALU.add)\
                   .then_inc(sem.f_out, 1)

            def p_stat(b, n):
                dve.wait_ge(sem.f_out, n.at(PER.f_out, 1))
                dve.bn_stats(p_bn[:, 0, :], x1[:, half(0)])
                dve.bn_stats(p_bn[:, 1, :], x1[:, half(1)]).then_inc(sem.p_dve, 1)
                dve.wait_ge(sem.p_dve, b.at(PER.p_dve, 1))
                dve.memset(p_ve[:, :], 0.0)
                dve.bn_aggr(p_mv[:, :], p_bn[:, :, :].rearrange("p a s -> p (a s)"))\
                   .then_inc(sem.p_dve, 1)
                dve.wait_ge(sem.p_dve, b.at(PER.p_dve, 2))
                dve.scalar_tensor_tensor(out=p_mv[:, 1:2], in0=p_mv[:, 0:1],
                                         scalar=p_mv[:, 0:1], in1=p_mv[:, 1:2],
                                         op0=ALU.mult, op1=ALU.add).then_inc(sem.p_stat, 1)

            def p_var(b):
                dve.wait_ge(sem.p_gstat, b.at(PER.p_gstat, 1))
                dve.tensor_copy(p_gs[:, :], P_ODD[:, 0:2]).then_inc(sem.p_dve, 1)
                dve.wait_ge(sem.p_dve, b.at(PER.p_dve, 3))
                dve.scalar_tensor_tensor(out=p_ve[:, 0:1], in0=p_gs[:, 0:1],
                                         scalar=p_gs[:, 0:1], in1=p_gs[:, 1:2],
                                         op0=ALU.mult, op1=ALU.subtract).then_inc(sem.p_dve, 1)
                dve.wait_ge(sem.p_dve, b.at(PER.p_dve, 4))
                dve.tensor_scalar(p_ve[:, 1:2], p_ve[:, 0:1], -1.0, EPS, ALU.mult, ALU.add)\
                   .then_inc(sem.p_veps, 1)

            def p_apply(b):
                dve.wait_ge(sem.p_rstd, b.at(PER.p_rstd, 1))
                dve.tensor_scalar(p_ac[:, 0:1], p_rs[:, :], col("gamma1"), None, ALU.mult)\
                   .then_inc(sem.p_dve, 1)
                dve.wait_ge(sem.p_dve, b.at(PER.p_dve, 5))
                dve.scalar_tensor_tensor(out=p_ac[:, 1:2], in0=p_gs[:, 0:1],
                                         scalar=p_ac[:, 0:1], in1=col("beta1"),
                                         op0=ALU.mult, op1=ALU.subtract).then_inc(sem.p_dve, 1)
                dve.wait_ge(sem.p_dve, b.at(PER.p_dve, 6))
                dve.tensor_scalar(h1[:, :], x1[:, :], p_ac[:, 0:1], p_ac[:, 1:2], ALU.mult,
                                  ALU.subtract).then_inc(sem.p_h, 1)

            def p_qk(b, u):
                dst, bias = (cq, "bq1") if u < 2 else (ck, "bk1")
                dve.wait_ge(sem.p_hi, b.at(PER.p_hi, u + 1))
                h = half(u % 2)
                dve.scalar_tensor_tensor(out=dst[1][:, h], in0=P_ODD[:, h], scalar=col(bias),
                                         in1=f32(dst[0][:, h]), op0=ALU.add, op1=ALU.subtract)\
                   .then_inc(sem.p_lo, 1)

            def m_max(b, u):
                dve.wait_ge(sem.m_s, b.at(PER.m_s, u + 1))
                dve.reduce_max(mx1[:, u // (G1 * T), u % (G1 * T):u % (G1 * T) + 1],
                               (P_EVEN, P_ODD)[u % 2][:, :], AX.X).then_inc(sem.m_max, 1)

            def m_half(b, v):
                u = M_FULL - G1 * T + v // 2
                dve.wait_ge(sem.m_s, b.at(PER.m_s, M_FULL + v + 1))
                dve.reduce_max(mx_half[:, u, v % 2:v % 2 + 1], P_F[:, half(v % 2)], AX.X)\
                   .then_inc(sem.m_max, 1)
                if v == 2 * (HEADS * T - M_FULL) - 1:
                    q = slice(M_FULL - G1 * T, G1 * T)
                    dve.wait_ge(sem.m_max, b.at(PER.m_max, PER.m_max))
                    dve.tensor_tensor(mx1[:, 1, q], mx_half[:, q, 0], mx_half[:, q, 1], ALU.max)\
                       .then_inc(sem.m_both, 1)

            def m_rows(b, g):
                dve.wait_ge(sem.m_t, b.at(PER.m_t, g + 1))
                if b.has_prev:
                    dve.wait_ge(sem.m_row, b.at(PER.m_row, 0))
                dve.tensor_copy(neg[:, g, :], (P_EVEN, P_F)[g][0:G1 * T, 0:C]).then_inc(sem.m_neg, 1)

            def o_sums(b, g):
                dve.wait_ge(sem.o_z, b.at(PER.o_z, g + 1))
                dve.reciprocal(rz[g][:, :, :].rearrange("p t j -> p (t j)"),
                               (P_EVEN, P_ODD)[g][:, 0:T * G1]).then_inc(sem.o_dve, 1)
                dve.wait_ge(sem.o_dve, b.at(PER.o_dve, g + 1))
                dve.tensor_copy(rx[g], rz[g][:, :, :].rearrange(
                    "p t (j a) -> p t j a", a=1).broadcast_to([C, T, G1, 32])).then_inc(sem.o_r, 1)

            def o_divide(b, g):
                dve.wait_ge(sem.o_rb, b.at(PER.o_rb, g + 1))
                dve.tensor_tensor(o1[g][:, :], o1[g][:, :], (P_ACC, P_EVEN)[g][:, :], ALU.mult)\
                   .then_inc(sem.o_n, 1)

            def o_residual(b):
                dve.wait_ge(sem.o_pj, b.at(PER.o_pj, 1))
                dve.wait_ge(sem.p_res, b.at(PER.p_res, 1))
                dve.tensor_tensor(x2[:, :], P_ACC[:, :], x1_res[:, :], ALU.add)\
                   .then_inc(sem.o_x2, 1)

            def t_norms(b):
                dve.wait_ge(sem.t_tm, b.at(PER.t_tm, 3))
                qk = tm[:, :, 0:2 * D3].rearrange("p t (a d) -> p t a d", a=2)
                dve.tensor_tensor(t_sq[:, :, :, :], qk, qk, ALU.mult)\
                   .then_inc(sem.t_dve, 1)
                dve.wait_ge(sem.t_dve, b.at(PER.t_dve, 1))
                dve.reduce_sum(t_ns[:, :], t_sq[:, :, :, :].rearrange("p t a d -> p (t a) d"), AX.X)\
                   .then_inc(sem.t_ns, 1)

            def t_keys(b):
                dve.wait_ge(sem.t_rn, b.at(PER.t_rn, 1))
                rn = t_rn[:, :].rearrange("p (t a) -> p t a", a=2)
                dve.tensor_tensor(ka[:, :, 0:D3], tm[:, :, D3:2 * D3],
                                  rn[:, :, 1:2].broadcast_to([C, T, D3]), ALU.mult)\
                   .then_inc(sem.t_k, 1)
                dve.tensor_tensor(qa[:, :, 0:D3], tm[:, :, 0:D3],
                                  rn[:, :, 0:1].broadcast_to([C, T, D3]), ALU.mult)\
                   .then_inc(sem.t_dve, 1)
                dve.wait_ge(sem.t_dve, b.at(PER.t_dve, 2))

            def t_scale(b):
                dve.wait_ge(sem.t_m, b.at(PER.t_m, 1))
                dve.tensor_scalar(wb[:, 0:D3], P_F[:, HALF:HALF + D3], EPS3, None, ALU.add)
                dve.tensor_copy(wb[:, D3:D3 + 1], P_F[:, HALF + D3:HALF + D3 + 1])\
                   .then_inc(sem.t_dve, 1)
                dve.wait_ge(sem.t_dve, b.at(PER.t_dve, 3))
                dve.tensor_tensor(t_dn[:, :, :], qa[:, :, :],
                                  wb[:, :].rearrange("p (a d) -> p a d", a=1).broadcast_to([C, T, D3 + 1]),
                                  ALU.mult)\
                   .then_inc(sem.t_dve, 1)
                dve.wait_ge(sem.t_dve, b.at(PER.t_dve, 4))
                dve.reduce_sum(t_ds[:, 0, :], t_dn[:, :, :], AX.X)\
                   .then_inc(sem.t_dve, 1)
                dve.wait_ge(sem.t_dve, b.at(PER.t_dve, 5))
                dve.reciprocal(t_ds[:, 1, :], t_ds[:, 0, :])\
                   .then_inc(sem.t_dve, 1)
                dve.wait_ge(sem.t_dve, b.at(PER.t_dve, 6))
                dve.tensor_scalar(t_ds[:, 2, :], t_ds[:, 1, :], col("gamma3"), None, ALU.mult)\
                   .then_inc(sem.t_dve, 1)
                dve.wait_ge(sem.t_dve, b.at(PER.t_dve, 7))
                dve.tensor_tensor(t_dn[:, :, :], qa[:, :, :],
                                  t_ds[:, 2, :].rearrange("p (t a) -> p t a", a=1).broadcast_to([C, T, D3 + 1]),
                                  ALU.mult).then_inc(sem.t_qs, 1)

            dve.wait_ge(s_const, 32)
            dve.wait_ge(s_ones, 8)
            dve.wait_ge(s_folded, 3)
            play(dve, dict(g_stat=g_stat, g_var=g_var, g_apply=g_apply, i_stat=i_stat, i_apply=i_apply, f_qk=f_qk, f_max=f_max,
                           f_shift=f_shift, f_sums=f_sums, f_out=f_out, p_stat=p_stat, p_var=p_var,
                           p_apply=p_apply, p_qk=p_qk, m_max=m_max, m_half=m_half, m_rows=m_rows, o_sums=o_sums,
                           o_divide=o_divide, o_residual=o_residual, t_norms=t_norms,
                           t_keys=t_keys, t_scale=t_scale))

        @block.tensor
        def _(pe):
            def mm(dst, lhsT, rhs, start=True, stop=True):
                return pe.matmul(dst, lhsT, rhs, start=start, stop=stop)

            def g_stat(b):
                pe.wait_ge(sem.g_stat, b.at(PER.g_stat, 1))
                if b.has_prev:
                    before = b.previous()
                    if before.has_prev:
                        pe.wait_ge(sem.t_ev, before.at(PER.t_ev, 0))
                    pe.wait_ge(sem.m_neg, before.at(PER.m_neg, 2))
                mm(P_F[:, 0:2], mat("group0"), g_mv[:, :]).then_inc(sem.g_gstat, 1)

            def f_qk(n, b, u, layer):
                src = xn if layer == 0 else xn2
                if u == 0 and layer == 0:
                    pe.wait_ge(sem.g_xn, b.at(PER.g_xn, 1))
                elif u == 0:
                    pe.wait_ge(sem.i_xn, b.at(PER.i_xn, 1))
                if u >= 2:
                    pe.wait_ge(sem.f_lo, n.at(PER.f_lo, u - 1))
                mm(full_pair(layer)[:, half(u % 2)], mat(f"wq{layer}" if u < 2 else f"wk{layer}"),
                   src[:, half(u % 2)]).then_inc(sem.f_qk, 1)

            def f_value(n, h, layer):
                pe.wait_ge(sem.f_max, n.at(PER.f_max, 2 * T - 1 + h))
                src = xn if layer == 0 else xn2
                for t in range(4 * h, 4 * h + 4):
                    last = mm(full_pair(layer)[:, tile(t)], src[:, tile(t)], wvp0[:, :] if layer == 0 else mat("wv2"))
                last.then_inc(sem.f_v, 1)

            def f_max(n, u, layer):
                if u < 2:
                    pe.wait_ge(sem.f_lo, n.at(PER.f_lo, 3 + u))
                else:
                    pe.wait_ge(sem.f_max, n.at(PER.f_max, u - 1))
                mm(full_pair(layer)[:, half(u % 2)], queries(layer)[0][:, tile(u // 2)], keys(layer)[0][:, half(u % 2)])\
                    .then_inc(sem.f_max_s, 1)

            def f_scores(n, u, layer):
                h, kt = u // T, u % T
                if u == 0:
                    pe.wait_ge(sem.f_vout, n.at(PER.f_vout, 1))
                else:
                    pe.wait_ge(sem.f_p, n.at(PER.f_p, u))
                dst = full_pair(layer)[:, half(0)]
                mm(dst, keys(layer)[0][:, tile(kt)], queries(layer)[0][:, half(h)], stop=False)
                mm(dst, keys(layer)[0][:, tile(kt)], queries(layer)[1][:, half(h)], start=False, stop=False)
                mm(dst, keys(layer)[1][:, tile(kt)], queries(layer)[0][:, half(h)], start=False, stop=False)
                if u % T == 0:
                    pe.wait_ge(sem.f_shift, n.at(PER.f_shift, h + 1))
                mm(dst, ones_r[:, :], f_diag[:, 4 * h:4 * h + 4, :].rearrange("p t c -> p (t c)"),
                   start=False).then_inc(sem.f_sc, 1)

            def f_pv(n, u, layer):
                h, kt = u // T, u % T
                pe.wait_ge(sem.f_p, n.at(PER.f_p, u + 1))
                if u == 0:
                    pe.wait_ge(sem.f_vout, n.at(PER.f_vout, 2))
                if u == T:
                    pe.wait_ge(sem.f_t, n.at(PER.f_t, 1))
                mm(full_pair(layer)[:, half(1)], fv[:, kt, :], fp[u % 3][:, :], start=kt == 0, stop=kt == T - 1)\
                    .then_inc(sem.f_pv, 1)

            def f_sums(n, layer):
                pe.wait_ge(sem.f_sum, n.at(PER.f_sum, PER.f_sum))
                for t in range(T):
                    last = mm(full_pair(layer)[:, t:t + 1], fsum[:, tile(t)], ones[:, 0:1])
                last.then_inc(sem.f_z, 1)

            def f_spread(n, layer):
                pe.wait_ge(sem.f_r, n.at(PER.f_r, 1))
                pe.wait_ge(sem.f_t, n.at(PER.f_t, 2))
                for t in range(T):
                    last = mm(full_pair(layer)[:, tile(t)], f_recip[:, t:t + 1].broadcast_to([C, C]), mat("ident"))
                last.then_inc(sem.f_rb, 1)

            def p_average(b):
                pe.wait_ge(sem.p_stat, b.at(PER.p_stat, 1))
                mm(P_ODD[:, 0:2], mat("group1"), p_mv[:, :]).then_inc(sem.p_gstat, 1)

            def p_qk(b, u):
                if u == 0:
                    pe.wait_ge(sem.p_h, b.at(PER.p_h, 1))
                if u >= 2:
                    pe.wait_ge(sem.p_lo, b.at(PER.p_lo, u - 1))
                mm(P_ODD[:, half(u % 2)], mat("wq1" if u < 2 else "wk1"),
                   h1[:, half(u % 2)]).then_inc(sem.p_qk, 1)

            def p_value(b, h):
                pe.wait_ge(sem.p_lo, b.at(PER.p_lo, 3 + h))
                for t in range(4 * h, 4 * h + 4):
                    last = mm(P_ODD[:, tile(t)], h1[:, tile(t)], mat("wv1"))
                last.then_inc(sem.p_v, 1)

            def m_max(b, u):
                h, t = u // T, u % T
                if u == 0:
                    pe.wait_ge(sem.stacked_first, b.at(PER.stacked_first, PER.stacked_first))
                    if b.has_prev:
                        pe.wait_ge(sem.o_n, b.at(PER.o_n, 0))
                elif u == 1:
                    pe.wait_ge(sem.p_vout, b.at(PER.p_vout, 2))
                else:
                    pe.wait_ge(sem.m_max, b.at(PER.m_max, u - 1))
                if u == 2 * T:
                    pe.wait_ge(sem.stacked_rest, b.at(PER.stacked_rest, PER.stacked_rest))
                if u == G1 * T:
                    pe.wait_ge(sem.m_neg, b.at(PER.m_neg, 1))
                for k in range(2):
                    last = mm((P_EVEN, P_ODD)[u % 2][:, half(k)], qs[0:SHIFT_ROW, h, tile(t)],
                              ks[0:SHIFT_ROW, h // 2, half(k)])
                last.then_inc(sem.m_s, 1)

            def m_half(b, v):
                u, k = M_FULL + v // 2, v % 2
                h, t = u // T, u % T
                if v < 2:
                    pe.wait_ge(sem.f_out, run0(b).at(PER.f_out, 1))
                else:
                    pe.wait_ge(sem.m_max, b.at(PER.m_max, M_FULL + v - 1))
                mm(P_F[:, half(k)], qs[0:SHIFT_ROW, h, tile(t)], ks[0:SHIFT_ROW, h // 2, half(k)])\
                    .then_inc(sem.m_s, 1)

            def m_rows(b, g):
                if g == 0:
                    pe.wait_ge(sem.m_max, b.at(PER.m_max, G1 * T))
                else:
                    pe.wait_ge(sem.m_both, b.at(PER.m_both, 1))
                mm((P_EVEN, P_F)[g][0:G1 * T, 0:C], mx1[:, g, :], mat("neg_ident")).then_inc(sem.m_t, 1)

            def s_scores(b, g, u):
                kt, h = u // G1, G1 * g + u % G1
                if u == 0:
                    pe.wait_ge(sem.m_row, b.at(PER.m_row, 64 * (g + 1)))
                    if g == 0:
                        pe.wait_ge(sem.p_vout, b.at(PER.p_vout, 2))
                if g == 0 and u < 2:
                    pe.wait_ge(sem.m_max, b.at(PER.m_max, M_FULL - 1 + u))
                if 32 * g + u >= 2:
                    pe.wait_ge(sem.s_p, b.at(PER.s_p, 32 * g + u - 1))
                for k in range(2):
                    last = mm((P_EVEN, P_ODD)[u % 2][:, half(k)], ks[:, h // 2, tile(kt)],
                              qs[:, h, half(k)])
                last.then_inc(sem.s_sc, 1)

            def s_pv(b, g, kt, k):
                pe.wait_ge(sem.s_p, b.at(PER.s_p, 32 * g + G1 * (kt + 1)))
                if kt == 0 and k == 0 and g == 0 and b.has_prev:
                    pe.wait_ge(sem.f_out, run2(b.previous(), False).at(PER.f_out, 1))
                if kt == 0 and k == 0 and g == 1:
                    pe.wait_ge(sem.o_ev, b.at(PER.o_ev, 1))
                for j in range(G1):
                    last = mm(P_ACC[32 * j:32 * j + 32, half(k)], v1[:, kt, G1 * g + j, :],
                              p1[kt % 2][:, j, half(k)], start=kt == 0, stop=kt == T - 1)
                if k == 1:
                    last.then_inc(sem.s_pv, 1)

            def o_sums(b, g):
                pe.wait_ge(sem.o_ev, b.at(PER.o_ev, g + 1))
                pe.wait_ge(sem.s_p, b.at(PER.s_p, PER.s_p - 1 + g))
                for t in range(T):
                    last = mm((P_EVEN, P_ODD)[g][:, t * G1:(t + 1) * G1], o1[g][:, tile(t)],
                              col("zsel", G1))
                last.then_inc(sem.o_z, 1)

            def o_spread(b, g):
                pe.wait_ge(sem.o_r, b.at(PER.o_r, g + 1))
                if g == 0:
                    pe.wait_ge(sem.o_ev, b.at(PER.o_ev, 2))
                for t in range(T):
                    last = mm((P_ACC, P_EVEN)[g][:, tile(t)],
                              rx[g][:, t, :, :].rearrange("p j a -> p (j a)"), mat("ident"))
                last.then_inc(sem.o_rb, 1)

            def o_project(b):
                pe.wait_ge(sem.o_n, b.at(PER.o_n, 2))
                for k in range(2):
                    for g in range(2):
                        last = mm(P_ACC[:, half(k)], mat(("wp1a", "wp1b")[g]), o1[g][:, half(k)],
                                  start=g == 0, stop=g == 1)
                last.then_inc(sem.o_pj, 1)

            def t_project(b, n, k, beside):
                if k == 0:
                    pe.wait_ge(sem.f_out, n.at(PER.f_out, 1))
                    pe.wait_ge(sem.m_neg, beside.at(PER.m_neg, 2))
                if k == 2:
                    pe.wait_ge(sem.t_tm, b.at(PER.t_tm, 1))
                for t in range(3 * k, min(3 * k + 3, T)):
                    dst = t_bank(k)[:, (t - 3 * k) * W3:(t - 3 * k + 1) * W3]
                    mm(dst, x3[:, tile(t)], col("w3", W3), stop=False)
                    last = mm(dst, ones[0:1, :], b3row[:, :], start=False)
                last.then_inc(sem.t_q, 1)

            def t_matrix(b):
                pe.wait_ge(sem.t_k, b.at(PER.t_k, 1))
                pe.wait_ge(sem.t_tm, b.at(PER.t_tm, 3))
                for t in range(T):
                    mm(P_F[0:D3 + 1, 0:C + 1], ka[:, t, :], tm[:, t, 2 * D3:W3 + 1],
                       start=t == 0, stop=t == T - 1)
                for t in range(T):
                    last = mm(P_F[:, HALF:HALF + D3 + 1], ones[:, :], ka[:, t, :],
                              start=t == 0, stop=t == T - 1)
                last.then_inc(sem.t_m, 1)

            def t_turn(b):
                pe.wait_ge(sem.t_qs, b.at(PER.t_qs, 1))
                pe.wait_ge(sem.t_ma, b.at(PER.t_ma, 1))
                for t in range(T):
                    last = mm(P_F[0:D3 + 1, tile(t)], t_dn[:, t, :], mat("ident"))
                last.then_inc(sem.t_tr, 1)

            def t_out(b):
                pe.wait_ge(sem.t_qt, b.at(PER.t_qt, 1))
                for k in range(2):
                    mm(P_F[:, half(k)], ma[:, :], qt3[:, half(k)]).then_inc(sem.t_o, 1)

            pe.wait_ge(s_const, 32)
            pe.wait_ge(s_ones, 8)
            mm(P_EVEN[:, 0:C], mat("wv0"), mat("wp0")).then_inc(s_fold, 1)
            mm(P_EVEN[:, C:C + 1], mat("wp0"), col("bv0")).then_inc(s_fold, 1)
            mm(P_EVEN[:, C + 1:C + 2], mat("wp1"), col("bv1")).then_inc(s_fold, 1)
            pe.wait_ge(s_folded, 3)
            play(pe, dict(g_stat=g_stat, f_qk=f_qk, f_value=f_value, f_max=f_max, f_scores=f_scores,
                          f_pv=f_pv, f_sums=f_sums, f_spread=f_spread, p_average=p_average, p_qk=p_qk,
                          p_value=p_value, m_max=m_max, m_half=m_half, m_rows=m_rows, s_scores=s_scores, s_pv=s_pv,
                          o_sums=o_sums, o_spread=o_spread, o_project=o_project,
                          t_project=t_project, t_matrix=t_matrix, t_turn=t_turn, t_out=t_out))


def kernel(x, **w):
    import numpy as np
    import concourse.bacc as bacc
    from concourse.bass_utils import run_bass_kernel_spmd as run

    a = {k: np.asarray(v) for k, v in w.items()}
    images = x.shape[0]

    packed = np.zeros((C, PACKED), np.float32)

    def put(name, value):
        packed[:, COL[name]:COL[name] + value.shape[1]] = value

    put("wq0", a["L0_conv_Wq"].T)
    put("wk0", a["L0_conv_Wk"].T)
    put("wv0", a["L0_conv_Wv"])
    put("wp0", a["L0_conv_Wp"].T)
    put("wq1", a["L1_conv_wq"].T)
    put("wk1", a["L1_conv_wk"].T)
    put("wv1", a["L1_conv_wv"].T)
    put("wp1", a["L1_conv_wp"].T)
    for g, name in enumerate(("wp1a", "wp1b")):
        for j in range(G1):
            h = G1 * g + j
            packed[32 * j:32 * j + DH, COL[name]:COL[name] + C] = a["L1_conv_wp"].T[h * DH:(h + 1) * DH]
    put("wq2", a["L2_conv_wq"].T)
    put("wk2", a["L2_conv_wk"].T)
    put("wv2", a["L2_conv_wv"].T)
    put("ident", np.eye(C, dtype=np.float32))
    put("neg_ident", -np.eye(C, dtype=np.float32))
    for name, group in (("group0", C // 8), ("group1", C // 32)):
        put(name, np.kron(np.eye(C // group), np.full((group, group), 1.0 / group)).astype(np.float32))
    put("w3", np.concatenate([a["L3_conv_Wq"].T, a["L3_conv_Wk"].T, a["L3_conv_Wv"].T], axis=1))
    for j in range(G1):
        packed[32 * j + DH, COL["zsel"] + j] = 1.0
    for name, key in dict(bq0="L0_conv_bq", bk0="L0_conv_bk", bv0="L0_conv_bv", bp0="L0_conv_bp",
                          gamma0="L0_conv_gamma", beta0="L0_conv_beta", bq1="L1_conv_bq",
                          bk1="L1_conv_bk", bv1="L1_conv_bv", bp1="L1_conv_bp",
                          gamma1="L1_conv_gn_w", beta1="L1_conv_gn_b", bq2="L2_conv_bq",
                          bk2="L2_conv_bk", bv2="L2_conv_bv").items():
        put(name, a[key].reshape(C, 1))
    put("gamma3", np.broadcast_to(a["L3_conv_gamma"].reshape(1, 1), (C, 1)))
    put("one", np.ones((C, 1), np.float32))
    bias3 = np.concatenate([a["L3_conv_bq"], a["L3_conv_bk"], a["L3_conv_bv"]]).reshape(1, W3)

    nc = bacc.Bacc("TRN2", target_bir_lowering=False, num_devices=1)
    arrays = {"x_dram": np.ascontiguousarray(x).reshape(images, C, N), "packed_dram": packed,
              "bias3_dram": np.ascontiguousarray(bias3)}
    args = [nc.dram_tensor(k, v.shape, F32, kind="ExternalInput").ap() for k, v in arrays.items()]
    args.append(nc.dram_tensor("out_dram", (images, C, N), F32, kind="ExternalOutput").ap())
    heads_kernel(nc, images, *args)
    r = run(nc, [arrays], core_ids=[0])
    return r.results[0]["out_dram"].reshape(x.shape)
```

```python
import concourse.bass as bass
from concourse import mybir
from contextlib import ExitStack

F32 = mybir.dt.float32
F32R = mybir.dt.float32r
ALU = mybir.AluOpType
ACT = mybir.ActivationFunctionType
AX = mybir.AxisListType

C = 128
N = 1024
HALF = N // 2
T = N // C
HEADS, DH = 8, 16
FULL_TILES = 36
EARLY_PRODUCTS = 16
G1 = 4
EPS = 1e-5
EPS3 = 1e-6
PAIR = 2 * DH
SHIFT_ROW = 3 * PAIR
D3 = 16
W3 = 2 * D3 + C

MATRICES = ["wq0", "wk0", "wv0", "wp0", "wq1", "wk1", "wv1", "wp1", "wp1a", "wp1b",
            "wq2", "wk2", "wv2", "ident", "neg_ident", "group0", "group1"]
VECTORS = ["bq0", "bk0", "bv0", "bp0", "gamma0", "beta0", "bq1", "bk1", "bv1", "bp1",
           "gamma1", "beta1", "bq2", "bk2", "bv2", "gamma3"]
COL = {name: C * i for i, name in enumerate(MATRICES)}
COL["w3"] = C * len(MATRICES)
COL["zsel"] = COL["w3"] + W3
COL.update({name: COL["zsel"] + G1 + i for i, name in enumerate(VECTORS)})
PACKED = COL["zsel"] + G1 + len(VECTORS)


class Batch:

    def __init__(self, index, plus=0, times=1):
        self.index, self.plus, self.times = index, plus, times

    @property
    def has_prev(self):
        return not isinstance(self.index, int) or self.times * self.index + self.plus > 0

    def at(self, per_batch, count):
        return self.index * (self.times * per_batch) + (self.plus * per_batch + count)

    def previous(self):
        return Batch(self.index, self.plus - 1, self.times)

    def next(self):
        return Batch(self.index, self.plus + 1, self.times)


class PER:
    x_loaded = 16
    g_stat = 1
    g_gstat = 1
    g_veps = 1
    g_rstd = 1
    g_xn = 1
    g_dve = 6
    i_veps = 1
    i_rstd = 1
    i_xn = 1
    i_dve = 3
    i_res = 1
    i_exact = 4
    f_qk = 4
    f_hi = 4
    f_lo = 4
    f_v = 2
    f_vout = 2
    f_max_s = 16
    f_max = 16
    f_shift = 2
    f_sc = 16
    f_p = 16
    f_pv = 16
    f_sum = 14
    f_t = 2
    f_z = 1
    f_r = 1
    f_rb = 1
    f_out = 1
    f_div = 1
    f_dve = 2
    p_stat = 1
    p_gstat = 1
    p_veps = 1
    p_rstd = 1
    p_h = 1
    p_qk = 4
    p_hi = 4
    p_lo = 4
    p_v = 2
    p_vout = 2
    p_res = 1
    p_dve = 6
    stacked_first = 9 * 16
    stacked_rest = 27 * 16
    m_s = FULL_TILES + 2 * (HEADS * T - FULL_TILES)
    m_max = FULL_TILES + 2 * (HEADS * T - FULL_TILES)
    m_both = 1
    m_t = 2
    m_neg = 2
    m_row = 2 * 4 * 16
    s_sc = 64
    s_p = 64
    s_pv = 16
    o_ev = 2
    o_z = 2
    o_r = 2
    o_rb = 2
    o_n = 2
    o_pj = 1
    o_x2 = 1
    o_dve = 2
    t_q = 3
    t_tm = 3
    t_ns = 1
    t_rn = 1
    t_k = 1
    t_m = 1
    t_ma = 1
    t_qs = 1
    t_tr = 1
    t_qt = 1
    t_o = 2
    t_ev = 2
    t_dve = 7
    stored = 16


class Semaphores:
    def __init__(self, new):
        self.x_loaded = new("x_loaded")
        self.g_stat = new("g_stat")
        self.g_gstat = new("g_gstat")
        self.g_veps = new("g_veps")
        self.g_rstd = new("g_rstd")
        self.g_xn = new("g_xn")
        self.g_dve = new("g_dve")
        self.i_veps = new("i_veps")
        self.i_rstd = new("i_rstd")
        self.i_xn = new("i_xn")
        self.i_dve = new("i_dve")
        self.i_res = new("i_res")
        self.i_exact = new("i_exact")
        self.f_qk = new("f_qk")
        self.f_hi = new("f_hi")
        self.f_lo = new("f_lo")
        self.f_v = new("f_v")
        self.f_vout = new("f_vout")
        self.f_max_s = new("f_max_s")
        self.f_max = new("f_max")
        self.f_shift = new("f_shift")
        self.f_sc = new("f_sc")
        self.f_p = new("f_p")
        self.f_pv = new("f_pv")
        self.f_sum = new("f_sum")
        self.f_t = new("f_t")
        self.f_z = new("f_z")
        self.f_r = new("f_r")
        self.f_rb = new("f_rb")
        self.f_out = new("f_out")
        self.f_div = new("f_div")
        self.f_dve = new("f_dve")
        self.p_stat = new("p_stat")
        self.p_gstat = new("p_gstat")
        self.p_veps = new("p_veps")
        self.p_rstd = new("p_rstd")
        self.p_h = new("p_h")
        self.p_qk = new("p_qk")
        self.p_hi = new("p_hi")
        self.p_lo = new("p_lo")
        self.p_v = new("p_v")
        self.p_vout = new("p_vout")
        self.p_res = new("p_res")
        self.p_dve = new("p_dve")
        self.stacked_first = new("stacked_first")
        self.stacked_rest = new("stacked_rest")
        self.m_s = new("m_s")
        self.m_max = new("m_max")
        self.m_both = new("m_both")
        self.m_t = new("m_t")
        self.m_neg = new("m_neg")
        self.m_row = new("m_row")
        self.s_sc = new("s_sc")
        self.s_p = new("s_p")
        self.s_pv = new("s_pv")
        self.o_ev = new("o_ev")
        self.o_z = new("o_z")
        self.o_r = new("o_r")
        self.o_rb = new("o_rb")
        self.o_n = new("o_n")
        self.o_pj = new("o_pj")
        self.o_x2 = new("o_x2")
        self.o_dve = new("o_dve")
        self.t_q = new("t_q")
        self.t_tm = new("t_tm")
        self.t_ns = new("t_ns")
        self.t_rn = new("t_rn")
        self.t_k = new("t_k")
        self.t_m = new("t_m")
        self.t_ma = new("t_ma")
        self.t_qs = new("t_qs")
        self.t_tr = new("t_tr")
        self.t_qt = new("t_qt")
        self.t_o = new("t_o")
        self.t_ev = new("t_ev")
        self.t_dve = new("t_dve")
        self.stored = new("stored")


def heads_kernel(nc, images, x, packed, bias3, out):
    ctx = ExitStack()
    with ctx:
        def sb(name, shape, dtype=F32):
            return ctx.enter_context(nc.sbuf_tensor(name, shape, dtype))

        cw = sb("cw", [C, PACKED])
        b3row = sb("b3row", [1, W3])
        ones = sb("ones", [C, C])
        ones_r = sb("ones_r", [C, C], F32R)
        minus_half = sb("minus_half", [C, 16])
        wvp0 = sb("wvp0", [C, C])
        const_bias = sb("const_bias", [C, 2])

        x_in = sb("x_in", [C, N])
        g_bn = sb("g_bn", [C, 2, 6])
        g_mv = sb("g_mv", [C, 2])
        g_gs = sb("g_gs", [C, 2])
        g_ve = sb("g_ve", [C, 2])
        g_rs = sb("g_rs", [C, 1])
        g_ac = sb("g_ac", [C, 2])
        i_bn = sb("i_bn", [C, 2, 6])
        i_mv = sb("i_mv", [C, 2])
        i_ve = sb("i_ve", [C, 1])
        i_rs = sb("i_rs", [C, 1])
        i_ac = sb("i_ac", [C, 1])
        xn = sb("xn", [C, N])

        fq2 = [sb("fq2_hi", [C, N], F32R), sb("fq2_lo", [C, N], F32R)]
        f_exact = sb("f_exact", [C, 2, HALF])
        fk2 = [sb("fk2_hi", [C, N], F32R), sb("fk2_lo", [C, N], F32R)]
        fv = sb("fv", [C, T, C])
        f_mx2 = sb("f_mx2", [C, T, 2])
        f_mx = sb("f_mx", [C, T])
        f_diag = sb("f_diag", [C, T, C], F32R)
        fp = [sb(f"fp{i}", [C, HALF]) for i in range(3)]
        fsum = sb("fsum", [C, N])
        f_recip = sb("f_recip", [C, T])
        f_num = sb("f_num", [C, N])
        x1 = sb("x1", [C, N])
        x2 = sb("x2", [C, N])
        x3 = sb("x3", [C, N])

        x1_res = sb("x1_res", [C, N])
        p_bn = sb("p_bn", [C, 2, 6])
        p_mv = sb("p_mv", [C, 2])
        p_gs = sb("p_gs", [C, 2])
        p_ve = sb("p_ve", [C, 2])
        p_rs = sb("p_rs", [C, 1])
        p_ac = sb("p_ac", [C, 2])
        h1 = sb("h1", [C, N])
        cq = fq0 = [sb("cq_hi", [C, N], F32R), sb("cq_lo", [C, N], F32R)]
        ck = fk0 = [sb("ck_hi", [C, N], F32R), sb("ck_lo", [C, N], F32R)]
        qs = sb("qs", [C, HEADS, N], F32R)
        ks = sb("ks", [C, HEADS // 2, N], F32R)
        v1 = sb("v1", [C, T, HEADS, 32])
        mx_half = sb("mx_half", [C, G1 * T, 2])
        mx1 = sb("mx1", [C, 2, G1 * T])
        neg = sb("neg", [G1 * T, 2, C], F32R)
        p1 = [sb(f"p1_{i}", [C, G1, N]) for i in range(2)]
        o1 = [sb(f"o1_{g}", [C, N]) for g in range(2)]
        rz = [sb(f"rz{g}", [C, T, G1]) for g in range(2)]
        xn2 = p1[0][:, 2, :]
        x2_bias = p1[0][:, 3, :]
        rx = [p1[0][:, g, :].rearrange("p (t j r) -> p t j r", t=T, j=G1) for g in range(2)]

        tm = sb("tm", [C, T, W3 + 1])
        t_sq = sb("t_sq", [C, T, 2, D3])
        t_ns = sb("t_ns", [C, T * 2])
        t_rn = sb("t_rn", [C, T * 2])
        qa = sb("qa", [C, T, D3 + 1])
        ka = sb("ka", [C, T, D3 + 1])
        ma = sb("ma", [D3 + 1, C])
        wb = sb("wb", [C, D3 + 1])
        t_dn = sb("t_dn", [C, T, D3 + 1])
        t_ds = sb("t_ds", [C, 3, T])
        qt3 = tm[0:D3 + 1, :, 0:C]

        pairs = [ctx.enter_context(nc.psum_tensor(f"pair{i}", [C, N], F32)) for i in range(4)]
        P_EVEN, P_ODD, P_ACC, P_F = pairs

        def full_pair(layer):
            return P_F if layer == 0 else P_ACC

        def queries(layer):
            return fq0 if layer == 0 else fq2

        def keys(layer):
            return fk0 if layer == 0 else fk2

        def t_bank(k):
            return P_F[:, half(k % 2)]

        sem = Semaphores(lambda name: ctx.enter_context(nc.semaphore(name)))
        s_const = ctx.enter_context(nc.semaphore("s_const"))
        s_ones = ctx.enter_context(nc.semaphore("s_ones"))
        s_fill = ctx.enter_context(nc.semaphore("s_fill"))
        s_fold = ctx.enter_context(nc.semaphore("s_fold"))
        s_folded = ctx.enter_context(nc.semaphore("s_folded"))

        def col(name, width=1):
            return cw[:, COL[name]:COL[name] + width]

        def mat(name):
            return col(name, C)

        def f32(ap):
            return ap.bitcast(F32)

        def tile(t):
            return slice(t * C, (t + 1) * C)

        def half(h):
            return slice(h * HALF, (h + 1) * HALF)

        def sums_through(u):
            return (T - 1) * (u // T) + max(u % T, 1)


        def group_norm(b):
            yield ("g_stat", 4, b)
            yield ("g_var", 4, b)
            yield ("g_apply", 4, b)

        def full_project(n, b, layer):
            for u in range(4):
                yield ("f_qk", 4, n, b, u, layer)

        def full_maxima(n, b, layer):
            for u in range(2 * T):
                yield ("f_max", 2 if layer else 3, n, b, u, layer)

        def full_values(n, layer):
            for h in range(2):
                yield ("f_value", 4, n, h, layer)
                yield ("f_shift", 0, n, h)

        def full_products(n, layer):
            for u in range(2 * T):
                yield ("f_scores", 4, n, u, layer)
                if u:
                    yield ("f_pv", 4, n, u - 1, layer)
            yield ("f_pv", 4, n, 2 * T - 1, layer)

        def full_finish(n, b, layer):
            yield ("f_sums", 8, n, layer)
            yield ("f_spread", 10, n, layer)
            yield ("f_out", 6, n, b, layer)

        def full_attention(n, b, layer):
            yield from full_project(n, b, layer)
            yield from full_maxima(n, b, layer)
            yield from full_values(n, layer)
            yield from full_products(n, layer)
            yield from full_finish(n, b, layer)

        def heads(b, g):
            for u in range(G1 * T):
                kt, j = u // G1, u % G1
                yield ("s_scores", 2, b, g, u)
                if kt and j % 2:
                    yield ("s_pv", 4, b, g, kt - 1, j // 2)
            if g == 1:
                yield ("o_sums", 4, b, 0)
            yield ("s_pv", 4, b, g, T - 1, 0)
            yield ("s_pv", 4, b, g, T - 1, 1)
            yield ("s_out", 0, b, g)

        def maxima(b):
            for u in range(FULL_TILES):
                yield ("m_max", 2, b, u)
                if u == G1 * T - 1:
                    yield ("m_rows", 1, b, 0)

        def rest_of_maxima(b):
            for v in range(2 * (HEADS * T - FULL_TILES)):
                yield ("m_half", 2, b, v)
            yield ("m_rows", 1, b, 1)

        def prepare(b, n):
            yield ("p_stat", 0, b, n)
            yield from pause(6)
            yield ("p_average", 0, b)
            yield ("p_var", 2, b)
            yield ("p_apply", 2, b)
            yield from pause(4)
            for u in range(4):
                yield ("p_qk", 4, b, u)
            yield ("p_stack", 0, b)
            for h in range(2):
                yield ("p_value", 4, b, h)

        def finish_heads(b):
            yield ("o_spread", 5, b, 0)
            yield ("o_sums", 4, b, 1)
            yield ("o_divide", 3, b, 0)
            yield ("o_spread", 5, b, 1)
            yield ("o_divide", 3, b, 1)
            yield ("o_project", 8, b)
            yield ("o_residual", 4, b)
            yield ("i_stat", 6, b)
            yield ("i_apply", 6, b)

        def linear_attention(b, n, beside):
            for k in range(3):
                yield ("t_project", 6, b, n, k, beside)
            yield ("t_norms", 8, b)
            yield ("t_keys", 4, b)
            yield ("t_matrix", 8, b)
            yield ("t_scale", 6, b)
            yield ("t_turn", 4, b)
            yield ("t_out", 8, b)

        def pause(cost):
            yield ("pause", cost)

        def after(name):
            yield ("after", 0, name)

        def merged(main, side, end=1.0):
            main, side = list(main), list(side)
            pace = (sum(s[1] for s in side) or 1) / (end * sum(s[1] for s in main) or 1)
            done = at = spent = 0
            for step in main:
                if step[0] == "after":
                    needed = max(i + 1 for i, s in enumerate(side) if s[0] == step[2])
                else:
                    needed = 0
                while at < len(side) and (spent < done * pace or at < needed):
                    yield side[at]
                    spent += side[at][1]
                    at += 1
                yield step
                done += step[1]
            yield from side[at:]

        def run0(b):
            return Batch(0) if isinstance(b.index, int) and b.index + b.plus == 0 else \
                Batch(b.index, 2 * b.plus - 1, 2)

        def run2(b, last):
            return Batch(b.index, 2 * b.plus + (1 if last else 2), 2)

        def first():
            b = Batch(0)
            yield ("load", 0, b)
            yield from group_norm(b)
            yield from full_attention(run0(b), b, 0)
            yield from prepare(b, run0(b))
            yield ("p_residual", 0, b, run0(b))
            yield from maxima(b)

        def image(b, last):
            nxt, n2 = b.next(), run2(b, last)
            if not last:
                yield ("load", 0, nxt)
            before = []
            if b.has_prev:
                before = [*linear_attention(b.previous(), run2(b.previous(), False), b)]
            if last:
                yield from merged([*heads(b, 0), *after("m_rows"), *heads(b, 1)],
                                  [*rest_of_maxima(b), *before], 1.0)
                yield from finish_heads(b)
                yield from full_attention(n2, b, 2)
                yield from linear_attention(b, n2, b)
            else:
                n0 = run0(nxt)
                products = [*full_products(n0, 0)]
                first_products, rest_products = products[:EARLY_PRODUCTS], products[EARLY_PRODUCTS:]
                yield from merged([*heads(b, 0), *after("m_rows"), *heads(b, 1)],
                                  [*rest_of_maxima(b), *before, *group_norm(nxt),
                                   *full_project(n0, nxt, 0), *full_maxima(n0, nxt, 0),
                                   *full_values(n0, 0), *first_products], 1.0)
                yield from merged(rest_products, finish_heads(b), 0.8)
                yield from merged([*full_project(n2, b, 2), *full_maxima(n2, b, 2)],
                                  [*full_finish(n0, nxt, 0), *prepare(nxt, n0),
                                   ("p_residual", 0, nxt, n0)], 0.9)
                yield from merged([*full_values(n2, 2), *full_products(n2, 2),
                                   *full_finish(n2, b, 2)],
                                  [*pause(4), *maxima(nxt)], 0.9)

        def play(eng, steps):
            def do(order):
                for name, _, *args in order:
                    if name in steps:
                        steps[name](*args)
            do(first())
            do(image(Batch(0), images == 1))
            if images > 2:
                with eng.Fori(1, images - 1) as i:
                    do(image(Batch(i), False))
            if images > 1:
                do(image(Batch(images - 1), True))

        block = ctx.enter_context(nc.Block())

        @block.sync
        def _(sp):
            sp.dma_start(cw[:, :], packed).then_inc(s_const, 16)
            sp.dma_start(b3row[:, :], bias3).then_inc(s_const, 16)

            def one(images_ap, b):
                i = b.at(1, 0)
                if isinstance(i, int):
                    return images_ap[i, :, :]
                return images_ap[bass.ds(i, 1), :, :].rearrange("a c n -> (a c) n")

            def load(b):
                if b.has_prev:
                    sp.wait_ge(sem.g_xn, b.at(PER.g_xn, 0))
                sp.dma_start(x_in[:, :], one(x, b)).then_inc(sem.x_loaded, 16)

            def p_stack(b):
                def stack_keys(part, t, row, done):
                    sp.dma_start(f32(ks[row:row + PAIR, t, :]),
                                 f32(ck[part][t * PAIR:(t + 1) * PAIR, :])).then_inc(done, 16)

                def stack_queries(part, t, row, done):
                    for e in range(2):
                        h = 2 * t + e
                        sp.dma_start(f32(qs[row + e * DH:row + (e + 1) * DH, h, :]),
                                     f32(cq[part][h * DH:(h + 1) * DH, :])).then_inc(done, 16)

                sp.wait_ge(sem.p_hi, b.at(PER.p_hi, 2))
                stack_queries(0, 0, 0, sem.stacked_first)
                stack_queries(0, 0, 2 * PAIR, sem.stacked_first)
                sp.wait_ge(sem.p_lo, b.at(PER.p_lo, 2))
                stack_queries(1, 0, PAIR, sem.stacked_first)
                sp.wait_ge(sem.p_hi, b.at(PER.p_hi, 4))
                stack_keys(0, 0, 0, sem.stacked_first)
                stack_keys(0, 0, PAIR, sem.stacked_first)
                sp.wait_ge(sem.p_lo, b.at(PER.p_lo, 4))
                stack_keys(1, 0, 2 * PAIR, sem.stacked_first)
                for t in range(1, HEADS // 2):
                    stack_queries(0, t, 0, sem.stacked_rest)
                    stack_queries(0, t, 2 * PAIR, sem.stacked_rest)
                    stack_queries(1, t, PAIR, sem.stacked_rest)
                    stack_keys(0, t, 0, sem.stacked_rest)
                    stack_keys(0, t, PAIR, sem.stacked_rest)
                    stack_keys(1, t, 2 * PAIR, sem.stacked_rest)

            def m_rows(b, g):
                sp.wait_ge(sem.m_neg, b.at(PER.m_neg, g + 1))
                for j in range(G1):
                    sp.dma_start(f32(qs[SHIFT_ROW:SHIFT_ROW + 1, G1 * g + j, :]),
                                 f32(neg[j * T:(j + 1) * T, g, :])).then_inc(sem.m_row, 16)

            def t_out(b):
                sp.wait_ge(sem.t_ev, b.at(PER.t_ev, 2))
                sp.dma_start(one(out, b), x3[:, :]).then_inc(sem.stored, 16)

            sp.wait_ge(s_fill, 2)
            play(sp, dict(load=load, p_stack=p_stack, m_rows=m_rows, t_out=t_out))
            sp.wait_ge(sem.stored, 16 * images)

        @block.gpsimd
        def _(pool):
            pool.memset(f32(qs[:, :, :]), 0.0).then_inc(s_fill, 1)
            pool.memset(f32(ks[:, :, :]), 1.0).then_inc(s_fill, 1)
            pool.memset(ones[:, :], 1.0).then_inc(s_ones, 1)
            pool.memset(f32(ones_r[:, :]), 1.0).then_inc(s_ones, 1)
            pool.memset(minus_half[:, :], -0.5).then_inc(s_ones, 1)
            pool.memset(v1[:, :, :, :], 0.0).then_inc(s_ones, 1)
            pool.memset(tm[:, :, W3:W3 + 1], 1.0).then_inc(s_ones, 1)
            pool.memset(qa[:, :, D3:D3 + 1], 1.0).then_inc(s_ones, 1)
            pool.memset(ka[:, :, D3:D3 + 1], 1.0).then_inc(s_ones, 1)
            pool.wait_ge(s_ones, 7)
            pool.memset(v1[:, :, :, DH:DH + 1], 1.0).then_inc(s_ones, 1)

            def g_var(b):
                pool.wait_ge(sem.g_veps, b.at(PER.g_veps, 1))
                pool.tensor_tensor(g_rs[:, :], g_ve[:, 1:2], minus_half[:, 0:1], ALU.pow)\
                    .then_inc(sem.g_rstd, 1)

            def f_qk(n, b, u, layer):
                if layer == 0:
                    return
                dst = queries(layer) if u < 2 else keys(layer)
                pool.wait_ge(sem.f_hi, n.at(PER.f_hi, u + 1))
                pool.wait_ge(sem.i_exact, b.at(PER.i_exact, u + 1))
                pool.tensor_tensor(dst[1][:, half(u % 2)], f_exact[:, u % 2, :],
                                   f32(dst[0][:, half(u % 2)]), ALU.subtract).then_inc(sem.f_lo, 1)

            def f_value(n, h, layer):
                if layer == 2 and h == 0:
                    pool.tensor_tensor(x2_bias, x2[:, :], col("bv2").broadcast_to([C, N]), ALU.add)\
                        .then_inc(sem.i_res, 1)

            def f_out(n, b, layer):
                if layer == 2:
                    pool.wait_ge(sem.f_div, n.at(PER.f_div, 1))
                    pool.wait_ge(sem.i_res, b.at(PER.i_res, 1))
                    if b.has_prev:
                        pool.wait_ge(sem.stored, b.at(PER.stored, 0))
                    pool.tensor_tensor(x3[:, :], f_num[:, :], x2_bias, ALU.add)\
                        .then_inc(sem.f_out, 1)

            def i_stat(b):
                pool.wait_ge(sem.i_veps, b.at(PER.i_veps, 1))
                pool.tensor_tensor(i_rs[:, :], i_ve[:, :], minus_half[:, 0:1], ALU.pow)\
                    .then_inc(sem.i_rstd, 1)

            def f_pv(n, u, layer):
                h, kt = u // T, u % T
                dst = fsum[:, half(h)]
                pool.wait_ge(sem.f_p, n.at(PER.f_p, u + 1))
                if kt == 1:
                    if u == 1:
                        if n.has_prev:
                            pool.wait_ge(sem.f_z, n.at(PER.f_z, 0))
                    pool.tensor_tensor(dst, fp[(u - 1) % 3][:, :], fp[u % 3][:, :], ALU.add)\
                        .then_inc(sem.f_sum, 1)
                elif kt > 1:
                    pool.wait_ge(sem.f_sum, n.at(PER.f_sum, sums_through(u) - 1))
                    pool.tensor_tensor(dst, dst, fp[u % 3][:, :], ALU.add).then_inc(sem.f_sum, 1)

            def p_var(b):
                pool.wait_ge(sem.p_veps, b.at(PER.p_veps, 1))
                pool.tensor_tensor(p_rs[:, :], p_ve[:, 1:2], minus_half[:, 0:1], ALU.pow)\
                    .then_inc(sem.p_rstd, 1)

            def p_residual(b, n):
                if b.has_prev:
                    pool.wait_ge(sem.o_x2, b.at(PER.o_x2, 0))
                pool.wait_ge(sem.f_out, n.at(PER.f_out, 1))
                pool.tensor_tensor(x1_res[:, :], x1[:, :], const_bias[:, 1:2].broadcast_to([C, N]),
                                   ALU.add).then_inc(sem.p_res, 1)

            def t_norms(b):
                pool.wait_ge(sem.t_ns, b.at(PER.t_ns, 1))
                pool.tensor_tensor(t_rn[:, :], t_ns[:, :], minus_half[:, :], ALU.pow)\
                    .then_inc(sem.t_rn, 1)

            pool.wait_ge(s_folded, 3)
            play(pool, dict(f_qk=f_qk, f_value=f_value, f_out=f_out, g_var=g_var, i_stat=i_stat,
                            f_pv=f_pv, p_var=p_var, p_residual=p_residual, t_norms=t_norms))

        @block.scalar
        def _(act):
            def f_qk(n, b, u, layer):
                if layer == 0 and u == 0 and b.has_prev:
                    act.wait_ge(sem.stacked_first, b.at(PER.stacked_first, 0))
                    act.wait_ge(sem.stacked_rest, b.at(PER.stacked_rest, 0))
                dst, bias = (queries(layer), f"bq{layer}") if u < 2 else (keys(layer), f"bk{layer}")
                act.wait_ge(sem.f_qk, n.at(PER.f_qk, u + 1))
                act.activation(dst[0][:, half(u % 2)], full_pair(layer)[:, half(u % 2)],
                               ACT.Identity, bias=col(bias)).then_inc(sem.f_hi, 1)
                if layer == 2:
                    if u >= 2:
                        act.wait_ge(sem.f_lo, n.at(PER.f_lo, u - 1))
                    elif b.has_prev:
                        act.wait_ge(sem.f_lo, n.at(PER.f_lo, 0))
                    act.activation(f_exact[:, u % 2, :], full_pair(layer)[:, half(u % 2)],
                                   ACT.Identity, bias=col(bias)).then_inc(sem.i_exact, 1)

            def f_value(n, h, layer):
                act.wait_ge(sem.f_v, n.at(PER.f_v, h + 1))
                act.activation(fv[:, 4 * h:4 * h + 4, :].rearrange("p t c -> p (t c)"),
                               full_pair(layer)[:, half(h)], ACT.Copy).then_inc(sem.f_vout, 1)

            def f_scores(n, u, layer):
                act.wait_ge(sem.f_sc, n.at(PER.f_sc, u + 1))
                if u >= 3:
                    act.wait_ge(sem.f_pv, n.at(PER.f_pv, u - 2))
                    act.wait_ge(sem.f_sum, n.at(PER.f_sum, sums_through(u - 3)))
                elif n.has_prev:
                    act.wait_ge(sem.f_pv, n.at(PER.f_pv, 0))
                    act.wait_ge(sem.f_sum, n.at(PER.f_sum, 0))
                act.activation(fp[u % 3][:, :], full_pair(layer)[:, half(0)], ACT.Exp,
                               scale=float(C) ** -0.5).then_inc(sem.f_p, 1)

            def f_pv(n, u, layer):
                if u % T == T - 1:
                    h = u // T
                    act.wait_ge(sem.f_pv, n.at(PER.f_pv, u + 1))
                    if h == 0:
                        if n.has_prev:
                            act.wait_ge(sem.f_out, n.at(PER.f_out, 0))
                    act.activation(f_num[:, half(h)], full_pair(layer)[:, half(1)], ACT.Copy)\
                       .then_inc(sem.f_t, 1)

            def p_qk(b, u):
                dst, bias = (cq, "bq1") if u < 2 else (ck, "bk1")
                act.wait_ge(sem.p_qk, b.at(PER.p_qk, u + 1))
                act.activation(dst[0][:, half(u % 2)], P_ODD[:, half(u % 2)], ACT.Identity,
                               bias=col(bias)).then_inc(sem.p_hi, 1)

            def p_value(b, h):
                act.wait_ge(sem.p_v, b.at(PER.p_v, h + 1))
                act.activation(v1[:, 4 * h:4 * h + 4, :, 0:DH],
                               P_ODD[:, half(h)].rearrange("p (t h d) -> p t h d", t=4, h=HEADS),
                               ACT.Copy).then_inc(sem.p_vout, 1)

            def s_scores(b, g, u):
                kt, j = u // G1, u % G1
                act.wait_ge(sem.s_sc, b.at(PER.s_sc, 32 * g + u + 1))
                if 8 * g + kt >= 2:
                    if j == 0:
                        act.wait_ge(sem.s_pv, b.at(PER.s_pv, 8 * g + kt - 1))
                elif j == 0:
                    if b.has_prev:
                        act.wait_ge(sem.s_pv, b.at(PER.s_pv, 0))
                        act.wait_ge(sem.o_rb, b.at(PER.o_rb, 0))
                if g == 0 and kt == 0 and j == G1 - 1 and b.has_prev:
                    act.wait_ge(sem.f_out, run2(b.previous(), False).at(PER.f_out, 1))
                act.activation(p1[kt % 2][:, j, :], (P_EVEN, P_ODD)[u % 2][:, :], ACT.Exp,
                               scale=float(DH) ** -0.5).then_inc(sem.s_p, 1)

            def s_out(b, g):
                act.wait_ge(sem.s_pv, b.at(PER.s_pv, 8 * (g + 1)))
                if b.has_prev:
                    act.wait_ge(sem.o_pj, b.at(PER.o_pj, 0))
                act.activation(o1[g][:, :], P_ACC[:, :], ACT.Copy).then_inc(sem.o_ev, 1)

            def t_project(b, n, k, beside):
                t0, t1 = 3 * k, min(3 * k + 3, T)
                act.wait_ge(sem.t_q, b.at(PER.t_q, k + 1))
                act.activation(tm[:, t0:t1, 0:W3],
                               t_bank(k)[:, 0:(t1 - t0) * W3].rearrange("p (t w) -> p t w", w=W3),
                               ACT.Copy).then_inc(sem.t_tm, 1)

            def t_matrix(b):
                act.wait_ge(sem.t_m, b.at(PER.t_m, 1))
                act.activation(ma[:, :], P_F[0:D3 + 1, 0:C], ACT.Copy).then_inc(sem.t_ma, 1)

            def t_turn(b):
                act.wait_ge(sem.t_tr, b.at(PER.t_tr, 1))
                act.activation(qt3, P_F[0:D3 + 1, :].rearrange("p (t c) -> p t c", c=C), ACT.Copy)\
                   .then_inc(sem.t_qt, 1)

            def t_out(b):
                for h in range(2):
                    act.wait_ge(sem.t_o, b.at(PER.t_o, h + 1))
                    act.activation(x3[:, half(h)], P_F[:, half(h)], ACT.Copy).then_inc(sem.t_ev, 1)

            act.wait_ge(s_const, 32)
            act.wait_ge(s_ones, 8)
            act.wait_ge(s_fold, 3)
            act.activation(wvp0[:, :], P_EVEN[:, 0:C], ACT.Copy).then_inc(s_folded, 1)
            act.activation(const_bias[:, 0:1], P_EVEN[:, C:C + 1], ACT.Identity, bias=col("bp0"))\
               .then_inc(s_folded, 1)
            act.activation(const_bias[:, 1:2], P_EVEN[:, C + 1:C + 2], ACT.Identity,
                           bias=col("bp1"))\
               .then_inc(s_folded, 1)
            play(act, dict(f_qk=f_qk, f_value=f_value, f_scores=f_scores, f_pv=f_pv, p_qk=p_qk,
                           p_value=p_value, s_scores=s_scores, s_out=s_out, t_project=t_project,
                           t_matrix=t_matrix, t_turn=t_turn, t_out=t_out))

        @block.vector
        def _(dve):
            def g_stat(b):
                dve.wait_ge(sem.x_loaded, b.at(PER.x_loaded, 16))
                dve.bn_stats(g_bn[:, 0, :], x_in[:, half(0)])
                dve.bn_stats(g_bn[:, 1, :], x_in[:, half(1)]).then_inc(sem.g_dve, 1)
                dve.wait_ge(sem.g_dve, b.at(PER.g_dve, 1))
                dve.memset(g_ve[:, :], 0.0)
                dve.bn_aggr(g_mv[:, :], g_bn[:, :, :].rearrange("p a s -> p (a s)"))\
                   .then_inc(sem.g_dve, 1)
                dve.wait_ge(sem.g_dve, b.at(PER.g_dve, 2))
                dve.scalar_tensor_tensor(out=g_mv[:, 1:2], in0=g_mv[:, 0:1],
                                         scalar=g_mv[:, 0:1], in1=g_mv[:, 1:2],
                                         op0=ALU.mult, op1=ALU.add).then_inc(sem.g_stat, 1)

            def g_var(b):
                dve.wait_ge(sem.g_gstat, b.at(PER.g_gstat, 1))
                dve.tensor_copy(g_gs[:, :], P_F[:, 0:2]).then_inc(sem.g_dve, 1)
                dve.wait_ge(sem.g_dve, b.at(PER.g_dve, 3))
                dve.scalar_tensor_tensor(out=g_ve[:, 0:1], in0=g_gs[:, 0:1],
                                         scalar=g_gs[:, 0:1], in1=g_gs[:, 1:2],
                                         op0=ALU.mult, op1=ALU.subtract).then_inc(sem.g_dve, 1)
                dve.wait_ge(sem.g_dve, b.at(PER.g_dve, 4))
                dve.tensor_scalar(g_ve[:, 1:2], g_ve[:, 0:1], -1.0, EPS, ALU.mult, ALU.add)\
                   .then_inc(sem.g_veps, 1)

            def g_apply(b):
                dve.wait_ge(sem.g_rstd, b.at(PER.g_rstd, 1))
                dve.tensor_scalar(g_ac[:, 0:1], g_rs[:, :], col("gamma0"), None, ALU.mult)\
                   .then_inc(sem.g_dve, 1)
                dve.wait_ge(sem.g_dve, b.at(PER.g_dve, 5))
                dve.scalar_tensor_tensor(out=g_ac[:, 1:2], in0=g_gs[:, 0:1],
                                         scalar=g_ac[:, 0:1], in1=col("beta0"),
                                         op0=ALU.mult, op1=ALU.subtract).then_inc(sem.g_dve, 1)
                dve.wait_ge(sem.g_dve, b.at(PER.g_dve, 6))
                dve.tensor_scalar(xn[:, :], x_in[:, :], g_ac[:, 0:1], g_ac[:, 1:2], ALU.mult,
                                  ALU.subtract).then_inc(sem.g_xn, 1)

            def i_stat(b):
                dve.wait_ge(sem.o_x2, b.at(PER.o_x2, 1))
                dve.bn_stats(i_bn[:, 0, :], x2[:, half(0)])
                dve.bn_stats(i_bn[:, 1, :], x2[:, half(1)]).then_inc(sem.i_dve, 1)
                dve.wait_ge(sem.i_dve, b.at(PER.i_dve, 1))
                dve.memset(i_ve[:, :], 0.0)
                dve.bn_aggr(i_mv[:, :], i_bn[:, :, :].rearrange("p a s -> p (a s)"))\
                   .then_inc(sem.i_dve, 1)
                dve.wait_ge(sem.i_dve, b.at(PER.i_dve, 2))
                dve.tensor_scalar(i_ve[:, :], i_mv[:, 1:2], EPS, None, ALU.add)\
                   .then_inc(sem.i_veps, 1)

            def i_apply(b):
                dve.wait_ge(sem.i_rstd, b.at(PER.i_rstd, 1))
                dve.tensor_scalar(i_ac[:, :], i_mv[:, 0:1], i_rs[:, :], None, ALU.mult)\
                   .then_inc(sem.i_dve, 1)
                dve.wait_ge(sem.i_dve, b.at(PER.i_dve, 3))
                dve.tensor_scalar(xn2, x2[:, :], i_rs[:, :], i_ac[:, :], ALU.mult, ALU.subtract)\
                   .then_inc(sem.i_xn, 1)

            def f_qk(n, b, u, layer):
                if layer == 2:
                    return
                if layer == 0 and u == 0 and b.has_prev:
                    dve.wait_ge(sem.stacked_first, b.at(PER.stacked_first, 0))
                    dve.wait_ge(sem.stacked_rest, b.at(PER.stacked_rest, 0))
                dst, bias = (queries(layer), f"bq{layer}") if u < 2 else (keys(layer), f"bk{layer}")
                dve.wait_ge(sem.f_hi, n.at(PER.f_hi, u + 1))
                h = half(u % 2)
                dve.scalar_tensor_tensor(out=dst[1][:, h], in0=full_pair(layer)[:, h],
                                         scalar=col(bias), in1=f32(dst[0][:, h]), op0=ALU.add, op1=ALU.subtract)\
                   .then_inc(sem.f_lo, 1)

            def f_max(n, b, u, layer):
                dve.wait_ge(sem.f_max_s, n.at(PER.f_max_s, u + 1))
                dve.reduce_max(f_mx2[:, u // 2, u % 2:u % 2 + 1], full_pair(layer)[:, half(u % 2)],
                               AX.X)\
                   .then_inc(sem.f_max, 1)

            def f_shift(n, h):
                q = slice(h * T // 2, (h + 1) * T // 2)
                dve.wait_ge(sem.f_max, n.at(PER.f_max, T * (h + 1)))
                dve.tensor_tensor(f_mx[:, q], f_mx2[:, q, 0], f_mx2[:, q, 1], ALU.max)\
                   .then_inc(sem.f_dve, 1)
                dve.wait_ge(sem.f_dve, n.at(PER.f_dve, h + 1))
                if h == 0 and n.has_prev:
                    dve.wait_ge(sem.f_sc, n.at(PER.f_sc, 0))
                shape = [C, T // 2, C]
                dve.tensor_tensor(f_diag[:, q, :],
                                  mat("neg_ident").rearrange("p (a c) -> p a c", a=1)
                                  .broadcast_to(shape),
                                  f_mx[:, q].rearrange("p (t a) -> p t a", a=1).broadcast_to(shape),
                                  ALU.mult).then_inc(sem.f_shift, 1)

            def f_sums(n, layer):
                dve.wait_ge(sem.f_z, n.at(PER.f_z, 1))
                dve.reciprocal(f_recip[:, :], full_pair(layer)[:, 0:T]).then_inc(sem.f_r, 1)

            def f_out(n, b, layer):
                dve.wait_ge(sem.f_rb, n.at(PER.f_rb, 1))
                dve.tensor_tensor(f_num[:, :], f_num[:, :], full_pair(layer)[:, :], ALU.mult)\
                   .then_inc(sem.f_div, 1)
                if layer == 2:
                    return
                dve.wait_ge(sem.f_div, n.at(PER.f_div, 1))
                if b.has_prev:
                    dve.wait_ge(sem.p_h, b.at(PER.p_h, 0))
                    dve.wait_ge(sem.p_res, b.at(PER.p_res, 0))
                dve.scalar_tensor_tensor(out=x1[:, :], in0=f_num[:, :], scalar=const_bias[:, 0:1],
                                         in1=xn[:, :], op0=ALU.add, op1=ALU.add)\
                   .then_inc(sem.f_out, 1)

            def p_stat(b, n):
                dve.wait_ge(sem.f_out, n.at(PER.f_out, 1))
                dve.bn_stats(p_bn[:, 0, :], x1[:, half(0)])
                dve.bn_stats(p_bn[:, 1, :], x1[:, half(1)]).then_inc(sem.p_dve, 1)
                dve.wait_ge(sem.p_dve, b.at(PER.p_dve, 1))
                dve.memset(p_ve[:, :], 0.0)
                dve.bn_aggr(p_mv[:, :], p_bn[:, :, :].rearrange("p a s -> p (a s)"))\
                   .then_inc(sem.p_dve, 1)
                dve.wait_ge(sem.p_dve, b.at(PER.p_dve, 2))
                dve.scalar_tensor_tensor(out=p_mv[:, 1:2], in0=p_mv[:, 0:1],
                                         scalar=p_mv[:, 0:1], in1=p_mv[:, 1:2],
                                         op0=ALU.mult, op1=ALU.add).then_inc(sem.p_stat, 1)

            def p_var(b):
                dve.wait_ge(sem.p_gstat, b.at(PER.p_gstat, 1))
                dve.tensor_copy(p_gs[:, :], P_ODD[:, 0:2]).then_inc(sem.p_dve, 1)
                dve.wait_ge(sem.p_dve, b.at(PER.p_dve, 3))
                dve.scalar_tensor_tensor(out=p_ve[:, 0:1], in0=p_gs[:, 0:1],
                                         scalar=p_gs[:, 0:1], in1=p_gs[:, 1:2],
                                         op0=ALU.mult, op1=ALU.subtract).then_inc(sem.p_dve, 1)
                dve.wait_ge(sem.p_dve, b.at(PER.p_dve, 4))
                dve.tensor_scalar(p_ve[:, 1:2], p_ve[:, 0:1], -1.0, EPS, ALU.mult, ALU.add)\
                   .then_inc(sem.p_veps, 1)

            def p_apply(b):
                dve.wait_ge(sem.p_rstd, b.at(PER.p_rstd, 1))
                dve.tensor_scalar(p_ac[:, 0:1], p_rs[:, :], col("gamma1"), None, ALU.mult)\
                   .then_inc(sem.p_dve, 1)
                dve.wait_ge(sem.p_dve, b.at(PER.p_dve, 5))
                dve.scalar_tensor_tensor(out=p_ac[:, 1:2], in0=p_gs[:, 0:1],
                                         scalar=p_ac[:, 0:1], in1=col("beta1"),
                                         op0=ALU.mult, op1=ALU.subtract).then_inc(sem.p_dve, 1)
                dve.wait_ge(sem.p_dve, b.at(PER.p_dve, 6))
                dve.tensor_scalar(h1[:, :], x1[:, :], p_ac[:, 0:1], p_ac[:, 1:2], ALU.mult,
                                  ALU.subtract).then_inc(sem.p_h, 1)

            def p_qk(b, u):
                dst, bias = (cq, "bq1") if u < 2 else (ck, "bk1")
                dve.wait_ge(sem.p_hi, b.at(PER.p_hi, u + 1))
                h = half(u % 2)
                dve.scalar_tensor_tensor(out=dst[1][:, h], in0=P_ODD[:, h], scalar=col(bias),
                                         in1=f32(dst[0][:, h]), op0=ALU.add, op1=ALU.subtract)\
                   .then_inc(sem.p_lo, 1)

            def m_max(b, u):
                dve.wait_ge(sem.m_s, b.at(PER.m_s, u + 1))
                dve.reduce_max(mx1[:, u // (G1 * T), u % (G1 * T):u % (G1 * T) + 1],
                               (P_EVEN, P_ODD)[u % 2][:, :], AX.X).then_inc(sem.m_max, 1)

            def m_half(b, v):
                u = FULL_TILES - G1 * T + v // 2
                dve.wait_ge(sem.m_s, b.at(PER.m_s, FULL_TILES + v + 1))
                dve.reduce_max(mx_half[:, u, v % 2:v % 2 + 1], P_F[:, half(v % 2)], AX.X)\
                   .then_inc(sem.m_max, 1)
                if v == 2 * (HEADS * T - FULL_TILES) - 1:
                    q = slice(FULL_TILES - G1 * T, G1 * T)
                    dve.wait_ge(sem.m_max, b.at(PER.m_max, PER.m_max))
                    dve.tensor_tensor(mx1[:, 1, q], mx_half[:, q, 0], mx_half[:, q, 1], ALU.max)\
                       .then_inc(sem.m_both, 1)

            def m_rows(b, g):
                dve.wait_ge(sem.m_t, b.at(PER.m_t, g + 1))
                if b.has_prev:
                    dve.wait_ge(sem.m_row, b.at(PER.m_row, 0))
                dve.tensor_copy(neg[:, g, :], P_F[0:G1 * T, 0:C]).then_inc(sem.m_neg, 1)

            def o_sums(b, g):
                dve.wait_ge(sem.o_z, b.at(PER.o_z, g + 1))
                dve.reciprocal(rz[g][:, :, :].rearrange("p t j -> p (t j)"),
                               (P_EVEN, P_ODD)[g][:, 0:T * G1]).then_inc(sem.o_dve, 1)
                dve.wait_ge(sem.o_dve, b.at(PER.o_dve, g + 1))
                dve.tensor_copy(rx[g], rz[g][:, :, :].rearrange(
                    "p t (j a) -> p t j a", a=1).broadcast_to([C, T, G1, 32])).then_inc(sem.o_r, 1)

            def o_divide(b, g):
                dve.wait_ge(sem.o_rb, b.at(PER.o_rb, g + 1))
                dve.tensor_tensor(o1[g][:, :], o1[g][:, :], (P_ACC, P_EVEN)[g][:, :], ALU.mult)\
                   .then_inc(sem.o_n, 1)

            def o_residual(b):
                dve.wait_ge(sem.o_pj, b.at(PER.o_pj, 1))
                dve.wait_ge(sem.p_res, b.at(PER.p_res, 1))
                dve.tensor_tensor(x2[:, :], P_ACC[:, :], x1_res[:, :], ALU.add)\
                   .then_inc(sem.o_x2, 1)

            def t_norms(b):
                dve.wait_ge(sem.t_tm, b.at(PER.t_tm, 3))
                qk = tm[:, :, 0:2 * D3].rearrange("p t (a d) -> p t a d", a=2)
                dve.tensor_tensor(t_sq[:, :, :, :], qk, qk, ALU.mult)\
                   .then_inc(sem.t_dve, 1)
                dve.wait_ge(sem.t_dve, b.at(PER.t_dve, 1))
                dve.reduce_sum(t_ns[:, :], t_sq[:, :, :, :].rearrange("p t a d -> p (t a) d"), AX.X)\
                   .then_inc(sem.t_ns, 1)

            def t_keys(b):
                dve.wait_ge(sem.t_rn, b.at(PER.t_rn, 1))
                rn = t_rn[:, :].rearrange("p (t a) -> p t a", a=2)
                dve.tensor_tensor(ka[:, :, 0:D3], tm[:, :, D3:2 * D3],
                                  rn[:, :, 1:2].broadcast_to([C, T, D3]), ALU.mult)\
                   .then_inc(sem.t_k, 1)
                dve.tensor_tensor(qa[:, :, 0:D3], tm[:, :, 0:D3],
                                  rn[:, :, 0:1].broadcast_to([C, T, D3]), ALU.mult)\
                   .then_inc(sem.t_dve, 1)
                dve.wait_ge(sem.t_dve, b.at(PER.t_dve, 2))

            def t_scale(b):
                dve.wait_ge(sem.t_m, b.at(PER.t_m, 1))
                dve.tensor_scalar(wb[:, 0:D3], P_F[:, HALF:HALF + D3], EPS3, None, ALU.add)
                dve.tensor_copy(wb[:, D3:D3 + 1], P_F[:, HALF + D3:HALF + D3 + 1])\
                   .then_inc(sem.t_dve, 1)
                dve.wait_ge(sem.t_dve, b.at(PER.t_dve, 3))
                dve.tensor_tensor(t_dn[:, :, :], qa[:, :, :],
                                  wb[:, :].rearrange("p (a d) -> p a d", a=1)
                                  .broadcast_to([C, T, D3 + 1]),
                                  ALU.mult)\
                   .then_inc(sem.t_dve, 1)
                dve.wait_ge(sem.t_dve, b.at(PER.t_dve, 4))
                dve.reduce_sum(t_ds[:, 0, :], t_dn[:, :, :], AX.X)\
                   .then_inc(sem.t_dve, 1)
                dve.wait_ge(sem.t_dve, b.at(PER.t_dve, 5))
                dve.reciprocal(t_ds[:, 1, :], t_ds[:, 0, :])\
                   .then_inc(sem.t_dve, 1)
                dve.wait_ge(sem.t_dve, b.at(PER.t_dve, 6))
                dve.tensor_scalar(t_ds[:, 2, :], t_ds[:, 1, :], col("gamma3"), None, ALU.mult)\
                   .then_inc(sem.t_dve, 1)
                dve.wait_ge(sem.t_dve, b.at(PER.t_dve, 7))
                dve.tensor_tensor(t_dn[:, :, :], qa[:, :, :],
                                  t_ds[:, 2, :].rearrange("p (t a) -> p t a", a=1)
                                  .broadcast_to([C, T, D3 + 1]),
                                  ALU.mult).then_inc(sem.t_qs, 1)

            dve.wait_ge(s_const, 32)
            dve.wait_ge(s_ones, 8)
            dve.wait_ge(s_folded, 3)
            play(dve, dict(g_stat=g_stat, g_var=g_var, g_apply=g_apply, i_stat=i_stat,
                           i_apply=i_apply, f_qk=f_qk, f_max=f_max, f_shift=f_shift,
                           f_sums=f_sums, f_out=f_out, p_stat=p_stat, p_var=p_var,
                           p_apply=p_apply, p_qk=p_qk, m_max=m_max, m_half=m_half, m_rows=m_rows,
                           o_sums=o_sums, o_divide=o_divide, o_residual=o_residual,
                           t_norms=t_norms, t_keys=t_keys, t_scale=t_scale))

        @block.tensor
        def _(pe):
            def mm(dst, lhsT, rhs, start=True, stop=True):
                return pe.matmul(dst, lhsT, rhs, start=start, stop=stop)

            def g_stat(b):
                pe.wait_ge(sem.g_stat, b.at(PER.g_stat, 1))
                if b.has_prev:
                    before = b.previous()
                    if before.has_prev:
                        pe.wait_ge(sem.t_ev, before.at(PER.t_ev, 0))
                    pe.wait_ge(sem.m_neg, before.at(PER.m_neg, 2))
                mm(P_F[:, 0:2], mat("group0"), g_mv[:, :]).then_inc(sem.g_gstat, 1)

            def f_qk(n, b, u, layer):
                src = xn if layer == 0 else xn2
                if u == 0 and layer == 0:
                    pe.wait_ge(sem.g_xn, b.at(PER.g_xn, 1))
                elif u == 0:
                    pe.wait_ge(sem.i_xn, b.at(PER.i_xn, 1))
                if u >= 2 and layer == 0:
                    pe.wait_ge(sem.f_lo, n.at(PER.f_lo, u - 1))
                elif u >= 2:
                    pe.wait_ge(sem.i_exact, b.at(PER.i_exact, u - 1))
                mm(full_pair(layer)[:, half(u % 2)], mat(f"wq{layer}" if u < 2 else f"wk{layer}"),
                   src[:, half(u % 2)]).then_inc(sem.f_qk, 1)

            def f_value(n, h, layer):
                pe.wait_ge(sem.f_max, n.at(PER.f_max, 2 * T - 1 + h))
                src = xn if layer == 0 else xn2
                for t in range(4 * h, 4 * h + 4):
                    last = mm(full_pair(layer)[:, tile(t)], src[:, tile(t)],
                              wvp0[:, :] if layer == 0 else mat("wv2"))
                last.then_inc(sem.f_v, 1)

            def f_max(n, b, u, layer):
                if u < 2:
                    if layer == 0:
                        pe.wait_ge(sem.f_lo, n.at(PER.f_lo, 3 + u))
                    else:
                        pe.wait_ge(sem.i_exact, b.at(PER.i_exact, 3 + u))
                else:
                    pe.wait_ge(sem.f_max, n.at(PER.f_max, u - 1))
                mm(full_pair(layer)[:, half(u % 2)], queries(layer)[0][:, tile(u // 2)],
                   keys(layer)[0][:, half(u % 2)])\
                    .then_inc(sem.f_max_s, 1)

            def f_scores(n, u, layer):
                h, kt = u // T, u % T
                if u == 0:
                    pe.wait_ge(sem.f_vout, n.at(PER.f_vout, 1))
                    pe.wait_ge(sem.f_lo, n.at(PER.f_lo, 4))
                else:
                    pe.wait_ge(sem.f_p, n.at(PER.f_p, u))
                dst, q, k = full_pair(layer)[:, half(0)], queries(layer), keys(layer)
                mm(dst, k[0][:, tile(kt)], q[0][:, half(h)], stop=False)
                mm(dst, k[0][:, tile(kt)], q[1][:, half(h)], start=False, stop=False)
                mm(dst, k[1][:, tile(kt)], q[0][:, half(h)], start=False, stop=False)
                if u % T == 0:
                    pe.wait_ge(sem.f_shift, n.at(PER.f_shift, h + 1))
                mm(dst, ones_r[:, :], f_diag[:, 4 * h:4 * h + 4, :].rearrange("p t c -> p (t c)"),
                   start=False).then_inc(sem.f_sc, 1)

            def f_pv(n, u, layer):
                h, kt = u // T, u % T
                pe.wait_ge(sem.f_p, n.at(PER.f_p, u + 1))
                if u == 0:
                    pe.wait_ge(sem.f_vout, n.at(PER.f_vout, 2))
                if u == T:
                    pe.wait_ge(sem.f_t, n.at(PER.f_t, 1))
                mm(full_pair(layer)[:, half(1)], fv[:, kt, :], fp[u % 3][:, :], start=kt == 0,
                   stop=kt == T - 1).then_inc(sem.f_pv, 1)

            def f_sums(n, layer):
                pe.wait_ge(sem.f_sum, n.at(PER.f_sum, PER.f_sum))
                for t in range(T):
                    last = mm(full_pair(layer)[:, t:t + 1], fsum[:, tile(t)], ones[:, 0:1])
                last.then_inc(sem.f_z, 1)

            def f_spread(n, layer):
                pe.wait_ge(sem.f_r, n.at(PER.f_r, 1))
                pe.wait_ge(sem.f_t, n.at(PER.f_t, 2))
                for t in range(T):
                    last = mm(full_pair(layer)[:, tile(t)], f_recip[:, t:t + 1].broadcast_to([C, C]),
                              mat("ident"))
                last.then_inc(sem.f_rb, 1)

            def p_average(b):
                pe.wait_ge(sem.p_stat, b.at(PER.p_stat, 1))
                mm(P_ODD[:, 0:2], mat("group1"), p_mv[:, :]).then_inc(sem.p_gstat, 1)

            def p_qk(b, u):
                if u == 0:
                    pe.wait_ge(sem.p_h, b.at(PER.p_h, 1))
                if u >= 2:
                    pe.wait_ge(sem.p_lo, b.at(PER.p_lo, u - 1))
                mm(P_ODD[:, half(u % 2)], mat("wq1" if u < 2 else "wk1"),
                   h1[:, half(u % 2)]).then_inc(sem.p_qk, 1)

            def p_value(b, h):
                pe.wait_ge(sem.p_lo, b.at(PER.p_lo, 3 + h))
                for t in range(4 * h, 4 * h + 4):
                    last = mm(P_ODD[:, tile(t)], h1[:, tile(t)], mat("wv1"))
                last.then_inc(sem.p_v, 1)

            def m_max(b, u):
                h, t = u // T, u % T
                if u == 0:
                    pe.wait_ge(sem.stacked_first, b.at(PER.stacked_first, PER.stacked_first))
                    if b.has_prev:
                        pe.wait_ge(sem.o_n, b.at(PER.o_n, 0))
                elif u == 1:
                    pe.wait_ge(sem.p_vout, b.at(PER.p_vout, 2))
                else:
                    pe.wait_ge(sem.m_max, b.at(PER.m_max, u - 1))
                if u == 2 * T:
                    pe.wait_ge(sem.stacked_rest, b.at(PER.stacked_rest, PER.stacked_rest))
                for k in range(2):
                    last = mm((P_EVEN, P_ODD)[u % 2][:, half(k)], qs[0:SHIFT_ROW, h, tile(t)],
                              ks[0:SHIFT_ROW, h // 2, half(k)])
                last.then_inc(sem.m_s, 1)

            def m_half(b, v):
                u, k = FULL_TILES + v // 2, v % 2
                h, t = u // T, u % T
                if v < 2:
                    pe.wait_ge(sem.m_neg, b.at(PER.m_neg, 1))
                else:
                    pe.wait_ge(sem.m_max, b.at(PER.m_max, FULL_TILES + v - 1))
                mm(P_F[:, half(k)], qs[0:SHIFT_ROW, h, tile(t)], ks[0:SHIFT_ROW, h // 2, half(k)])\
                    .then_inc(sem.m_s, 1)

            def m_rows(b, g):
                if g == 0:
                    pe.wait_ge(sem.m_max, b.at(PER.m_max, G1 * T))
                    pe.wait_ge(sem.f_out, run0(b).at(PER.f_out, 1))
                else:
                    pe.wait_ge(sem.m_both, b.at(PER.m_both, 1))
                mm(P_F[0:G1 * T, 0:C], mx1[:, g, :], mat("neg_ident")).then_inc(sem.m_t, 1)

            def s_scores(b, g, u):
                kt, h = u // G1, G1 * g + u % G1
                if u == 0:
                    pe.wait_ge(sem.m_row, b.at(PER.m_row, 64 * (g + 1)))
                    if g == 0:
                        pe.wait_ge(sem.p_vout, b.at(PER.p_vout, 2))
                if g == 0 and u < 2:
                    pe.wait_ge(sem.m_max, b.at(PER.m_max, FULL_TILES - 1 + u))
                if 32 * g + u >= 2:
                    pe.wait_ge(sem.s_p, b.at(PER.s_p, 32 * g + u - 1))
                for k in range(2):
                    last = mm((P_EVEN, P_ODD)[u % 2][:, half(k)], ks[:, h // 2, tile(kt)],
                              qs[:, h, half(k)])
                last.then_inc(sem.s_sc, 1)

            def s_pv(b, g, kt, k):
                pe.wait_ge(sem.s_p, b.at(PER.s_p, 32 * g + G1 * (kt + 1)))
                if kt == 0 and k == 0 and g == 0 and b.has_prev:
                    pe.wait_ge(sem.f_div, run2(b.previous(), False).at(PER.f_div, 1))
                if kt == 0 and k == 0 and g == 1:
                    pe.wait_ge(sem.o_ev, b.at(PER.o_ev, 1))
                for j in range(G1):
                    last = mm(P_ACC[32 * j:32 * j + 32, half(k)], v1[:, kt, G1 * g + j, :],
                              p1[kt % 2][:, j, half(k)], start=kt == 0, stop=kt == T - 1)
                if k == 1:
                    last.then_inc(sem.s_pv, 1)

            def o_sums(b, g):
                pe.wait_ge(sem.o_ev, b.at(PER.o_ev, g + 1))
                pe.wait_ge(sem.s_p, b.at(PER.s_p, PER.s_p - 1 + g))
                for t in range(T):
                    last = mm((P_EVEN, P_ODD)[g][:, t * G1:(t + 1) * G1], o1[g][:, tile(t)],
                              col("zsel", G1))
                last.then_inc(sem.o_z, 1)

            def o_spread(b, g):
                pe.wait_ge(sem.o_r, b.at(PER.o_r, g + 1))
                if g == 0:
                    pe.wait_ge(sem.o_ev, b.at(PER.o_ev, 2))
                for t in range(T):
                    last = mm((P_ACC, P_EVEN)[g][:, tile(t)],
                              rx[g][:, t, :, :].rearrange("p j a -> p (j a)"), mat("ident"))
                last.then_inc(sem.o_rb, 1)

            def o_project(b):
                pe.wait_ge(sem.o_n, b.at(PER.o_n, 2))
                for k in range(2):
                    for g in range(2):
                        last = mm(P_ACC[:, half(k)], mat(("wp1a", "wp1b")[g]), o1[g][:, half(k)],
                                  start=g == 0, stop=g == 1)
                last.then_inc(sem.o_pj, 1)

            def t_project(b, n, k, beside):
                if k == 0:
                    pe.wait_ge(sem.f_out, n.at(PER.f_out, 1))
                    pe.wait_ge(sem.m_neg, beside.at(PER.m_neg, 2))
                if k == 2:
                    pe.wait_ge(sem.t_tm, b.at(PER.t_tm, 1))
                for t in range(3 * k, min(3 * k + 3, T)):
                    dst = t_bank(k)[:, (t - 3 * k) * W3:(t - 3 * k + 1) * W3]
                    mm(dst, x3[:, tile(t)], col("w3", W3), stop=False)
                    last = mm(dst, ones[0:1, :], b3row[:, :], start=False)
                last.then_inc(sem.t_q, 1)

            def t_matrix(b):
                pe.wait_ge(sem.t_k, b.at(PER.t_k, 1))
                pe.wait_ge(sem.t_tm, b.at(PER.t_tm, 3))
                for t in range(T):
                    mm(P_F[0:D3 + 1, 0:C + 1], ka[:, t, :], tm[:, t, 2 * D3:W3 + 1],
                       start=t == 0, stop=t == T - 1)
                for t in range(T):
                    last = mm(P_F[:, HALF:HALF + D3 + 1], ones[:, :], ka[:, t, :],
                              start=t == 0, stop=t == T - 1)
                last.then_inc(sem.t_m, 1)

            def t_turn(b):
                pe.wait_ge(sem.t_qs, b.at(PER.t_qs, 1))
                pe.wait_ge(sem.t_ma, b.at(PER.t_ma, 1))
                for t in range(T):
                    last = mm(P_F[0:D3 + 1, tile(t)], t_dn[:, t, :], mat("ident"))
                last.then_inc(sem.t_tr, 1)

            def t_out(b):
                pe.wait_ge(sem.t_qt, b.at(PER.t_qt, 1))
                for k in range(2):
                    mm(P_F[:, half(k)], ma[:, :], qt3[:, 4 * k:4 * k + 4, :]).then_inc(sem.t_o, 1)

            pe.wait_ge(s_const, 32)
            pe.wait_ge(s_ones, 8)
            mm(P_EVEN[:, 0:C], mat("wv0"), mat("wp0")).then_inc(s_fold, 1)
            mm(P_EVEN[:, C:C + 1], mat("wp0"), col("bv0")).then_inc(s_fold, 1)
            mm(P_EVEN[:, C + 1:C + 2], mat("wp1"), col("bv1")).then_inc(s_fold, 1)
            pe.wait_ge(s_folded, 3)
            play(pe, dict(g_stat=g_stat, f_qk=f_qk, f_value=f_value, f_max=f_max,
                          f_scores=f_scores, f_pv=f_pv, f_sums=f_sums, f_spread=f_spread,
                          p_average=p_average, p_qk=p_qk, p_value=p_value, m_max=m_max,
                          m_half=m_half, m_rows=m_rows, s_scores=s_scores, s_pv=s_pv,
                          o_sums=o_sums, o_spread=o_spread, o_project=o_project,
                          t_project=t_project, t_matrix=t_matrix, t_turn=t_turn, t_out=t_out))


def kernel(x, **w):
    import numpy as np
    import concourse.bacc as bacc
    from concourse.bass_utils import run_bass_kernel_spmd as run

    a = {k: np.asarray(v) for k, v in w.items()}
    images = x.shape[0]

    packed = np.zeros((C, PACKED), np.float32)

    def put(name, value):
        packed[:, COL[name]:COL[name] + value.shape[1]] = value

    put("wq0", a["L0_conv_Wq"].T)
    put("wk0", a["L0_conv_Wk"].T)
    put("wv0", a["L0_conv_Wv"])
    put("wp0", a["L0_conv_Wp"].T)
    put("wq1", a["L1_conv_wq"].T)
    put("wk1", a["L1_conv_wk"].T)
    put("wv1", a["L1_conv_wv"].T)
    put("wp1", a["L1_conv_wp"].T)
    for g, name in enumerate(("wp1a", "wp1b")):
        for j in range(G1):
            h = G1 * g + j
            rows = a["L1_conv_wp"].T[h * DH:(h + 1) * DH]
            packed[32 * j:32 * j + DH, COL[name]:COL[name] + C] = rows
    put("wq2", a["L2_conv_wq"].T)
    put("wk2", a["L2_conv_wk"].T)
    put("wv2", a["L2_conv_wv"].T)
    put("ident", np.eye(C, dtype=np.float32))
    put("neg_ident", -np.eye(C, dtype=np.float32))
    for name, group in (("group0", C // 8), ("group1", C // 32)):
        block = np.full((group, group), 1.0 / group)
        put(name, np.kron(np.eye(C // group), block).astype(np.float32))
    put("w3", np.concatenate([a["L3_conv_Wq"].T, a["L3_conv_Wk"].T, a["L3_conv_Wv"].T], axis=1))
    for j in range(G1):
        packed[32 * j + DH, COL["zsel"] + j] = 1.0
    for name, key in dict(bq0="L0_conv_bq", bk0="L0_conv_bk", bv0="L0_conv_bv", bp0="L0_conv_bp",
                          gamma0="L0_conv_gamma", beta0="L0_conv_beta", bq1="L1_conv_bq",
                          bk1="L1_conv_bk", bv1="L1_conv_bv", bp1="L1_conv_bp",
                          gamma1="L1_conv_gn_w", beta1="L1_conv_gn_b", bq2="L2_conv_bq",
                          bk2="L2_conv_bk", bv2="L2_conv_bv").items():
        put(name, a[key].reshape(C, 1))
    put("gamma3", np.broadcast_to(a["L3_conv_gamma"].reshape(1, 1), (C, 1)))
    bias3 = np.concatenate([a["L3_conv_bq"], a["L3_conv_bk"], a["L3_conv_bv"]]).reshape(1, W3)

    nc = bacc.Bacc("TRN2", target_bir_lowering=False, num_devices=1)
    arrays = {"x_dram": np.ascontiguousarray(x).reshape(images, C, N), "packed_dram": packed,
              "bias3_dram": np.ascontiguousarray(bias3)}
    args = [nc.dram_tensor(k, v.shape, F32, kind="ExternalInput").ap() for k, v in arrays.items()]
    args.append(nc.dram_tensor("out_dram", (images, C, N), F32, kind="ExternalOutput").ap())
    heads_kernel(nc, images, *args)
    r = run(nc, [arrays], core_ids=[0])
    return r.results[0]["out_dram"].reshape(x.shape)
```
